# Optimizing a Trainium2 kernel written in Bass

```python
import numpy as np
import jax
import jax.numpy as jnp

def _softmax(x, axis=-1):
    return jax.nn.softmax(x, axis=axis)

def _gelu(x):
    return jax.nn.gelu(x, approximate=True)

def _silu(x):
    return jax.nn.silu(x)

def _sigmoid(x):
    return jax.nn.sigmoid(x)

def _layernorm(x, axis=-1, eps=1e-05):
    m = jnp.mean(x, axis=axis, keepdims=True)
    v = jnp.var(x, axis=axis, keepdims=True)
    return (x - m) / jnp.sqrt(v + eps)

def _scatter_add(tgt, idx, src, axis=0):
    return tgt.at[idx].add(src)

def _segment_sum(src, seg, n):
    return jax.ops.segment_sum(src, seg, n)
kernel_name = 'mk_gnn_ffn_d1_gnn_r32_958f5f'

def setup_inputs(seed: int=0):
    np.random.seed(seed)
    _w = jnp.asarray

    def _rec_inputs():
        import jax
        import jax.numpy as jnp
        _gk = jax.random.key(seed)
        x = 7.22e-05 + 1 * jax.random.normal(jax.random.fold_in(_gk, 1), (3125, 256), jnp.float32)
        src = jax.random.randint(jax.random.fold_in(_gk, 2), (50000,), 0, 3125, jnp.int32)
        dst = jax.random.randint(jax.random.fold_in(_gk, 3), (50000,), 0, 3125, jnp.int32)
        _o = jnp.argsort(dst, stable=True)
        src = src[_o]
        dst = dst[_o]
        edge_attr_5 = jax.random.uniform(jax.random.fold_in(_gk, 11), (50000, 5), jnp.float32, 0.0, 99.9996)
        node_type_19 = jax.random.randint(jax.random.fold_in(_gk, 13), (3125,), 0, 19, jnp.int32)
        return (x, src, dst, edge_attr_5, node_type_19)
    x, src, dst, edge_attr_5, node_type_19 = _rec_inputs()

    def _L0_gnn_setup():
        import jax, jax.numpy as jnp
        import numpy as np
        N = 1024
        E = 4096
        IN = 256
        OUT = 256
        TD = 32
        H = 4
        T = 19
        PROJ = OUT - 2 * TD
        DK = (OUT - TD) // H
        SQRT_DK = float(np.sqrt(DK))
        LN_EPS = 1e-05

        def time_emb(t, w, b):
            return jnp.cos(jnp.log(t + 1.0)[:, None] * w[None, :] + b[None, :])

        def typed_linear(x, W, b, node_type):
            out = jnp.zeros((x.shape[0], W.shape[2]), x.dtype)
            for t in range(W.shape[0]):
                out = jnp.where((node_type == t)[:, None], x @ W[t] + b[t], out)
            return out

        def seg_softmax(att, idx, n):
            m = jax.ops.segment_max(att, idx, num_segments=n)
            e = jnp.exp(att - m[idx])
            s = jax.ops.segment_sum(e, idx, num_segments=n)
            return e / (s[idx] + 1e-16)
        key = jax.random.key(seed)
        ks = jax.random.split(key, 8)
        x = jax.random.normal(ks[0], (N, IN), jnp.float32)
        node_type = jax.random.randint(ks[1], (N,), 0, T, jnp.int32)
        edge_index = jax.random.randint(ks[2], (2, E), 0, N, jnp.int32)
        times = jax.random.uniform(ks[3], (E, 3), jnp.float32, 0.0, 100.0)
        edge_attr = jnp.concatenate([times, node_type[edge_index[0]][:, None].astype(jnp.float32), node_type[edge_index[1]][:, None].astype(jnp.float32)], axis=1)
        s = 0.02
        Wk = jax.random.normal(ks[4], (T, IN, PROJ), jnp.float32) * s
        Wq = jax.random.normal(ks[5], (T, IN, PROJ), jnp.float32) * s
        Wv = jax.random.normal(ks[6], (T, IN, PROJ), jnp.float32) * s
        bk = jnp.zeros((T, PROJ), jnp.float32)
        bq = jnp.zeros((T, PROJ), jnp.float32)
        bv = jnp.zeros((T, PROJ), jnp.float32)
        Wa = jax.random.normal(ks[7], (T, 2 * OUT, IN), jnp.float32) * s
        ba = jnp.zeros((T, IN), jnp.float32)
        gamma = jnp.ones((T, IN), jnp.float32)
        beta = jnp.zeros((T, IN), jnp.float32)
        w_time = jnp.asarray(1.0 / 10 ** np.linspace(0, 1.5, TD), jnp.float32)
        b_time = jnp.zeros((TD,), jnp.float32)
        return dict(x=x, node_type=node_type, edge_index=edge_index, edge_attr=edge_attr, Wk=Wk, bk=bk, Wq=Wq, bq=bq, Wv=Wv, bv=bv, Wa=Wa, ba=ba, gamma=gamma, beta=beta, w_time=w_time, b_time=b_time)
    _L0_gnn_all = _L0_gnn_setup()
    _L0_gnn_in = {k: v for k, v in _L0_gnn_all.items() if k in ('Wk', 'bk', 'Wq', 'bq', 'Wv', 'bv', 'Wa', 'ba', 'gamma', 'beta', 'w_time', 'b_time')}
    del _L0_gnn_all

    def _L0_ffn_setup():
        import jax, jax.numpy as jnp
        import numpy as np
        B, S, H, F, E, K = (8, 128, 256, 512, 16, 2)
        EPS = 1e-05
        key = jax.random.key(seed)
        ks = jax.random.split(key, 9)
        sc = 0.02
        return {'x': jax.random.normal(ks[0], (B, S, H), dtype=jnp.float32), 'gate_w': jax.random.normal(ks[1], (H, E), dtype=jnp.float32) * sc, 'gate_b': jnp.zeros((E,), dtype=jnp.float32), 'w1': jax.random.normal(ks[2], (E, H, F), dtype=jnp.float32) * sc, 'b1': jnp.zeros((E, F), dtype=jnp.float32), 'w2': jax.random.normal(ks[3], (E, F, H), dtype=jnp.float32) * sc, 'b2': jnp.zeros((E, H), dtype=jnp.float32), 'gamma': jnp.ones((H,), dtype=jnp.float32), 'beta': jnp.zeros((H,), dtype=jnp.float32)}
    _L0_ffn_all = _L0_ffn_setup()
    _L0_ffn_in = {k: v for k, v in _L0_ffn_all.items() if k in ('gate_w', 'gate_b', 'w1', 'b1', 'w2', 'b2', 'gamma', 'beta')}
    del _L0_ffn_all
    return {'x': x, 'src': src, 'dst': dst, 'edge_attr_5': edge_attr_5, 'node_type_19': node_type_19, 'L0_gnn_Wk': _L0_gnn_in['Wk'], 'L0_gnn_bk': _L0_gnn_in['bk'], 'L0_gnn_Wq': _L0_gnn_in['Wq'], 'L0_gnn_bq': _L0_gnn_in['bq'], 'L0_gnn_Wv': _L0_gnn_in['Wv'], 'L0_gnn_bv': _L0_gnn_in['bv'], 'L0_gnn_Wa': _L0_gnn_in['Wa'], 'L0_gnn_ba': _L0_gnn_in['ba'], 'L0_gnn_gamma': _L0_gnn_in['gamma'], 'L0_gnn_beta': _L0_gnn_in['beta'], 'L0_gnn_w_time': _L0_gnn_in['w_time'], 'L0_gnn_b_time': _L0_gnn_in['b_time'], 'L0_ffn_gate_w': _L0_ffn_in['gate_w'], 'L0_ffn_gate_b': _L0_ffn_in['gate_b'], 'L0_ffn_w1': _L0_ffn_in['w1'], 'L0_ffn_b1': _L0_ffn_in['b1'], 'L0_ffn_w2': _L0_ffn_in['w2'], 'L0_ffn_b2': _L0_ffn_in['b2'], 'L0_ffn_gamma': _L0_ffn_in['gamma'], 'L0_ffn_beta': _L0_ffn_in['beta']}

def reference(x, src, dst, edge_attr_5, node_type_19, L0_gnn_Wk, L0_gnn_bk, L0_gnn_Wq, L0_gnn_bq, L0_gnn_Wv, L0_gnn_bv, L0_gnn_Wa, L0_gnn_ba, L0_gnn_gamma, L0_gnn_beta, L0_gnn_w_time, L0_gnn_b_time, L0_ffn_gate_w, L0_ffn_gate_b, L0_ffn_w1, L0_ffn_b1, L0_ffn_w2, L0_ffn_b2, L0_ffn_gamma, L0_ffn_beta):
    import jax
    import jax.numpy as jnp

    def _L0_gnn_ref(x, node_type, edge_index, edge_attr, Wk, bk, Wq, bq, Wv, bv, Wa, ba, gamma, beta, w_time, b_time):
        import jax, jax.numpy as jnp
        import numpy as np
        N = 1024
        E = 4096
        IN = 256
        OUT = 256
        TD = 32
        H = 4
        T = 19
        PROJ = OUT - 2 * TD
        DK = (OUT - TD) // H
        SQRT_DK = float(np.sqrt(DK))
        LN_EPS = 1e-05

        def time_emb(t, w, b):
            return jnp.cos(jnp.log(t + 1.0)[:, None] * w[None, :] + b[None, :])

        def typed_linear(x, W, b, node_type):
            out = jnp.zeros((x.shape[0], W.shape[2]), x.dtype)
            for t in range(W.shape[0]):
                out = jnp.where((node_type == t)[:, None], x @ W[t] + b[t], out)
            return out

        def seg_softmax(att, idx, n):
            m = jax.ops.segment_max(att, idx, num_segments=n)
            e = jnp.exp(att - m[idx])
            s = jax.ops.segment_sum(e, idx, num_segments=n)
            return e / (s[idx] + 1e-16)
        row, col = (edge_index[0], edge_index[1])
        n = x.shape[0]
        K = typed_linear(x, Wk, bk, node_type)
        Q = typed_linear(x, Wq, bq, node_type)
        V = typed_linear(x, Wv, bv, node_type)
        e0 = time_emb(edge_attr[:, 0], w_time, b_time)
        e1 = time_emb(edge_attr[:, 1], w_time, b_time)
        e2 = time_emb(edge_attr[:, 2], w_time, b_time)

        def edge_msgs(Kn, Qn, Vn, ek, eq):
            k = jnp.concatenate([Kn, ek], axis=1).reshape(-1, H, DK)
            q = jnp.concatenate([Qn, eq], axis=1).reshape(-1, H, DK)
            att = jnp.einsum('ehd,ed->eh', k, q.sum(axis=1)) / SQRT_DK
            v = jnp.concatenate([Vn, ek], axis=1).reshape(-1, H, DK)
            return (att, v)
        att, v = edge_msgs(K[row], Q[col], V[row], e1, e2)
        att_i, v_i = edge_msgs(K[col], Q[row], V[col], e2, e1)
        att = seg_softmax(att, col, n)
        att_i = seg_softmax(att_i, row, n)
        res = (v * att[:, :, None]).reshape(-1, H * DK)
        res = jnp.concatenate([res, e0], axis=1)
        res_i = (v_i * att_i[:, :, None]).reshape(-1, H * DK)
        res_i = jnp.concatenate([res_i, e0], axis=1)
        agg = jax.ops.segment_sum(res, col, num_segments=n) + jax.ops.segment_sum(res_i, row, num_segments=n)
        h = jnp.concatenate([agg, agg], axis=1)
        o = typed_linear(h, Wa, ba, node_type)
        y = o + x
        mu = y.mean(axis=-1, keepdims=True)
        var = y.var(axis=-1, keepdims=True)
        yn = (y - mu) / jnp.sqrt(var + LN_EPS)
        return yn * gamma[node_type] + beta[node_type]

    def _L0_ffn_ref(x, gate_w, gate_b, w1, b1, w2, b2, gamma, beta):
        import jax, jax.numpy as jnp
        import numpy as np
        B, S, H, F, E, K = (8, 128, 256, 512, 16, 2)
        EPS = 1e-05
        gate_logits = x @ gate_w + gate_b
        topk_vals, topk_idx = jax.lax.top_k(gate_logits, K)
        topk_w = jax.nn.softmax(topk_vals, axis=-1)
        h = jax.nn.relu(jnp.einsum('bsh,ehf->bsef', x, w1) + b1)
        expert_out = jnp.einsum('bsef,efh->bseh', h, w2) + b2
        sel = jnp.take_along_axis(expert_out, topk_idx[:, :, :, None], axis=2)
        moe = jnp.sum(topk_w[..., None] * sel, axis=2)
        y = x + moe
        mu = jnp.mean(y, axis=-1, keepdims=True)
        var = jnp.var(y, axis=-1, keepdims=True)
        return (y - mu) / jnp.sqrt(var + EPS) * gamma + beta
    edge_index = jnp.stack([src, dst])
    x = x + _L0_gnn_ref(_layernorm(x, axis=-1), node_type_19, edge_index, edge_attr_5, L0_gnn_Wk, L0_gnn_bk, L0_gnn_Wq, L0_gnn_bq, L0_gnn_Wv, L0_gnn_bv, L0_gnn_Wa, L0_gnn_ba, L0_gnn_gamma, L0_gnn_beta, L0_gnn_w_time, L0_gnn_b_time)
    x = x + _L0_ffn_ref(_layernorm(x, axis=-1)[None], L0_ffn_gate_w, L0_ffn_gate_b, L0_ffn_w1, L0_ffn_b1, L0_ffn_w2, L0_ffn_b2, L0_ffn_gamma, L0_ffn_beta)[0]
    return x

_drawn_inputs = setup_inputs


def setup_inputs(seed=0):
    import zlib

    import numpy as np

    out = dict(_drawn_inputs(seed))
    spreads = {'L0_gnn_bk': (0.0, 0.8),
     'L0_gnn_bq': (0.0, 0.8),
     'L0_gnn_bv': (0.0, 0.8),
     'L0_gnn_ba': (0.0, 0.47),
     'L0_gnn_gamma': (1.0, 0.2),
     'L0_gnn_beta': (0.0, 0.1),
     'L0_gnn_b_time': (0.0, 0.1),
     'L0_ffn_gate_b': (0.0, 0.301),
     'L0_ffn_b1': (0.0, 0.8),
     'L0_ffn_b2': (0.0, 0.283),
     'L0_ffn_gamma': (1.0, 0.2),
     'L0_ffn_beta': (0.0, 0.1)}
    factors = {'L0_gnn_Wk': 8.0, 'L0_gnn_Wq': 8.0, 'L0_gnn_Wv': 6.537}
    for name, (base, spread) in spreads.items():
        noise = np.random.default_rng([zlib.crc32(name.encode()), seed]).standard_normal(out[name].shape)
        drawn = base * np.exp(spread * noise) if base else spread * noise
        out[name] = jnp.asarray(drawn.astype(out[name].dtype))
    for name, factor in factors.items():
        out[name] = (out[name] * factor).astype(out[name].dtype)
    return out
```

```python
from contextlib import ExitStack

import concourse.bass as bass
from concourse import mybir

P = 128
F32 = mybir.dt.float32
BF16 = mybir.dt.bfloat16
I32 = mybir.dt.int32
ALU = mybir.AluOpType
ACT = mybir.ActivationFunctionType
AX_X = mybir.AxisListType.X
RMAX = bass.bass_isa.ReduceOp.max

NODES = 3125
EDGES = 50000
TILES = -(-NODES // P)
TYPES = 19
IN = 256
KC = IN // P
PROJ = 192
TD = 32
HEADS = 4
DK = 56
HD = HEADS * DK
HEAD_SCALE = 1.0 / 56.0 ** 0.5
EPS = 1e-5
WCOLS = 2 * PROJ + DK
ROW = 2 * HD
EXPERTS = 16
FF = 512
FC = FF // P

EC = 400
HG = 20
C = 4
BLOCKS = 2 * TILES
WIN = 8
WCOL = WIN * C
GMAX = -(-(2 * EDGES // C + BLOCKS + 4 * WIN) // 16) * 16
UNITS = EC // 4
PAD_SLOT = 1.3e7
ROUND = 1.5 * 2.0 ** 23
TWO_PI = 6.283185307179586
PEN = -1e30
MINIT = -1e20
PVW = HEADS * (DK + 1) + TD
TPG = 5
NG = TILES // TPG
HALF = TPG * P // 2
EW = KC * FF + FC * IN + FC


class Chain:

    def __init__(self, eng, sem):
        self.eng, self.sem, self.base, self.n = eng, sem, 0, 0

    def mark(self, ins):
        ins.then_inc(self.sem, 1)
        self.n += 1

    def wait(self):
        self.eng.wait_ge(self.sem, self.base + self.n)

    def link(self, ins):
        self.mark(ins)
        self.wait()

    def at(self, base):
        self.base, self.n = base, 0


def build(nc, cst, ids, attr, x, types, Wk, Wv, Wq, bk, bv, bq, Wa, ba, gb, wt, bt,
          gate_w, gate_b, ew, b2, fgb, out):
    with ExitStack() as ctx:
        def sb(name, shape, dt=F32):
            return ctx.enter_context(nc.sbuf_tensor(name, shape, dt))

        def sem(name):
            return ctx.enter_context(nc.semaphore(name))

        ell = nc.dram_tensor("ell", [GMAX * C * P, 4], F32, kind="Internal").ap()
        kv = nc.dram_tensor("kv", [TILES * P + 1, ROW], F32, kind="Internal").ap()
        ell_fill = ell.rearrange("(n p r) w -> n p (r w)", p=P, r=16 * C)
        ell_win = ell.rearrange("(n i p c) w -> n p i (c w)", i=WIN, p=P, c=C)

        con = sb("con", [P, 3 * P + 1])
        ident, iota, tri, pidx = con[:, 0:P], con[:, P:2 * P], con[:, 2 * P:3 * P], con[:, 3 * P:3 * P + 1]
        xn = sb("xn", [P, TILES, IN])
        qs = sb("qs", [P, TILES, DK])
        start_i = sb("start_i", [P, BLOCKS + 1], I32)
        fills_i = sb("fills_i", [P, 4], I32)
        stats = sb("stats", [P, TILES, 6])
        lnv = sb("lnv", [P, 6, TILES])
        mean, rstd = lnv[:, 0, :], lnv[:, 5, :]
        acc = sb("acc", [P, BLOCKS, HEADS, DK + 1])
        esum = sb("esum", [P, BLOCKS, TD])
        zero = sb("zero", [P, 256])
        dummy = sb("hold_in", [P, 4])
        init_done = sb("init_done", [P, 1])
        ones = sb("ones", [P, TILES])
        ones_row = sb("ones_row", [1, P])
        accflat = acc[:, :, :, :].rearrange("p a b c -> p (a b c)")

        ARENA = 26600
        arena = sb("arena", [P, ARENA])

        class Arena:

            def __init__(self, at=0):
                self.at = at

            def take(self, *shape, dt=F32):
                n = 1
                for s in shape:
                    n *= s
                words = n if dt != BF16 else (n + 1) // 2
                v = arena[:, self.at:self.at + words]
                self.at += words
                assert self.at <= ARENA, self.at
                if dt != F32:
                    v = v.bitcast(dt)
                if len(shape) == 2:
                    v = v.rearrange("p (a b) -> p a b", a=shape[0])
                elif len(shape) == 3:
                    v = v.rearrange("p (a b c) -> p a b c", a=shape[0], b=shape[1])
                elif len(shape) == 4:
                    v = v.rearrange("p (a b c d) -> p a b c d", a=shape[0], b=shape[1], c=shape[2])
                return v

        bank = [ctx.enter_context(nc.psum_tensor(f"bank{i}", [P, 512], F32)) for i in range(8)]

        s1 = Arena()
        ids_i = s1.take(2, EC, dt=I32)
        tmp_i = s1.take(2, EC, dt=I32)
        idf = s1.take(2, EC)
        hif = s1.take(2, EC)
        lohb = s1.take(2, EC, 2, dt=BF16)
        lof = s1.take(2, EC)
        pay = s1.take(2, EC, 4)
        pay_i = pay.bitcast(I32)
        ohl = s1.take(2, HG, P, dt=BF16)
        ohh = s1.take(2, HG, TILES + 1, dt=BF16)
        identb = s1.take(P, dt=BF16)
        lohs = s1.take(2, 4, 2, dt=BF16)
        oht = s1.take(2, 4, P)
        junk = s1.take(4, P)
        ohhf = s1.take(4, TILES)
        selp = s1.take(4, 2, TILES)
        selv = s1.take(4, 2)
        rank = s1.take(4)
        rtot = s1.take(4)
        rank_i = s1.take(4, dt=I32)
        quad_i = s1.take(4, dt=I32)
        quad = s1.take(4)
        padp = s1.take(4)
        slotf = s1.take(4)
        slot = s1.take(2, 4, dt=I32)
        stage = s1.take(2, 4, 4)
        stage_i = stage.bitcast(I32)
        base = s1.take(TILES)
        deg = s1.take(TILES)
        maxdeg = s1.take(TILES)
        chunks_i = s1.take(TILES, dt=I32)
        chunks = s1.take(TILES)
        startf = s1.take(BLOCKS + 1)
        fillf = s1.take(4)
        at_hist = s1.at
        hist = s1.take(EC, TILES)
        attr_sb = arena[:, at_hist:at_hist + EC * 5].rearrange("p (e w) -> p e w", w=5)
        excl = accflat[:, 0:EC * TILES].rearrange("p (e b) -> p e b", b=TILES)

        s2 = Arena()
        w_kvq = s2.take(KC, TYPES, WCOLS)
        at_q = s2.at
        q_rest = s2.take(KC, TYPES, PROJ - DK)
        xm = arena[:, at_q:at_q + TYPES * IN].rearrange("p (t k n) -> p t k n", t=TYPES, k=KC)
        b_kvq = s2.take(WCOLS)
        bq_rest = s2.take(PROJ - DK)
        xt = s2.take(KC, P)
        xtile = s2.take(2, IN)
        oh_type = s2.take(P)
        kvt = s2.take(ROW)
        typrow = accflat[:, 0:TILES * P]
        typrow_i = typrow.bitcast(I32)

        s3 = Arena()
        payw = s3.take(2 * WCOL, 4)
        payw_i = payw.bitcast(I32)
        emb = s3.take(2 * WCOL, 3, TD)
        rnd = s3.take(WCOL, 3, TD)
        valid = s3.take(2 * WCOL)
        penal = s3.take(2 * WCOL)
        idx = [s3.take(C, dt=I32) for _ in range(2)]
        rows = [s3.take(C, ROW) for _ in range(2)]
        qe = s3.take(C, DK)
        prod = s3.take(C, HEADS, DK)
        att = s3.take(C, HEADS)
        cmax = s3.take(HEADS)
        mrun = s3.take(HEADS)
        mnew = s3.take(HEADS)
        ex = [s3.take(C + 1, HEADS) for _ in range(2)]
        pe_ = [s3.take(C + 1, HEADS) for _ in range(2)]
        pv = [s3.take(C, PVW) for _ in range(2)]
        wtb = s3.take(2, TD)

        s4 = Arena()
        w_out = s4.take(KC, TYPES, IN)
        at_b = s4.at
        w_low = s4.take(TYPES, IN)
        xm4 = arena[:, at_b:at_b + TYPES * IN].rearrange("p (t k n) -> p t k n", t=TYPES, k=KC)
        b_out = s4.take(IN)
        gb_sb = s4.take(2 * IN)
        xt4 = s4.take(KC, P)
        xtile4 = s4.take(2, IN)
        oh_type4 = s4.take(P)
        part = s4.take(2, HD)
        inv = s4.take(BLOCKS, HEADS)
        typrow4 = s4.take(TILES * P)
        typrow4_i = typrow4.bitcast(I32)
        xraw = arena[:, 0:TILES * IN].rearrange("p (t n) -> p t n", t=TILES)
        ln4 = s4.take(2, IN)

        xn2 = accflat[:, 0:TILES * IN].rearrange("p (t n) -> p t n", t=TILES)
        s5 = Arena()
        xn2t = s5.take(KC, TILES * P)
        wexp = s5.take(2, EW)
        ht = s5.take(2, FC, TPG * P)
        moe = s5.take(TILES, IN)
        logit = s5.take(TILES, EXPERTS)
        sel1 = s5.take(TILES, EXPERTS)
        sel2 = s5.take(TILES, EXPERTS)
        cand = s5.take(TILES, EXPERTS)
        gate = s5.take(TILES, EXPERTS)
        top = s5.take(6, TILES)
        xt5 = s5.take(2, IN)
        tt5 = s5.take(2, KC, P)
        gw_sb = s5.take(KC, EXPERTS)
        gb16 = s5.take(EXPERTS)
        b2_sb = s5.take(IN)
        gt_sb = s5.take(P)
        gstat = s5.take(EXPERTS)
        fgb_sb = s5.take(2 * IN)

        names = """s_con s_ids s_attr s_x s_wt s_w s_typ s_out s_dve s_ln s_sq s_zero s_oh s_hps s_hcp s_deg s_mdeg
            s_start s_rows s_copy s_oht s_pg s_slot s_hold s_fill s_kvz s_log s_xtile s_tp s_xt s_mask s_kmm s_kout
            s_kvw s_ohty s_payw s_idx s_gap0 s_gap1 s_ang s_dvw s_emb s_ex s_pe s_pvd s_dv3 s_pa0 s_pa1 s_g0 s_g1
            s_pool3 s_sc0 s_sc1 s_agg s_init s_dvf s_dvs s_xn
            s_last s_w40 s_w41 s_w4m s_gb s_typ4 s_x4 s_tp4 s_xt4 s_m4 s_mm4 s_y4 s_oht4
            s_bn s_xraw s_gbp s_z4 s_x5 s_tp5 s_t5 s_w5 s_gps s_lg s_xn2 s_e5 s_e5d s_gst s_gtp
            s_gt s_b2p s_hp s_relu s_op s_acc5 s_we0 s_we1 s_o5 s_dv4 s_mo""".split()
        S = {n: sem(n) for n in names}
        s_g, s_gap, s_pa, s_sc = ([S[f"{n}{i}"] for i in range(2)] for n in ("s_g", "s_gap", "s_pa", "s_sc"))
        s_we, s_w4 = [S["s_we0"], S["s_we1"]], [S["s_w40"], S["s_w41"]]

        block = ctx.enter_context(nc.Block())
        GROUPS = EC // HG

        def chunk_range(eng, b):
            lo = eng.value_load(start_i[0:1, bass.ds(b, 1)], min_val=0, max_val=GMAX - 64)
            hi = eng.value_load(start_i[0:1, bass.ds(b + 1, 1)], min_val=1, max_val=GMAX - 48)
            return lo, hi

        def chunk_total(eng):
            return eng.value_load(start_i[0:1, BLOCKS:BLOCKS + 1], min_val=BLOCKS, max_val=GMAX - 48)

        def flat(ap):
            return ap.rearrange("p o n -> p (o n)")

        @block.sync
        def _(sp):
            sp.dma_start(con[:, :], cst).then_inc(S["s_con"], 16)
            sp.dma_start(ids_i, ids).then_inc(S["s_ids"], 16)
            sp.dma_start(attr_sb, attr).then_inc(S["s_attr"], 16)
            sp.dma_start(xn[:, :, :], x.rearrange("(t p) n -> p t n", p=P)).then_inc(S["s_x"], 16)
            sp.wait_ge(S["s_zero"], 1)
            for k in range(2):
                sp.dma_start(kv[0:1, HD * k:HD * k + HD], zero[0:1, 0:HD]).then_inc(S["s_kvz"], 16)
            for l in range(2):
                sp.wait_ge(S["s_start"], l + 1)
                lo = sp.value_load(fills_i[0:1, 2 * l:2 * l + 1], min_val=0, max_val=GMAX // 16 - 1)
                hi = sp.value_load(fills_i[0:1, 2 * l + 1:2 * l + 2], min_val=1, max_val=GMAX // 16)
                with sp.Fori(lo, hi, 1) as i:
                    sp.dma_start(ell_fill[bass.ds(i, 1), :, :].rearrange("o p w -> (o p) w"),
                                 zero[:, :]).then_inc(S["s_fill"], 16)
            sp.wait_ge(S["s_slot"], 2 * UNITS)
            sp.wait_ge(s_sc[0], 64 * UNITS)
            sp.wait_ge(s_sc[1], 64 * UNITS)
            for k in range(KC):
                sp.dma_start(w_kvq[:, k, :, 0:PROJ], Wk[:, k, :, :]).then_inc(S["s_w"], 16)
                sp.dma_start(w_kvq[:, k, :, PROJ:2 * PROJ], Wv[:, k, :, :]).then_inc(S["s_w"], 16)
                sp.dma_start(w_kvq[:, k, :, 2 * PROJ:WCOLS], Wq[:, k, :, 0:DK]).then_inc(S["s_w"], 16)
                sp.dma_start(q_rest[:, k, :, :], Wq[:, k, :, DK:PROJ]).then_inc(S["s_w"], 16)
            sp.dma_start(b_kvq[0:TYPES, 0:PROJ], bk).then_inc(S["s_w"], 16)
            sp.dma_start(b_kvq[0:TYPES, PROJ:2 * PROJ], bv).then_inc(S["s_w"], 16)
            sp.dma_start(b_kvq[0:TYPES, 2 * PROJ:WCOLS], bq[:, 0:DK]).then_inc(S["s_w"], 16)
            sp.dma_start(bq_rest[0:TYPES, :], bq[:, DK:PROJ]).then_inc(S["s_w"], 16)
            sp.dma_start(typrow_i, types.to_broadcast([P, TILES * P])).then_inc(S["s_typ"], 16)
            with sp.Fori(0, TILES, 1) as t:
                row = sp.snap(t * P + 1)
                sp.wait_ge(S["s_kout"], 3 * t + 3)
                sp.dma_start(kv[bass.ds(row, P), :], kvt).then_inc(S["s_kvw"], 16)
            sp.wait_ge(S["s_kvw"], 16 * TILES)
            total = chunk_total(sp)
            sp.dma_start(wtb[:, 0, :], wt.to_broadcast([P, TD])).then_inc(S["s_wt"], 16)
            sp.dma_start(wtb[:, 1, :], bt.to_broadcast([P, TD])).then_inc(S["s_wt"], 16)

            def window(w, at):
                sp.dma_start(payw[:, at, :].rearrange("p (i c) w -> p i (c w)", c=C),
                             ell_win[w, :, :, :].rearrange("o p i w -> (o p) i w")).then_inc(S["s_payw"], 16)

            window(slice(0, 1), slice(0, WCOL))
            sp.wait_ge(S["s_payw"], 16)
            window(slice(1, 2), slice(WCOL, 2 * WCOL))
            angles_done, indices_done, loaded = (sp.alloc_register(n) for n in ("ang", "ind", "load"))
            with sp.Fori(2, (total - 1) // WIN + 2, 1) as w:
                at, w_at = sp.snap((w % 2) * WCOL), sp.snap(w)
                sp.reg_mov(angles_done, w - 1)
                sp.reg_mov(indices_done, WIN * (w - 1))
                sp.reg_mov(loaded, 16 * w)
                sp.wait_ge(S["s_ang"], angles_done)
                sp.wait_ge(S["s_idx"], indices_done)
                sp.wait_ge(S["s_payw"], loaded)
                window(bass.ds(w_at, 1), bass.ds(at, WCOL))
            sp.wait_ge(S["s_last"], 1)
            sp.wait_ge(S["s_pool3"], 1)
            sp.wait_ge(S["s_payw"], 16 * ((total + WIN - 1) // WIN + 1))
            for k in range(KC):
                sp.dma_start(w_out[:, k, :, :], Wa[:, k, :, :]).then_inc(s_w4[k], 16)
                if k:
                    sp.wait_ge(S["s_w4m"], 1)
                sp.dma_start(w_low, Wa[:, KC + k, :, :]).then_inc(s_w4[k], 16)
            sp.dma_start(b_out[0:TYPES, :], ba).then_inc(S["s_gb"], 16)
            sp.dma_start(gb_sb[0:TYPES, :], gb).then_inc(S["s_gb"], 16)
            sp.dma_start(typrow4_i, types.to_broadcast([P, TILES * P])).then_inc(S["s_typ4"], 16)
            sp.wait_ge(S["s_mm4"], TYPES * TILES)
            sp.dma_start(xraw, x.rearrange("(t p) n -> p t n", p=P)).then_inc(S["s_xraw"], 16)
            sp.wait_ge(S["s_z4"], TILES)
            sp.dma_start(gw_sb, gate_w).then_inc(S["s_w5"], 16)
            sp.dma_start(gb16[0:1, :], gate_b).then_inc(S["s_w5"], 16)
            sp.dma_start(b2_sb[0:EXPERTS, :], b2).then_inc(S["s_w5"], 16)
            sp.dma_start(fgb_sb, fgb.to_broadcast([P, 2 * IN])).then_inc(S["s_w5"], 16)
            for b in range(2):
                sp.dma_start(wexp[:, b, :], ew[b, :, :]).then_inc(s_we[b], 16)
            with sp.Fori(1, EXPERTS // 2, 1) as e:
                for b in range(2):
                    sp.wait_ge(S["s_op"], (2 * e + b - 1) * TILES)
                    sp.dma_start(wexp[:, b, :], ew[bass.ds(2 * e + b, 1), :, :].rearrange("o p w -> (o p) w"))\
                        .then_inc(s_we[b], 16)
            out_t = out.rearrange("(t p) n -> t p n", p=P)
            with sp.Fori(0, TILES, 1) as t:
                sp.wait_ge(S["s_o5"], t + 1)
                sp.dma_start(out_t[bass.ds(t, 1), :, :].rearrange("o p n -> (o p) n"), flat(xn[:, bass.ds(t, 1), :]))\
                    .then_inc(S["s_out"], 16)
            sp.wait_ge(S["s_out"], 16 * TILES)
        @block.gpsimd
        def _(pool):
            pool.memset(dummy[:, :], 0.0).then_inc(S["s_hold"], 1)

            def hold(n):
                pool.wait_ge(S["s_hold"], n)
                pool.tensor_tensor(dummy[:, 0:1], dummy[:, 1:2], dummy[:, 2:3], ALU.add).then_inc(S["s_hold"], 1)

            for l in range(2):
                pool.wait_ge(S["s_deg"], l + 1)
                pool.partition_all_reduce(maxdeg, deg, P, RMAX).then_inc(S["s_mdeg"], 1)
                pool.wait_ge(S["s_start"], l + 1)
                hi = pool.value_load(fills_i[0:1, 2 * l + 1:2 * l + 2], min_val=1, max_val=GMAX // 16)
                pool.wait_ge(S["s_fill"], 16 * hi)
                hold(1 + l * (UNITS + 1))
                with pool.Fori(0, UNITS // 2, 1) as i:
                    for b in range(2):
                        pool.wait_ge(S["s_slot"], 2 * i + b + 1 + l * UNITS)
                        hold(2 * i + b + 2 + l * (UNITS + 1))
                        for c in range(4):
                            pool.indirect_dma_start(
                                out=ell, out_offset=bass.IndirectOffsetOnAxis(ap=slot[:, b, c:c + 1], axis=0),
                                in_=stage[:, b, c, :], in_offset=None, bounds_check=GMAX * C * P - 1,
                                oob_is_err=False).then_inc(s_sc[b], 16)
            total = chunk_total(pool)
            pool.wait_ge(S["s_kvw"], 16 * TILES)
            pool.wait_ge(S["s_kvz"], 32)

            HELD = 1 + 2 * (UNITS + 1)

            def gather(g, b):
                pool.wait_ge(S["s_payw"], 16 * (g // WIN + 1))
                pool.tensor_copy(idx[b], payw_i[:, bass.ds((g % (2 * WIN)) * C, C), 0:1]
                                 .rearrange("p c o -> p (c o)")).then_inc(S["s_idx"], 1)
                pool.wait_ge(S["s_idx"], g + 1)
                hold(g + HELD)
                for c in range(C):
                    pool.indirect_dma_start(
                        out=rows[b][:, c, :], out_offset=None, in_=kv,
                        in_offset=bass.IndirectOffsetOnAxis(ap=idx[b][:, c:c + 1], axis=0)).then_inc(s_g[b], 16)

            for b in range(2):
                gather(b, b)
            with pool.Fori(1, (total + 1) // 2, 1) as h:
                for b in range(2):
                    pool.wait_ge(S["s_pvd"], 2 * h + b - 1)
                    pool.wait_ge(s_g[b], 16 * C * h)
                    gather(2 * h + b, b)
            for b in range(2):
                pool.wait_ge(s_g[b], 16 * C * ((total + 1) // 2))
            hold(HELD + 2 * ((total + 1) // 2))
            pool.memset(dummy[:, 3:4], 0.0).then_inc(S["s_pool3"], 1)

        @block.scalar
        def _(act):
            act.wait_ge(S["s_attr"], 16)
            for l in range(2):
                for k, src in enumerate((0, 1 + l, 2 - l)):
                    act.activation(pay[:, l, :, 1 + k:2 + k], attr_sb[:, :, src:src + 1], ACT.Ln, bias=1.0)\
                        .then_inc(S["s_log"], 1)
            act.wait_ge(S["s_log"], 6)
            for l in range(2):
                with act.Fori(0, GROUPS // 2, 1) as i:
                    for b in range(2):
                        act.wait_ge(S["s_hps"], 2 * i + b + 1 + l * GROUPS)
                        act.copy(hist[:, bass.ds((2 * i + b) * HG, HG), :],
                                 bank[b][:, 0:HG * TILES].rearrange("p (e b) -> p e b", b=TILES))\
                            .then_inc(S["s_hcp"], 1)
            act.wait_ge(S["s_ln"], 1)
            act.activation(lnv[:, 4, :], lnv[:, 3, :], ACT.Sqrt).then_inc(S["s_sq"], 1)

            def typed_in(t, first=False):
                act.wait_ge(S["s_tp"], t + 1)
                if not first:
                    act.wait_ge(S["s_mask"], TYPES * t)
                act.copy(xt, bank[2][:, 0:IN].rearrange("p (k n) -> p k n", k=KC)).then_inc(S["s_xt"], 1)

            def kv_out(t, first=False):
                act.wait_ge(S["s_kmm"], TYPES * (t + 1))
                if not first:
                    act.wait_ge(S["s_kvw"], 16 * t)
                act.copy(kvt[:, 0:PROJ], bank[3][:, 0:PROJ]).then_inc(S["s_kout"], 1)
                act.copy(kvt[:, HD:HD + PROJ], bank[3][:, PROJ:2 * PROJ]).then_inc(S["s_kout"], 1)
                act.copy(flat(qs[:, bass.ds(t, 1), :]), bank[3][:, 2 * PROJ:WCOLS]).then_inc(S["s_kout"], 1)

            typed_in(0, True)
            typed_in(1)
            kv_out(0, True)
            with act.Fori(1, TILES - 1, 1) as t:
                typed_in(t + 1)
                kv_out(t)
            kv_out(TILES - 1)

            def cosines(w, at):
                act.wait_ge(S["s_ang"], w + 1)
                act.activation(emb[:, at, :, :], emb[:, at, :, :], ACT.Sin, scale=-TWO_PI).then_inc(S["s_emb"], 1)

            def attend(g, b):
                act.wait_ge(s_g[b], 16 * C * (g // 2 + 1))
                act.wait_ge(S["s_emb"], g // WIN + 1)
                src = emb[:, bass.ds((g % (2 * WIN)) * C, C), 1, :]
                for k in range(2):
                    act.copy(rows[b][:, :, HD * k + PROJ:HD * k + HD], src).then_inc(s_gap[b], 1)
                act.wait_ge(S["s_ex"], g + 1)
                act.activation(pe_[b], ex[b], ACT.Exp, scale=HEAD_SCALE).then_inc(S["s_pe"], 1)

            cosines(0, slice(0, WCOL))
            with act.Fori(0, BLOCKS, 1) as blk:
                lo, hi = chunk_range(act, blk)
                with act.Fori(lo, hi, 1) as g:
                    with act.If(g % 2 == 0):
                        attend(g, 0)
                    with act.Else():
                        attend(g, 1)
                    with act.If(g % WIN == WIN // 2):
                        cosines(g // WIN + 1, bass.ds(((g // WIN + 1) % 2) * WCOL, WCOL))
            def typed_in4(t, first=False):
                act.wait_ge(S["s_tp4"], t + 1)
                if not first:
                    act.wait_ge(S["s_m4"], TYPES * t)
                act.copy(xt4, bank[2][:, 0:IN].rearrange("p (k n) -> p k n", k=KC)).then_inc(S["s_xt4"], 1)

            typed_in4(0, True)
            with act.Fori(1, TILES, 1) as t:
                typed_in4(t)
            for n in range(2):
                act.wait_ge(S["s_ln"], n + 2)
                act.activation(lnv[:, 4, :], lnv[:, 3, :], ACT.Sqrt).then_inc(S["s_sq"], 1)

            def turned5(t, b):
                act.wait_ge(S["s_tp5"], t + 1)
                src = bank[b][:, 0:IN].rearrange("p (k n) -> p k n", k=KC)
                act.copy(tt5[:, b, :, :], src)
                act.copy(xn2t[:, :, bass.ds(t * P, P)], src).then_inc(S["s_t5"], 1)

            turned5(0, 0)
            with act.Fori(0, TILES // 2, 1) as i:
                for b in range(2):
                    turned5(2 * i + b + 1, 1 - b)
            act.wait_ge(S["s_e5"], 1)
            act.activation(top[:, 3, :], top[:, 2, :], ACT.Exp).then_inc(S["s_e5d"], 1)
            with act.Fori(0, TILES, 1) as t:
                act.wait_ge(S["s_gtp"], t + 1)
                act.copy(gt_sb[0:EXPERTS, :], bank[2][0:EXPERTS, 0:P]).then_inc(S["s_gt"], 1)

            def relu(e, b, gi, first=False):
                it = (2 * e + b) * NG + gi
                hb = (b * NG + gi) % 2
                for f in range(FC):
                    for hh in range(2):
                        act.wait_ge(S["s_hp"], it * FC * 2 + f * 2 + hh + 1)
                        if f == 0 and hh == 0 and not first:
                            act.wait_ge(S["s_op"], (it - 1) * TPG)
                        act.activation(ht[:, hb, f, hh * HALF:(hh + 1) * HALF], bank[2 * (f % 2) + hh][:, 0:HALF],
                                       ACT.Relu, bias=wexp[:, b, EW - FC + f:EW - FC + f + 1]).then_inc(S["s_relu"], 1)

            for b in range(2):
                for gi in range(NG):
                    relu(0, b, gi, b * NG + gi < 2)
            with act.Fori(1, EXPERTS // 2, 1) as e:
                for b in range(2):
                    for gi in range(NG):
                        relu(e, b, gi)
            act.wait_ge(S["s_ln"], 4)
            act.activation(lnv[:, 4, :], lnv[:, 3, :], ACT.Sqrt).then_inc(S["s_sq"], 1)
        @block.tensor
        def _(pe):
            def counts(n, b, l, first=False):
                pe.wait_ge(S["s_oh"], n + 1 + l * GROUPS)
                if not first:
                    pe.wait_ge(S["s_hcp"], n - 1 + l * GROUPS)
                for c in range(HG):
                    last = pe.matmul(bank[b][:, c * TILES:(c + 1) * TILES], ohl[:, b, c, :],
                                     ohh[:, b, c, 0:TILES], start=True, stop=True)
                last.then_inc(S["s_hps"], 1)

            def places(i, b, l):
                n = 2 * i + b + 1 + l * UNITS
                pe.wait_ge(S["s_rows"], n)
                for c in range(4):
                    pe.matmul(bank[2 + b][:, c * P:(c + 1) * P], lohs[:, b, c, 0:1].to_broadcast([P, P]),
                              identb, start=True, stop=True)
                for c in range(4):
                    pe.matmul(bank[4 + b][:, c * P:(c + 1) * P], lohs[:, b, c, 0:1].to_broadcast([P, P]),
                              identb, start=True, stop=False)
                    last = pe.matmul(bank[4 + b][:, c * P:(c + 1) * P], lohs[:, b, c, 1:2].to_broadcast([P, P]),
                                     identb, start=False, stop=True)
                last.then_inc(S["s_copy"], 1)
                pe.wait_ge(S["s_oht"], n)
                for c in range(4):
                    pe.matmul(bank[6 + b][:, (2 * c) * TILES:(2 * c + 1) * TILES], oht[:, b, c, :],
                              flat(excl[:, bass.ds((2 * i + b) * 4 + c, 1), :]), start=True, stop=True)
                    last = pe.matmul(bank[6 + b][:, (2 * c + 1) * TILES:(2 * c + 2) * TILES], oht[:, b, c, :],
                                     base, start=True, stop=True)
                last.then_inc(S["s_pg"], 1)

            for l in range(2):
                for b in range(2):
                    counts(b, b, l, l == 0)
                with pe.Fori(1, GROUPS // 2, 1) as i:
                    for b in range(2):
                        counts(2 * i + b, b, l)
                with pe.Fori(0, UNITS // 2, 1) as i:
                    for b in range(2):
                        places(i, b, l)

            def turn(t, b, first=False):
                pe.wait_ge(S["s_xtile"], t + 1)
                if not first:
                    pe.wait_ge(S["s_xt"], t)
                for k in range(KC):
                    last = pe.transpose(bank[2][:, k * P:(k + 1) * P], xtile[:, b, k * P:(k + 1) * P], ident)
                last.then_inc(S["s_tp"], 1)

            def typed(t, first=False):
                pe.wait_ge(S["s_ohty"], t + 1)
                if not first:
                    pe.wait_ge(S["s_kout"], 3 * t)
                pe.matmul(bank[3][:, 0:WCOLS], oh_type[0:TYPES, :], b_kvq[0:TYPES, :], start=True, stop=False)
                for y in range(TYPES):
                    pe.wait_ge(S["s_mask"], TYPES * t + y + 1)
                    for k in range(KC):
                        last = pe.matmul(bank[3][:, 0:WCOLS], xm[:, y, k, :], w_kvq[:, k, y, :], start=False,
                                         stop=(y == TYPES - 1 and k == KC - 1))
                    last.then_inc(S["s_kmm"], 1)

            turn(0, 0, True)
            turn(1, 1)
            typed(0, True)
            with pe.Fori(0, (TILES - 3) // 2, 1) as i:
                for b in range(2):
                    turn(2 * i + b + 2, b)
                    typed(2 * i + b + 1)
            turn(TILES - 1, (TILES - 1) % 2)
            typed(TILES - 2)
            typed(TILES - 1)

            def chunk(g, b):
                pe.wait_ge(S["s_pvd"], g + 1)
                for c in range(C):
                    last = pe.matmul(bank[b][:, 0:PVW], ident, pv[b][:, c, :], start=(c == 0), stop=(c == C - 1))
                last.then_inc(s_pa[b], 1)

            total = chunk_total(pe)
            pe.wait_ge(S["s_init"], 1)
            with pe.Fori(0, total, 1) as g:
                with pe.If(g % 2 == 0):
                    chunk(g, 0)
                with pe.Else():
                    chunk(g, 1)
            def turn4(t, b, first=False):
                pe.wait_ge(S["s_x4"], t + 1)
                if not first:
                    pe.wait_ge(S["s_xt4"], t)
                for k in range(KC):
                    last = pe.transpose(bank[2][:, k * P:(k + 1) * P], xtile4[:, b, k * P:(k + 1) * P], ident)
                last.then_inc(S["s_tp4"], 1)

            def typed4(t, first=False):
                pe.wait_ge(S["s_oht4"], t + 1)
                if not first:
                    pe.wait_ge(S["s_y4"], t)
                pe.matmul(bank[3][:, 0:IN], oh_type4[0:TYPES, :], b_out[0:TYPES, :], start=True, stop=False)
                for y in range(TYPES):
                    pe.wait_ge(S["s_m4"], TYPES * t + y + 1)
                    for k in range(KC):
                        last = pe.matmul(bank[3][:, 0:IN], xm4[:, y, k, :], w_out[:, k, y, :], start=False,
                                         stop=(y == TYPES - 1 and k == KC - 1))
                    last.then_inc(S["s_mm4"], 1)

            pe.wait_ge(S["s_gb"], 32)
            turn4(0, 0, True)
            turn4(1, 1)
            typed4(0, True)
            with pe.Fori(0, (TILES - 3) // 2, 1) as i:
                for b in range(2):
                    turn4(2 * i + b + 2, b)
                    typed4(2 * i + b + 1)
            turn4(TILES - 1, (TILES - 1) % 2)
            typed4(TILES - 2)
            typed4(TILES - 1)
            with pe.Fori(0, TILES, 1) as t:
                pe.wait_ge(S["s_oht4"], TILES + t + 1)
                pe.matmul(bank[4][:, 0:2 * IN], oh_type4[0:TYPES, :], gb_sb[0:TYPES, :], start=True, stop=True)\
                    .then_inc(S["s_gbp"], 1)

            def turn5(t, b):
                pe.wait_ge(S["s_x5"], t + 1)
                for k in range(KC):
                    last = pe.transpose(bank[b][:, k * P:(k + 1) * P], xt5[:, b, k * P:(k + 1) * P], ident)
                last.then_inc(S["s_tp5"], 1)

            def gates(t, b):
                pe.wait_ge(S["s_t5"], t + 1)
                for k in range(KC):
                    pe.matmul(bank[2 + b][:, 0:EXPERTS], tt5[:, b, k, :], gw_sb[:, k, :], start=(k == 0), stop=False)
                pe.matmul(bank[2 + b][:, 0:EXPERTS], ones_row[:, :], gb16[0:1, :], start=False, stop=True)\
                    .then_inc(S["s_gps"], 1)

            pe.wait_ge(S["s_w5"], 64)
            turn5(0, 0)
            with pe.Fori(0, TILES // 2, 1) as i:
                for b in range(2):
                    turn5(2 * i + b + 1, 1 - b)
                    gates(2 * i + b, b)
            gates(TILES - 1, 0)
            with pe.Fori(0, TILES, 1) as t:
                pe.wait_ge(S["s_gst"], t + 1)
                pe.transpose(bank[2][0:EXPERTS, 0:P], gstat, ident).then_inc(S["s_gtp"], 1)
                pe.wait_ge(S["s_gt"], t + 1)
                pe.matmul(bank[3][:, 0:IN], gt_sb[0:EXPERTS, :], b2_sb[0:EXPERTS, :], start=True, stop=True)\
                    .then_inc(S["s_b2p"], 1)

            def hidden(e, b, gi, first=False):
                it = (2 * e + b) * NG + gi
                if gi == 0:
                    pe.wait_ge(s_we[b], 16 * (e + 1))
                for f in range(FC):
                    for hh in range(2):
                        if not first or f > 1:
                            pe.wait_ge(S["s_relu"], it * FC * 2 + f * 2 + hh - 3)
                        for k in range(KC):
                            last = pe.matmul(bank[2 * (f % 2) + hh][:, 0:HALF],
                                             wexp[:, b, k * FF + f * P:k * FF + (f + 1) * P],
                                             xn2t[:, k, (2 * gi + hh) * HALF:(2 * gi + hh + 1) * HALF],
                                             start=(k == 0), stop=(k == KC - 1))
                        last.then_inc(S["s_hp"], 1)

            def outs(e, b, gi, first=False):
                it = (2 * e + b) * NG + gi
                hb = (b * NG + gi) % 2
                pe.wait_ge(S["s_relu"], (it + 1) * FC * 2)
                for ti in range(TPG):
                    if ti == TPG - 1:
                        pe.wait_ge(S["s_acc5"], it * TPG + 2)
                    elif not first:
                        pe.wait_ge(S["s_acc5"], (it - 1) * TPG + (ti if ti else TPG - 1) + 2)
                    place = bank[4 + ti % 4][:, (ti // 4) * IN:(ti // 4 + 1) * IN]
                    for f in range(FC):
                        last = pe.matmul(place, ht[:, hb, f, ti * P:(ti + 1) * P],
                                         wexp[:, b, KC * FF + f * IN:KC * FF + (f + 1) * IN],
                                         start=(f == 0), stop=(f == FC - 1))
                    last.then_inc(S["s_op"], 1)

            order = [(b, gi) for b in range(2) for gi in range(NG)]

            def pair(e, first=False, final=False):
                for n, (b, gi) in enumerate(order):
                    if n + 1 < len(order):
                        hidden(e, *order[n + 1])
                    elif not final:
                        hidden(e + 1, 0, 0)
                    outs(e, b, gi, first and n == 0)

            pe.wait_ge(S["s_mo"], TILES)
            hidden(0, 0, 0, True)
            pair(0, first=True)
            with pe.Fori(1, EXPERTS // 2 - 1, 1) as e:
                pair(e)
            pair(EXPERTS // 2 - 1, final=True)
        @block.vector
        def _(dve):
            ch = Chain(dve, S["s_dve"])
            dve.memset(zero[:, :], 0.0).then_inc(S["s_zero"], 1)
            ch.mark(dve.memset(ones[:, :], 1.0))
            ch.mark(dve.memset(ones_row[:, :], 1.0))
            dve.wait_ge(S["s_ids"], 16)
            dve.wait_ge(S["s_con"], 16)
            ch.mark(dve.tensor_copy(identb, ident))
            ch.mark(dve.tensor_copy(idf, ids_i))
            ch.link(dve.tensor_scalar(tmp_i, ids_i, P - 1, None, ALU.bitwise_and))
            ch.link(dve.tensor_copy(lof, tmp_i))
            ch.mark(dve.tensor_copy(lohb[:, :, :, 0], lof))
            ch.link(dve.tensor_scalar(tmp_i, ids_i, 7, None, ALU.logical_shift_right))
            ch.link(dve.tensor_copy(hif, tmp_i))
            ch.mark(dve.tensor_scalar(lohb[:, :, :, 1], hif, float(P), None, ALU.mult))
            for l in range(2):
                ch.mark(dve.tensor_scalar(pay_i[:, l, :, 0], ids_i[:, 1 - l, :], 1.0, None, ALU.add))
            ch.wait()

            def one_hots(n, b, l, first=False):
                if not first:
                    dve.wait_ge(S["s_hps"], n - 1 + l * GROUPS)
                at = bass.ds(n * HG, HG)
                dve.tensor_tensor(ohl[:, b, :, :], iota.unsqueeze(1).to_broadcast([P, HG, P]),
                                  lof[:, l, at].unsqueeze(2).to_broadcast([P, HG, P]), ALU.is_equal)
                dve.tensor_tensor(ohh[:, b, :, 0:TILES], iota[:, 0:TILES].unsqueeze(1).to_broadcast([P, HG, TILES]),
                                  hif[:, l, at].unsqueeze(2).to_broadcast([P, HG, TILES]), ALU.is_equal)\
                    .then_inc(S["s_oh"], 1)

            def row_parts(u, b, l):
                dve.tensor_copy(lohs[:, b, :, :], lohb[:, l, bass.ds(u * 4, 4), :]).then_inc(S["s_rows"], 1)

            def slots(u, b, l, first=False):
                at = bass.ds(u * 4, 4)
                n = u + 1 + l * UNITS
                dve.wait_ge(S["s_copy"], n)
                dve.tensor_scalar(oht[:, b, :, :], bank[2 + b][:, :].rearrange("p (c n) -> p c n", c=4), pidx, None,
                                  ALU.is_equal).then_inc(S["s_oht"], 1)
                for c in range(4):
                    ins = dve.scalar_tensor_tensor(junk[:, c, :], bank[4 + b][:, c * P:(c + 1) * P],
                                                   idf[:, l, bass.ds(u * 4 + c, 1)], tri, ALU.is_equal, ALU.mult,
                                                   accum_out=rank[:, c:c + 1])
                    ch.mark(ins)
                ch.link(dve.tensor_tensor(ohhf, iota[:, 0:TILES].unsqueeze(1).to_broadcast([P, 4, TILES]),
                                          hif[:, l, at].unsqueeze(2).to_broadcast([P, 4, TILES]), ALU.is_equal))
                dve.wait_ge(S["s_pg"], n)
                ch.link(dve.tensor_tensor(selp, bank[6 + b][:, 0:8 * TILES].rearrange("p (c k b) -> p c k b", c=4, k=2),
                                          ohhf.unsqueeze(2).to_broadcast([P, 4, 2, TILES]), ALU.mult))
                ch.link(dve.tensor_reduce(selv, selp, AX_X, ALU.add))
                ch.mark(dve.tensor_tensor(rtot, rank, selv[:, :, 0], ALU.add))
                ch.link(dve.tensor_scalar(padp, hif[:, l, at], float(TILES), PAD_SLOT, ALU.is_ge, ALU.mult))
                ch.link(dve.tensor_copy(rank_i, rtot))
                dve.tensor_scalar(quad_i, rank_i, 2, None, ALU.logical_shift_right).then_inc(S["s_dvf"], 1)
                dve.wait_ge(S["s_dvf"], 4 * (u + l * UNITS) + 1)
                dve.tensor_copy(quad, quad_i).then_inc(S["s_dvf"], 1)
                dve.wait_ge(S["s_dvf"], 4 * (u + l * UNITS) + 2)
                dve.scalar_tensor_tensor(slotf, quad, float((P - 1) * C), rtot, ALU.mult, ALU.add)\
                    .then_inc(S["s_dvf"], 1)
                dve.wait_ge(S["s_dvf"], 4 * (u + l * UNITS) + 3)
                dve.tensor_tensor(slotf, slotf, selv[:, :, 1], ALU.add).then_inc(S["s_dvf"], 1)
                dve.wait_ge(S["s_dvf"], 4 * (u + l * UNITS) + 4)
                if not first:
                    dve.wait_ge(s_sc[b], 64 * ((u + l * UNITS) // 2))
                ch.mark(dve.tensor_scalar(stage_i[:, b, :, :], pay_i[:, l, at, :], 0, None, ALU.bitwise_or))
                dve.tensor_tensor(slot[:, b, :], slotf, padp, ALU.add).then_inc(S["s_slot"], 1)

            dve.wait_ge(S["s_log"], 6)
            for l in range(2):
                for b in range(2):
                    one_hots(b, b, l, l == 0)
                with dve.Fori(1, GROUPS // 2, 1) as i:
                    for b in range(2):
                        one_hots(2 * i + b, b, l)
                dve.wait_ge(S["s_hcp"], GROUPS * (l + 1))
                with dve.Fori(0, TILES, 1) as t:
                    dve.tensor_tensor_scan(excl[:, :, bass.ds(t, 1)].rearrange("p e o -> p (e o)"),
                                           ones[:, 0:1].to_broadcast([P, EC]),
                                           hist[:, :, bass.ds(t, 1)].rearrange("p e o -> p (e o)"),
                                           0.0, ALU.mult, ALU.add).then_inc(S["s_agg"], 1)
                dve.wait_ge(S["s_agg"], TILES * (l + 1))
                dve.tensor_copy(deg, excl[:, EC - 1, :]).then_inc(S["s_deg"], 1)
                dve.wait_ge(S["s_deg"], l + 1)
                ch.link(dve.tensor_tensor(excl, excl, hist, ALU.subtract))
                dve.wait_ge(S["s_mdeg"], l + 1)
                if l == 0:
                    ch.mark(dve.memset(startf[:, 0:1], 0.0))
                ch.link(dve.tensor_scalar(chunks_i, maxdeg, float(C - 1), None, ALU.add))
                ch.link(dve.tensor_scalar(chunks_i, chunks_i, 2, None, ALU.logical_shift_right))
                ch.link(dve.tensor_copy(chunks, chunks_i))
                ch.link(dve.tensor_scalar(chunks, chunks, 1.0, None, ALU.max))
                o = l * TILES
                ch.link(dve.tensor_tensor_scan(startf[:, o + 1:o + TILES + 1], ones[:, :], chunks,
                                               startf[:, o:o + 1], ALU.mult, ALU.add))
                ch.mark(dve.tensor_copy(start_i[:, o:o + TILES + 1], startf[:, o:o + TILES + 1]))
                ch.mark(dve.tensor_scalar(fillf[:, 1:2], startf[:, o + TILES:o + TILES + 1],
                                          float(15 + l * 24), None, ALU.add))
                ch.link(dve.tensor_scalar(base, startf[:, o:o + TILES], float(C * P), None, ALU.mult))
                ch.mark(dve.tensor_scalar(fillf[:, 0:1], pidx, float(C), None, ALU.mult))
                ch.link(dve.tensor_copy(fills_i[:, 2 * l + 1:2 * l + 2], fillf[:, 1:2]))
                ch.mark(dve.tensor_scalar(base, base, fillf[:, 0:1], None, ALU.add))
                ch.link(dve.tensor_scalar(fills_i[:, 2 * l + 1:2 * l + 2], fills_i[:, 2 * l + 1:2 * l + 2], 4, None,
                                          ALU.logical_shift_right))
                if l == 0:
                    ch.mark(dve.tensor_copy(fills_i[:, 2:3], fills_i[:, 1:2]))
                    ch.link(dve.memset(fills_i[:, 0:1], 0))
                dve.tensor_copy(fillf[:, 2:3], fillf[:, 1:2]).then_inc(S["s_start"], 1)
                row_parts(0, 0, l)
                k0 = ch.base + ch.n
                for b in range(2):
                    row_parts(b + 1, (b + 1) % 2, l)
                    slots(b, b, l, l == 0)
                per = ch.base + ch.n - k0
                with dve.Fori(1, UNITS // 2 - 1, 1) as i:
                    for b in range(2):
                        ch.at(k0 + i * per + b * (per // 2))
                        row_parts(2 * i + b + 1, (b + 1) % 2, l)
                        slots(2 * i + b, b, l)
                ch.at(k0 + (UNITS // 2 - 1) * per)
                row_parts(UNITS - 1, 1, l)
                slots(UNITS - 2, 0, l)
                slots(UNITS - 1, 1, l)

            def ln_rest(k):
                me, mo, ve, vo = (stats[:, :, j] for j in (1, 4, 2, 5))
                ch.mark(dve.tensor_tensor(lnv[:, 0, :], me, mo, ALU.add))
                ch.mark(dve.tensor_tensor(lnv[:, 1, :], me, mo, ALU.subtract))
                ch.link(dve.tensor_tensor(lnv[:, 2, :], ve, vo, ALU.add))
                ch.mark(dve.tensor_scalar(lnv[:, 0, :], lnv[:, 0, :], 0.5, None, ALU.mult))
                ch.mark(dve.tensor_tensor(lnv[:, 1, :], lnv[:, 1, :], lnv[:, 1, :], ALU.mult))
                ch.link(dve.tensor_scalar(lnv[:, 2, :], lnv[:, 2, :], 1.0 / IN, EPS, ALU.mult, ALU.add))
                dve.scalar_tensor_tensor(lnv[:, 3, :], lnv[:, 1, :], 0.25, lnv[:, 2, :], ALU.mult, ALU.add)\
                    .then_inc(S["s_ln"], 1)
                dve.wait_ge(S["s_sq"], k)
                ch.link(dve.reciprocal(lnv[:, 5, :], lnv[:, 4, :]))

            dve.wait_ge(S["s_x"], 16)
            with dve.Fori(0, TILES, 1) as t:
                dve.bn_stats(flat(stats[:, bass.ds(t, 1), :]), flat(xn[:, bass.ds(t, 1), :])).then_inc(S["s_dvs"], 1)
            dve.wait_ge(S["s_dvs"], TILES)
            ln_rest(1)

            dve.wait_ge(S["s_w"], 16 * 12)
            dve.wait_ge(S["s_typ"], 16)
            q = w_kvq[:, :, :, 2 * PROJ:WCOLS]
            qb = b_kvq[0:TYPES, 2 * PROJ:WCOLS]
            for j in range(3):
                n = min(DK, PROJ - DK - j * DK)
                ch.mark(dve.tensor_tensor(q[:, :, :, 0:n], q[:, :, :, 0:n], q_rest[:, :, :, j * DK:j * DK + n], ALU.add))
                ch.link(dve.tensor_tensor(qb[:, 0:n], qb[:, 0:n], bq_rest[0:TYPES, j * DK:j * DK + n], ALU.add))
            ch.mark(dve.tensor_copy(typrow, typrow_i))
            ch.link(dve.memset(kvt, 0.0))

            def tile_in(t, b, first=False):
                if not first:
                    dve.wait_ge(S["s_tp"], t - 1)
                tl = flat(xn[:, bass.ds(t, 1), :])
                dve.tensor_scalar(xtile[:, b, :], tl, mean[:, bass.ds(t, 1)], rstd[:, bass.ds(t, 1)],
                                  ALU.subtract, ALU.mult).then_inc(S["s_xtile"], 1)
                dve.wait_ge(S["s_xtile"], t + 1)
                dve.tensor_scalar(tl, xtile[:, b, :], 0.0, None, ALU.add).then_inc(S["s_xn"], 1)

            def masks(t, first=False):
                if not first:
                    dve.wait_ge(S["s_kmm"], TYPES * (t - 1) + 1)
                dve.tensor_scalar(oh_type[0:TYPES, :], typrow[0:TYPES, bass.ds(t * P, P)], pidx[0:TYPES, :], None,
                                  ALU.is_equal).then_inc(S["s_ohty"], 1)
                dve.wait_ge(S["s_xt"], t + 1)
                kinds = typrow[:, bass.ds(t * P, P)].unsqueeze(1).to_broadcast([P, KC, P])
                for y in range(TYPES):
                    if not first:
                        dve.wait_ge(S["s_kmm"], TYPES * (t - 1) + y + 1)
                    dve.scalar_tensor_tensor(xm[:, y, :, :], kinds, float(y), xt, ALU.is_equal, ALU.mult)\
                        .then_inc(S["s_mask"], 1)

            tile_in(0, 0, True)
            tile_in(1, 1, True)
            masks(0, True)
            tile_in(2, 0)
            with dve.Fori(0, (TILES - 3) // 2, 1) as i:
                for b in range(2):
                    masks(2 * i + b + 1)
                    tile_in(2 * i + b + 3, (b + 1) % 2)
            masks(TILES - 2)
            masks(TILES - 1)

            dve.wait_ge(S["s_kvw"], 16 * TILES)
            dve.wait_ge(S["s_xn"], TILES)
            dve.wait_ge(S["s_wt"], 32)
            ch.mark(dve.memset(acc[:, :, :, :], 0.0))
            ch.mark(dve.memset(esum[:, :, :], 0.0))
            ch.mark(dve.memset(pe_[1], 1.0))
            ch.mark(dve.tensor_scalar(wtb[:, 1, :], wtb[:, 1, :], TWO_PI / 4, None, ALU.add))
            ch.wait()
            ch.mark(dve.tensor_scalar(wtb, wtb, 1.0 / TWO_PI, None, ALU.mult))
            dve.memset(bank[1][:, :], 0.0).then_inc(s_pa[1], 1)
            dve.wait_ge(s_pa[1], 1)
            ch.link(dve.memset(mrun, MINIT))
            dve.memset(init_done[:, :], 0.0).then_inc(S["s_init"], 1)

            def angles(w, at):
                dve.wait_ge(S["s_payw"], 16 * (w + 1))
                em = emb[:, at, :, :]
                shape = [P, WCOL, 3, TD]
                dve.tensor_scalar(valid[:, at], payw_i[:, at, 0], 0.0, None, ALU.is_gt)
                dve.tensor_scalar(penal[:, at], payw_i[:, at, 0], 0.0, PEN, ALU.is_equal, ALU.mult)
                dve.tensor_tensor(em, payw[:, at, 1:4].unsqueeze(3).to_broadcast(shape),
                                  wtb[:, 0, :].unsqueeze(1).unsqueeze(1).to_broadcast(shape), ALU.mult)\
                    .then_inc(S["s_dvw"], 1)
                dve.wait_ge(S["s_dvw"], 3 * w + 1)
                dve.tensor_tensor(em, em, wtb[:, 1, :].unsqueeze(1).unsqueeze(1).to_broadcast(shape), ALU.add)\
                    .then_inc(S["s_dvw"], 1)
                dve.wait_ge(S["s_dvw"], 3 * w + 2)
                dve.tensor_scalar(rnd, em, ROUND, ROUND, ALU.add, ALU.subtract).then_inc(S["s_dvw"], 1)
                dve.wait_ge(S["s_dvw"], 3 * w + 3)
                dve.tensor_tensor(em, rnd, em, ALU.subtract).then_inc(S["s_ang"], 1)

            def fold(prev, b):
                tot = acc[:, bass.ds(prev, 1), :, :].rearrange("p o h d -> p (o h) d")
                es = flat(esum[:, bass.ds(prev, 1), :])
                c3.link(dve.tensor_tensor(tot, tot, pe_[b][:, C, :].unsqueeze(2).to_broadcast([P, HEADS, DK + 1]),
                                          ALU.mult))
                c3.mark(dve.tensor_tensor(tot, tot, bank[b][:, 0:PVW - TD].rearrange("p (h d) -> p h d", h=HEADS),
                                          ALU.add))
                c3.mark(dve.tensor_tensor(es, es, bank[b][:, PVW - TD:PVW], ALU.add))

            def chunk(g, b, tile, prev):
                at = bass.ds((g % (2 * WIN)) * C, C)
                own = flat(qs[:, bass.ds(tile, 1), :])
                dve.wait_ge(S["s_emb"], g // WIN + 1)
                c3.mark(dve.tensor_scalar(qe[:, :, 0:DK - TD], own[:, 0:DK - TD].unsqueeze(1).to_broadcast([P, C, DK - TD]),
                                          0.0, None, ALU.add))
                c3.link(dve.tensor_tensor(qe[:, :, DK - TD:DK], emb[:, at, 2, :],
                                          own[:, DK - TD:DK].unsqueeze(1).to_broadcast([P, C, TD]), ALU.add))
                dve.wait_ge(s_gap[b], 2 * (g // 2) + 2)
                keys = rows[b][:, :, 0:HD].rearrange("p c (h d) -> p c h d", h=HEADS)
                vals = rows[b][:, :, HD:ROW].rearrange("p c (h d) -> p c h d", h=HEADS)
                c3.link(dve.tensor_tensor(prod, keys, qe.unsqueeze(2).to_broadcast([P, C, HEADS, DK]), ALU.mult))
                c3.link(dve.tensor_reduce(att, prod, AX_X, ALU.add))
                c3.link(dve.tensor_tensor(att, att, penal[:, at].unsqueeze(2).to_broadcast([P, C, HEADS]), ALU.add))
                c3.link(dve.tensor_reduce(cmax, att.rearrange("p c h -> p h c"), AX_X, ALU.max))
                c3.link(dve.tensor_tensor(mnew, mrun, cmax, ALU.max))
                c3.mark(dve.tensor_tensor(ex[b][:, 0:C, :], att, mnew.unsqueeze(1).to_broadcast([P, C, HEADS]),
                                          ALU.subtract))
                dve.tensor_tensor(ex[b][:, C, :], mrun, mnew, ALU.subtract).then_inc(S["s_ex"], 1)
                dve.wait_ge(S["s_ex"], g + 1)
                c3.mark(dve.tensor_copy(mrun, mnew))
                dve.wait_ge(s_pa[1 - b], g // 2 + 1)
                fold(prev, 1 - b)
                dve.wait_ge(S["s_pe"], g + 1)
                w3 = pv[b][:, :, 0:PVW - TD].rearrange("p c (h d) -> p c h d", h=HEADS)
                c3.mark(dve.tensor_tensor(w3[:, :, :, 0:DK], vals, pe_[b][:, 0:C, :].unsqueeze(3)
                                          .to_broadcast([P, C, HEADS, DK]), ALU.mult))
                c3.mark(dve.tensor_copy(w3[:, :, :, DK], pe_[b][:, 0:C, :]))
                dve.tensor_tensor(pv[b][:, :, PVW - TD:PVW], emb[:, at, 0, :],
                                  valid[:, at].unsqueeze(2).to_broadcast([P, C, TD]), ALU.mult).then_inc(S["s_pvd"], 1)

            c3 = Chain(dve, S["s_dv3"])
            PER = 14
            total = chunk_total(dve)
            prev_reg = dve.alloc_register("prev_block")
            dve.reg_mov(prev_reg, 0)
            angles(0, slice(0, WCOL))
            with dve.Fori(0, 2, 1) as l:
                with dve.Fori(0, TILES, 1) as tile:
                    blk = l * TILES + tile
                    lo, hi = chunk_range(dve, blk)
                    dve.memset(mrun, MINIT).then_inc(S["s_dv3"], 1)
                    with dve.Fori(lo, hi, 1) as g:
                        with dve.If(g % WIN == 1):
                            dve.wait_ge(S["s_pvd"], g)
                            angles(g // WIN + 1, bass.ds(((g // WIN + 1) % 2) * WCOL, WCOL))
                        prev = dve.snap(prev_reg, min_val=0, max_val=BLOCKS - 1)
                        for b in range(2):
                            with (dve.Else() if b else dve.If(g % 2 == 0)):
                                c3.at(g * PER + blk + 1)
                                chunk(g, b, tile, prev)
                                assert c3.n == PER, c3.n
                        dve.reg_mov(prev_reg, blk)
            for b in range(2):
                with (dve.Else() if b else dve.If(total % 2 == 1)):
                    dve.wait_ge(s_pa[b], total // 2 + 1)
                    c3.at(total * PER + BLOCKS)
                    fold(BLOCKS - 1, b)
            dve.wait_ge(S["s_dv3"], total * PER + BLOCKS + 3)
            dve.wait_ge(S["s_pool3"], 1)
            ch.mark(dve.tensor_scalar(inv, acc[:, :, :, DK], 1e-16, None, ALU.add))
            dve.memset(init_done[:, :], 0.0).then_inc(S["s_last"], 1)
            ch.wait()
            ch.link(dve.reciprocal(inv, inv))
            for k in range(KC):
                dve.wait_ge(s_w4[k], 32)
                dve.tensor_tensor(w_out[:, k, :, :], w_out[:, k, :, :], w_low, ALU.add).then_inc(S["s_w4m"], 1)
            dve.wait_ge(S["s_typ4"], 16)
            dve.wait_ge(S["s_w4m"], KC)
            ch.link(dve.tensor_copy(typrow4, typrow4_i))

            def tile_in4(t, b, first=False):
                if not first:
                    dve.wait_ge(S["s_tp4"], t - 1)
                for l in range(2):
                    blk = bass.ds(t + l * TILES, 1)
                    c4.mark(dve.tensor_tensor(part[:, l, :].rearrange("p (h d) -> p h d", h=HEADS),
                                              acc[:, blk, :, 0:DK].rearrange("p o h d -> p (o h) d"),
                                              flat(inv[:, blk, :]).unsqueeze(2).to_broadcast([P, HEADS, DK]), ALU.mult))
                c4.wait()
                c4.link(dve.tensor_tensor(xtile4[:, b, 0:HD], part[:, 0, :], part[:, 1, :], ALU.add))
                dve.tensor_tensor(xtile4[:, b, HD:IN], flat(esum[:, bass.ds(t, 1), :]),
                                  flat(esum[:, bass.ds(t + TILES, 1), :]), ALU.add).then_inc(S["s_x4"], 1)

            def one_hot4(t):
                dve.tensor_scalar(oh_type4[0:TYPES, :], typrow4[0:TYPES, bass.ds(t * P, P)], pidx[0:TYPES, :], None,
                                  ALU.is_equal).then_inc(S["s_oht4"], 1)

            def masks4(t, first=False):
                if not first:
                    dve.wait_ge(S["s_mm4"], TYPES * (t - 1) + 1)
                one_hot4(t)
                dve.wait_ge(S["s_xt4"], t + 1)
                kinds = typrow4[:, bass.ds(t * P, P)].unsqueeze(1).to_broadcast([P, KC, P])
                for y in range(TYPES):
                    if not first:
                        dve.wait_ge(S["s_mm4"], TYPES * (t - 1) + y + 1)
                    dve.scalar_tensor_tensor(xm4[:, y, :, :], kinds, float(y), xt4, ALU.is_equal, ALU.mult)\
                        .then_inc(S["s_m4"], 1)

            def residual4(t):
                dve.wait_ge(S["s_mm4"], TYPES * (t + 1))
                tl = flat(xn[:, bass.ds(t, 1), :])
                dve.tensor_tensor(tl, bank[3][:, 0:IN], tl, ALU.add).then_inc(S["s_y4"], 1)
                dve.wait_ge(S["s_y4"], t + 1)
                dve.bn_stats(flat(stats[:, bass.ds(t, 1), :]), tl).then_inc(S["s_bn"], 1)

            c4 = Chain(dve, S["s_dv4"])
            PER4 = 3

            def step4(t, b, first=False):
                masks4(t, first)
                if not first:
                    residual4(t - 1)
                c4.at((t + 2) * PER4)
                tile_in4(t + 2, b)

            for t in range(2):
                c4.at(t * PER4)
                tile_in4(t, t, True)
            step4(0, 0, True)
            with dve.Fori(0, (TILES - 3) // 2, 1) as i:
                for b in range(2):
                    step4(2 * i + b + 1, 1 - b)
            for t in (TILES - 2, TILES - 1):
                masks4(t)
                residual4(t - 1)
            residual4(TILES - 1)
            dve.wait_ge(S["s_bn"], TILES)
            ln_rest(2)
            dve.wait_ge(S["s_xraw"], 16)
            c4.at(TILES * PER4)
            k4 = TILES * PER4

            def scale4(t, first=False):
                if not first:
                    dve.wait_ge(S["s_gbp"], t)
                one_hot4(t)
                c4.at(k4 + t * 4)
                tl, ti = flat(xn[:, bass.ds(t, 1), :]), bass.ds(t, 1)
                c4.link(dve.tensor_scalar(ln4[:, 0, :], tl, mean[:, ti], rstd[:, ti], ALU.subtract, ALU.mult))
                dve.wait_ge(S["s_gbp"], t + 1)
                c4.link(dve.tensor_tensor(ln4[:, 1, :], ln4[:, 0, :], bank[4][:, 0:IN], ALU.mult))
                c4.link(dve.tensor_tensor(ln4[:, 0, :], ln4[:, 1, :], bank[4][:, IN:2 * IN], ALU.add))
                c4.link(dve.tensor_tensor(tl, ln4[:, 0, :], xraw[:, ti, :].rearrange("p o n -> p (o n)"), ALU.add))
                dve.bn_stats(flat(stats[:, ti, :]), tl).then_inc(S["s_z4"], 1)

            scale4(0, True)
            with dve.Fori(1, TILES, 1) as t:
                scale4(t)
            dve.wait_ge(S["s_z4"], TILES)
            c4.at(k4 + TILES * 4)
            ln_rest(3)

            def tile_in5(t, b, first=False):
                if not first:
                    dve.wait_ge(S["s_tp5"], t - 1)
                ti = bass.ds(t, 1)
                dve.tensor_scalar(xt5[:, b, :], flat(xn[:, ti, :]), mean[:, ti], rstd[:, ti], ALU.subtract, ALU.mult)\
                    .then_inc(S["s_x5"], 1)
                dve.tensor_scalar(flat(xn2[:, ti, :]), flat(xn[:, ti, :]), mean[:, ti], rstd[:, ti],
                                  ALU.subtract, ALU.mult).then_inc(S["s_xn2"], 1)

            def logits(t, b):
                dve.wait_ge(S["s_gps"], t + 1)
                dve.tensor_scalar(flat(logit[:, bass.ds(t, 1), :]), bank[2 + b][:, 0:EXPERTS], 0.0, None, ALU.add)\
                    .then_inc(S["s_lg"], 1)

            tile_in5(0, 0, True)
            tile_in5(1, 1, True)
            with dve.Fori(0, (TILES - 3) // 2, 1) as i:
                for b in range(2):
                    logits(2 * i + b, b)
                    tile_in5(2 * i + b + 2, b)
            logits(TILES - 3, 0)
            tile_in5(TILES - 1, 0)
            logits(TILES - 2, 1)
            logits(TILES - 1, 0)
            dve.wait_ge(S["s_lg"], TILES)
            wide = [P, TILES, EXPERTS]
            rev = gstat
            ch.link(dve.tensor_scalar(rev, iota[:, 0:EXPERTS], -1.0, float(EXPERTS), ALU.mult, ALU.add))
            for k, sel in enumerate((sel1, sel2)):
                ch.link(dve.tensor_reduce(top[:, k, :], logit, AX_X, ALU.max))
                ch.link(dve.tensor_tensor(cand, logit, top[:, k, :].unsqueeze(2).to_broadcast(wide), ALU.is_equal))
                ch.link(dve.tensor_tensor(cand, cand, rev.unsqueeze(1).to_broadcast(wide), ALU.mult))
                ch.link(dve.tensor_reduce(top[:, 4, :], cand, AX_X, ALU.max))
                ch.link(dve.tensor_tensor(sel, cand, top[:, 4, :].unsqueeze(2).to_broadcast(wide), ALU.is_equal))
                if k == 0:
                    ch.link(dve.scalar_tensor_tensor(logit, sel, PEN, logit, ALU.mult, ALU.add))
            dve.tensor_tensor(top[:, 2, :], top[:, 1, :], top[:, 0, :], ALU.subtract).then_inc(S["s_e5"], 1)
            dve.wait_ge(S["s_e5d"], 1)
            ch.link(dve.tensor_scalar(top[:, 4, :], top[:, 3, :], 1.0, None, ALU.add))
            ch.link(dve.reciprocal(top[:, 4, :], top[:, 4, :]))
            ch.mark(dve.tensor_tensor(sel1, sel1, top[:, 4, :].unsqueeze(2).to_broadcast(wide), ALU.mult))
            ch.link(dve.tensor_tensor(top[:, 5, :], top[:, 3, :], top[:, 4, :], ALU.mult))
            ch.link(dve.tensor_tensor(sel2, sel2, top[:, 5, :].unsqueeze(2).to_broadcast(wide), ALU.mult))
            ch.link(dve.tensor_tensor(gate, sel1, sel2, ALU.add))

            def bias5(t, first=False):
                if not first:
                    dve.wait_ge(S["s_mo"], t)
                dve.tensor_scalar(gstat, flat(gate[:, bass.ds(t, 1), :]), 0.0, None, ALU.add).then_inc(S["s_gst"], 1)
                dve.wait_ge(S["s_b2p"], t + 1)
                dve.tensor_scalar(flat(moe[:, bass.ds(t, 1), :]), bank[3][:, 0:IN], 0.0, None, ALU.add)\
                    .then_inc(S["s_mo"], 1)

            bias5(0, True)
            with dve.Fori(1, TILES, 1) as t:
                bias5(t)
            dve.wait_ge(S["s_mo"], TILES)
            dve.memset(init_done[:, :], 0.0).then_inc(S["s_acc5"], 1)
            with dve.Fori(0, EXPERTS, 1) as e:
                for tile in range(TILES):
                    dve.wait_ge(S["s_op"], e * TILES + tile + 1)
                    dve.wait_ge(S["s_acc5"], e * TILES + tile + 1)
                    ti = tile % TPG
                    dve.scalar_tensor_tensor(moe[:, tile, :], bank[4 + ti % 4][:, (ti // 4) * IN:(ti // 4 + 1) * IN],
                                             gate[:, tile, bass.ds(e, 1)], moe[:, tile, :], ALU.mult, ALU.add)\
                        .then_inc(S["s_acc5"], 1)
            dve.wait_ge(S["s_acc5"], EXPERTS * TILES + 1)
            ch.link(dve.tensor_tensor(moe, moe, xn2, ALU.add))
            with dve.Fori(0, TILES, 1) as t:
                dve.bn_stats(flat(stats[:, bass.ds(t, 1), :]), flat(moe[:, bass.ds(t, 1), :])).then_inc(S["s_bn"], 1)
            dve.wait_ge(S["s_bn"], 2 * TILES)
            ln_rest(4)
            with dve.Fori(0, TILES, 1) as t:
                c4.at(k4 + TILES * 4 + t * 3)
                m, tl, ti = flat(moe[:, bass.ds(t, 1), :]), flat(xn[:, bass.ds(t, 1), :]), bass.ds(t, 1)
                c4.link(dve.tensor_scalar(m, m, mean[:, ti], rstd[:, ti], ALU.subtract, ALU.mult))
                c4.link(dve.tensor_tensor(m, m, fgb_sb[:, 0:IN], ALU.mult))
                c4.link(dve.tensor_tensor(m, m, fgb_sb[:, IN:2 * IN], ALU.add))
                dve.tensor_tensor(tl, tl, m, ALU.add).then_inc(S["s_o5"], 1)


def kernel(x, src, dst, edge_attr_5, node_type_19, L0_gnn_Wk, L0_gnn_bk, L0_gnn_Wq, L0_gnn_bq, L0_gnn_Wv, L0_gnn_bv,
           L0_gnn_Wa, L0_gnn_ba, L0_gnn_gamma, L0_gnn_beta, L0_gnn_w_time, L0_gnn_b_time, L0_ffn_gate_w,
           L0_ffn_gate_b, L0_ffn_w1, L0_ffn_b1, L0_ffn_w2, L0_ffn_b2, L0_ffn_gamma, L0_ffn_beta):
    import numpy as np
    import concourse.bacc as bacc
    from concourse import mybir as mb
    from concourse.bass_utils import run_bass_kernel_spmd as run

    def rows_first(a, *shape):
        return a

    f32 = np.float32
    a = np.arange(P)
    cst = np.concatenate([np.eye(P), np.broadcast_to(a, (P, P)), (a[None, :] < a[:, None]), a[:, None]], 1).astype(f32)
    pad_e = P * EC - EDGES
    edge = lambda v, fill: np.concatenate([np.asarray(v), np.full((pad_e,) + v.shape[1:], fill, np.asarray(v).dtype)])
    ids = np.stack([edge(dst, 4095).reshape(P, EC), edge(src, 4095).reshape(P, EC)], 1)
    attr = edge(edge_attr_5, 0).reshape(P, EC, 5)
    pad_n = TILES * P - NODES
    xp = np.concatenate([np.asarray(x), np.zeros((pad_n, IN), f32)])
    types = np.concatenate([np.asarray(node_type_19), np.zeros(pad_n, np.int32)])[None]
    by_type = lambda w: np.asarray(w).reshape(TYPES, -1, P, w.shape[-1]).transpose(2, 1, 0, 3)
    w1 = np.asarray(L0_ffn_w1).reshape(EXPERTS, KC, P, FF).transpose(0, 2, 1, 3).reshape(EXPERTS, P, KC * FF)
    w2 = np.asarray(L0_ffn_w2).reshape(EXPERTS, FC, P, IN).transpose(0, 2, 1, 3).reshape(EXPERTS, P, FC * IN)
    b1 = np.asarray(L0_ffn_b1).reshape(EXPERTS, FC, P).transpose(0, 2, 1)
    ins = dict(
        cst=cst, ids=ids, attr=attr, x=xp, types=types, Wk=by_type(L0_gnn_Wk), Wv=by_type(L0_gnn_Wv),
        Wq=by_type(L0_gnn_Wq), bk=L0_gnn_bk, bv=L0_gnn_bv, bq=L0_gnn_bq, Wa=by_type(L0_gnn_Wa), ba=L0_gnn_ba,
        gb=np.concatenate([np.asarray(L0_gnn_gamma), np.asarray(L0_gnn_beta)], 1),
        wt=np.asarray(L0_gnn_w_time)[None], bt=np.asarray(L0_gnn_b_time)[None],
        gate_w=np.asarray(L0_ffn_gate_w).reshape(KC, P, EXPERTS).transpose(1, 0, 2),
        gate_b=np.asarray(L0_ffn_gate_b)[None], ew=np.concatenate([w1, w2, b1], 2), b2=L0_ffn_b2,
        fgb=np.concatenate([np.asarray(L0_ffn_gamma), np.asarray(L0_ffn_beta)])[None])
    nc = bacc.Bacc("TRN2", target_bir_lowering=False, num_devices=1)
    arrays, args = {}, {}
    for name, v in ins.items():
        v = np.ascontiguousarray(v)
        arrays[f"in_{name}_dram"] = v
        args[name] = nc.dram_tensor(f"in_{name}_dram", v.shape, mb.dt.from_np(v.dtype), kind="ExternalInput").ap()
    args["out"] = nc.dram_tensor("out_dram", (TILES * P, IN), mb.dt.float32, kind="ExternalOutput").ap()
    build(nc, **args)
    r = run(nc, [arrays], core_ids=[0])
    return r.results[0]["out_dram"][:NODES]
```

```python
from contextlib import ExitStack

import concourse.bass as bass
from concourse import mybir

P = 128
F32 = mybir.dt.float32
BF16 = mybir.dt.bfloat16
I32 = mybir.dt.int32
ALU = mybir.AluOpType
ACT = mybir.ActivationFunctionType
AX_X = mybir.AxisListType.X
RMAX = bass.bass_isa.ReduceOp.max

NODES = 3125
EDGES = 50000
TILES = -(-NODES // P)
TYPES = 19
IN = 256
KC = IN // P
PROJ = 192
TD = 32
HEADS = 4
DK = 56
HD = HEADS * DK
HEAD_SCALE = 1.0 / 56.0 ** 0.5
EPS = 1e-5
WCOLS = 2 * PROJ + DK
ROW = 2 * HD
EXPERTS = 16
FF = 512
FC = FF // P

EC = 400
HG = 20
C = 4
BLOCKS = 2 * TILES
WIN = 8
WCOL = WIN * C
GMAX = -(-(2 * EDGES // C + BLOCKS + 4 * WIN) // 16) * 16
UNITS = EC // 4
TT = 2 * ((TILES + TYPES) // 2)
TCOLS = TT + 2
PAD_SLOT = 1.3e7
ROUND = 1.5 * 2.0 ** 23
TWO_PI = 6.283185307179586
PEN = -1e30
MINIT = -1e20
SUMW = HEADS * (DK + 1)
PVW = SUMW + TD
PAY = 5
PCOL = 2 * C
PW = 3 * TD
AHEAD = WIN // 2 + 2
RING = 4
TPG = 5
NG = TILES // TPG
HALF = TPG * P // 2
EW = KC * FF + FC * IN + FC


class Chain:

    def __init__(self, eng, sem):
        self.eng, self.sem, self.base, self.n = eng, sem, 0, 0

    def mark(self, ins):
        ins.then_inc(self.sem, 1)
        self.n += 1

    def wait(self, n=None):
        self.eng.wait_ge(self.sem, self.base + (self.n if n is None else n))

    def link(self, ins):
        self.mark(ins)
        self.wait()

    def at(self, base):
        self.base, self.n = base, 0


def build(nc, cst, ids, attr, x, types, types_col, Wk, Wv, Wq, bk, bv, bq, Wa, ba, gb, wt, bt,
          gate_w, gate_b, ew, b2, fgb, out):
    with ExitStack() as ctx:
        def sb(name, shape, dt=F32):
            return ctx.enter_context(nc.sbuf_tensor(name, shape, dt))

        def sem(name):
            return ctx.enter_context(nc.semaphore(name))

        ell = nc.dram_tensor("ell", [GMAX * C * P, PAY], F32, kind="Internal").ap()
        kv = nc.dram_tensor("kv", [TILES * P + 1, ROW], F32, kind="Internal").ap()
        order = nc.dram_tensor("order", [TCOLS * P, 1], I32, kind="Internal").ap()
        rows_in, agg_rows, out_rows = (nc.dram_tensor(n, [TILES * P + 1, IN], F32, kind="Internal").ap()
                                       for n in ("rows_in", "agg_rows", "out_rows"))
        ell_fill = ell.rearrange("(n p r) w -> n p (r w)", p=P, r=16 * C)
        ell_win = ell.rearrange("(n i p c) w -> n p i (c w)", i=WIN, p=P, c=C)

        con = sb("con", [P, 3 * P + 1 + 4 * PCOL])
        ident, iota, tri, pidx = con[:, 0:P], con[:, P:2 * P], con[:, 2 * P:3 * P], con[:, 3 * P:3 * P + 1]
        embsel = con[:, 3 * P + 1:]
        xn = sb("xn", [P, TILES, IN])
        qs = sb("qs", [P, TILES, DK])
        start_i = sb("start_i", [P, BLOCKS + 1], I32)
        fills_i = sb("fills_i", [P, 4], I32)
        stats = sb("stats", [P, TILES, 6])
        lnv = sb("lnv", [P, 6, TILES])
        mean, rstd = lnv[:, 0, :], lnv[:, 5, :]
        acc_all = sb("acc", [P, BLOCKS, PVW])
        acc = acc_all[:, :, 0:SUMW].rearrange("p b (h d) -> p b h d", h=HEADS)
        esum = acc_all[:, :, SUMW:PVW]
        ones_sq = sb("ones_sq", [P, P])
        zero = sb("zero", [P, 16 * C * PAY])
        dummy = sb("hold_in", [P, 4])
        init_done = sb("init_done", [P, 1])
        ones = sb("ones", [P, TILES])
        ones_row = sb("ones_row", [1, P])
        node_of = sb("node_of", [P, TCOLS], I32)
        tile_type = sb("tile_type", [P, TT])
        tile_type_i = sb("tile_type_i", [P, TT], I32)
        pairs_i = sb("pairs_i", [P, 1], I32)
        place_i = sb("place_i", [P, TILES], I32)
        row_i = sb("row_i", [P, TILES], I32)
        type_i = sb("type_i", [P, TILES], I32)
        idx_in, idx_out = ([sb(f"{n}{b}", [P, 1], I32) for b in range(2)] for n in ("idx_in", "idx_out"))
        rows_g = [sb(f"rows_g{b}", [P, IN]) for b in range(2)]
        rows_t = [sb(f"rows_t{b}", [P, KC, P]) for b in range(2)]
        rows_o = [sb(f"rows_o{b}", [P, ROW]) for b in range(2)]
        oh_tile = [sb(f"oh_tile{b}", [P, P]) for b in range(2)]
        accflat = acc_all[:, :, :].rearrange("p a b -> p (a b)")

        ARENA = 26600
        arena = sb("arena", [P, ARENA])

        class Arena:

            def __init__(self, at=0):
                self.at = at

            def take(self, *shape, dt=F32):
                n = 1
                for s in shape:
                    n *= s
                words = n if dt != BF16 else (n + 1) // 2
                v = arena[:, self.at:self.at + words]
                self.at += words
                assert self.at <= ARENA, self.at
                if dt != F32:
                    v = v.bitcast(dt)
                if len(shape) == 2:
                    v = v.rearrange("p (a b) -> p a b", a=shape[0])
                elif len(shape) == 3:
                    v = v.rearrange("p (a b c) -> p a b c", a=shape[0], b=shape[1])
                elif len(shape) == 4:
                    v = v.rearrange("p (a b c d) -> p a b c d", a=shape[0], b=shape[1], c=shape[2])
                return v

        bank = [ctx.enter_context(nc.psum_tensor(f"bank{i}", [P, 512], F32)) for i in range(8)]

        s1 = Arena()
        ids_i = s1.take(2, EC, dt=I32)
        tmp_i = s1.take(2, EC, dt=I32)
        idf = s1.take(2, EC)
        hif = s1.take(2, EC)
        lohb = s1.take(2, EC, 2, dt=BF16)
        lof = s1.take(2, EC)
        pay = s1.take(2, EC, PAY)
        pay_i = pay.bitcast(I32)
        ohl = s1.take(2, HG, P, dt=BF16)
        ohh = s1.take(2, HG, TILES + 1, dt=BF16)
        identb = s1.take(P, dt=BF16)
        lohs = s1.take(2, 4, 2, dt=BF16)
        oht = s1.take(2, 4, P)
        junk = s1.take(4, P)
        ohhf = s1.take(4, TILES)
        selp = s1.take(4, 2, TILES)
        selv = s1.take(4, 2)
        rank = s1.take(4)
        rtot = s1.take(4)
        rank_i = s1.take(4, dt=I32)
        quad_i = s1.take(4, dt=I32)
        quad = s1.take(4)
        padp = s1.take(4)
        slotf = s1.take(4)
        slot = s1.take(2, 4, dt=I32)
        stage = s1.take(2, 4, PAY)
        stage_i = stage.bitcast(I32)
        base = s1.take(TILES)
        deg = s1.take(TILES)
        maxdeg = s1.take(TILES)
        chunks_i = s1.take(TILES, dt=I32)
        chunks = s1.take(TILES)
        startf = s1.take(BLOCKS + 1)
        fillf = s1.take(4)
        at_hist = s1.at
        hist = s1.take(EC, TILES)
        attr_sb = arena[:, at_hist:at_hist + EC * 5].rearrange("p (e w) -> p e w", w=5)
        excl = accflat[:, 0:EC * TILES].rearrange("p (e b) -> p e b", b=TILES)

        s2 = Arena()
        w_kvq = s2.take(KC, TYPES, WCOLS)
        at_q = s2.at
        q_rest = s2.take(KC, TYPES, PROJ - DK)
        b_kvq = s2.take(WCOLS)
        bq_rest = s2.take(PROJ - DK)

        so_at = [EC * TILES]

        def so(*shape):
            n = shape[0] * (shape[1] if len(shape) > 1 else 1)
            v = accflat[:, so_at[0]:so_at[0] + n]
            so_at[0] += n
            return v if len(shape) == 1 else v.rearrange("p (a b) -> p a b", a=shape[0])

        type_f = so(TILES)
        oh_node = so(TILES, TYPES)
        tcount = so(TYPES, TILES + 1)
        tscan = so(TYPES, TILES + 1)
        tbefore = so(TILES, TYPES)
        tnum = so(4, TYPES)
        tnum_i = so(TYPES).bitcast(I32)
        tgrid = so(TT)
        tend = so(TT, TYPES)
        place = so(TILES)

        s3 = Arena()
        payw = s3.take(RING * WCOL, PAY)
        payw_i = payw.bitcast(I32)
        emb = s3.take(2 * WCOL, 3, TD)
        piece = s3.take(P)
        piecet = s3.take(P)
        rnd = s3.take(2, C * PW)
        embw = s3.take(PCOL, 3, TD)
        embb = s3.take(PCOL, 3, TD)
        penal = s3.take(2 * WCOL)
        roundc = s3.take(1)
        idx = [s3.take(C, dt=I32) for _ in range(4)]
        rows = s3.take(4 * C, ROW)
        qe = s3.take(C, DK)
        prod = s3.take(C, HEADS, DK)
        att = [s3.take(C + 1, HEADS) for _ in range(2)]
        ex = [s3.take(C + 1, HEADS) for _ in range(2)]
        pv = [s3.take(C, PVW) for _ in range(2)]
        pvh = [v[:, :, 0:SUMW].rearrange("p c (h d) -> p c h d", h=HEADS) for v in pv]
        wtb = s3.take(2, TD)
        rescale = s3.take(4, HEADS)

        s4 = Arena()
        w_out = s4.take(KC, TYPES, IN)
        w_low = s4.take(TYPES, IN)
        b_out = s4.take(IN)
        gb_sb = s4.take(2 * IN)
        agg = s4.take(TILES, IN)
        inv = s4.take(BLOCKS, HEADS)
        oh_type4 = s4.take(P)
        typrow4 = s4.take(TILES * P)
        typrow4_i = typrow4.bitcast(I32)
        xraw = arena[:, 0:TILES * IN].rearrange("p (t n) -> p t n", t=TILES)
        ln4 = s4.take(2, IN)

        xn2 = accflat[:, 0:TILES * IN].rearrange("p (t n) -> p t n", t=TILES)
        s5 = Arena()
        xn2t = s5.take(KC, TILES * P)
        wexp = s5.take(2, EW)
        ht = s5.take(2, FC, TPG * P)
        moe = s5.take(TILES, IN)
        logit = s5.take(TILES, EXPERTS)
        sel1 = s5.take(TILES, EXPERTS)
        sel2 = s5.take(TILES, EXPERTS)
        cand = s5.take(TILES, EXPERTS)
        gate = s5.take(TILES, EXPERTS)
        top = s5.take(6, TILES)
        xt5 = s5.take(2, IN)
        tt5 = s5.take(2, KC, P)
        gw_sb = s5.take(KC, EXPERTS)
        gb16 = s5.take(EXPERTS)
        b2_sb = s5.take(IN)
        gt_sb = s5.take(P)
        gstat = s5.take(EXPERTS)
        fgb_sb = s5.take(2 * IN)

        names = """s_types s_cnt s_cntp s_order s_full s_scat s_nodes s_rin s_fold s_qs s_aggd s_aggw s_od s_con s_ids s_attr s_x s_wt s_w s_typ s_out s_dve s_ln s_sq s_zero s_oh s_hps s_hcp s_deg s_mdeg
            s_start s_rows s_copy s_oht s_pg s_slot s_hold s_fill s_kvz s_log s_xtile s_tp s_xt s_mask s_kmm s_kout
            s_kvw s_ohty s_payw s_idx s_gap s_ang s_dvw s_emb s_ex s_pe s_pvd s_dv3 s_pa0 s_pa1 s_g0 s_g1 s_g2 s_g3 s_pvc s_ptp s_ptc s_pang s_rnd s_pen s_e0
            s_pool3 s_sc0 s_sc1 s_agg s_init s_dvf s_dvs s_xn
            s_last s_w40 s_w41 s_w4m s_gb s_typ4 s_x4 s_tp4 s_xt4 s_m4 s_mm4 s_y4 s_oht4
            s_bn s_xraw s_gbp s_z4 s_x5 s_tp5 s_t5 s_w5 s_gps s_lg s_xn2 s_e5 s_e5d s_gst s_gtp
            s_gt s_b2p s_hp s_relu s_op s_acc5 s_we0 s_we1 s_o5 s_dv4 s_mo""".split()
        S = {n: sem(n) for n in names}
        passes = [{n: sem(f"s_{n}_{name}") for n in ("idx_in", "idx_out", "in0", "in1", "turned", "rows", "onehot",
                                                     "product", "out", "put0", "put1")} for name in ("kvq", "out")]
        s_pa, s_sc = ([S[f"{n}{i}"] for i in range(2)] for n in ("s_pa", "s_sc"))
        s_g = [S[f"s_g{i}"] for i in range(4)]
        s_we, s_w4 = [S["s_we0"], S["s_we1"]], [S["s_w40"], S["s_w41"]]

        block = ctx.enter_context(nc.Block())
        GROUPS = EC // HG

        def chunk_range(eng, b):
            lo = eng.value_load(start_i[0:1, bass.ds(b, 1)], min_val=0, max_val=GMAX - 64)
            hi = eng.value_load(start_i[0:1, bass.ds(b + 1, 1)], min_val=1, max_val=GMAX - 48)
            return lo, hi

        def chunk_total(eng):
            return eng.value_load(start_i[0:1, BLOCKS:BLOCKS + 1], min_val=BLOCKS, max_val=GMAX - 48)

        def tile_pairs(eng):
            return eng.value_load(pairs_i[0:1, 0:1], min_val=TILES // 2, max_val=TT // 2)

        def flat(ap):
            return ap.rearrange("p o n -> p (o n)")

        @block.sync
        def _(sp):
            sp.dma_start(con[:, :], cst).then_inc(S["s_con"], 16)
            sp.dma_start(ids_i, ids).then_inc(S["s_ids"], 16)
            sp.dma_start(attr_sb, attr).then_inc(S["s_attr"], 16)
            sp.dma_start(xn[:, :, :], x.rearrange("(t p) n -> p t n", p=P)).then_inc(S["s_x"], 16)
            sp.dma_start(type_i[:, :], types_col).then_inc(S["s_types"], 16)
            sp.wait_ge(S["s_nodes"], 1)
            sp.dma_start(order.rearrange("(p j) o -> p (j o)", p=P), node_of[:, :]).then_inc(S["s_full"], 16)
            sp.wait_ge(S["s_zero"], 1)
            for k in range(2):
                sp.dma_start(kv[0:1, HD * k:HD * k + HD], zero[0:1, 0:HD]).then_inc(S["s_kvz"], 16)
            for table in (rows_in, agg_rows, out_rows):
                sp.dma_start(table[0:1, :], zero[0:1, 0:IN]).then_inc(S["s_kvz"], 16)
            for l in range(2):
                sp.wait_ge(S["s_start"], l + 1)
                lo = sp.value_load(fills_i[0:1, 2 * l:2 * l + 1], min_val=0, max_val=GMAX // 16 - 1)
                hi = sp.value_load(fills_i[0:1, 2 * l + 1:2 * l + 2], min_val=1, max_val=GMAX // 16)
                with sp.Fori(lo, hi, 1) as i:
                    sp.dma_start(ell_fill[bass.ds(i, 1), :, :].rearrange("o p w -> (o p) w"),
                                 zero[:, :]).then_inc(S["s_fill"], 16)
            sp.wait_ge(S["s_slot"], 2 * UNITS)
            sp.wait_ge(s_sc[0], 64 * UNITS)
            sp.wait_ge(s_sc[1], 64 * UNITS)
            for k in range(KC):
                sp.dma_start(w_kvq[:, k, :, 0:PROJ], Wk[:, k, :, :]).then_inc(S["s_w"], 16)
                sp.dma_start(w_kvq[:, k, :, PROJ:2 * PROJ], Wv[:, k, :, :]).then_inc(S["s_w"], 16)
                sp.dma_start(w_kvq[:, k, :, 2 * PROJ:WCOLS], Wq[:, k, :, 0:DK]).then_inc(S["s_w"], 16)
                sp.dma_start(q_rest[:, k, :, :], Wq[:, k, :, DK:PROJ]).then_inc(S["s_w"], 16)
            sp.dma_start(b_kvq[0:TYPES, 0:PROJ], bk).then_inc(S["s_w"], 16)
            sp.dma_start(b_kvq[0:TYPES, PROJ:2 * PROJ], bv).then_inc(S["s_w"], 16)
            sp.dma_start(b_kvq[0:TYPES, 2 * PROJ:WCOLS], bq[:, 0:DK]).then_inc(S["s_w"], 16)
            sp.dma_start(bq_rest[0:TYPES, :], bq[:, DK:PROJ]).then_inc(S["s_w"], 16)
            sp.wait_ge(S["s_scat"], 16 * TILES)
            sp.dma_start(node_of[:, :], order.rearrange("(p j) o -> p (j o)", p=P)).then_inc(S["s_full"], 16)
            sp.wait_ge(S["s_xn"], TILES)
            sp.dma_start(rows_in[1:, :].rearrange("(t p) n -> p t n", p=P), xn[:, :, :]).then_inc(S["s_rin"], 16)
            pairs = tile_pairs(sp)
            kvq, outp = passes
            for b in range(2):
                sp.wait_ge(kvq[f"put{b}"], 16 * pairs)
            for at, lo, n in ((PROJ, 0, TD), (HD + PROJ, TD, DK - TD)):
                sp.dma_start(qs[:, :, lo:lo + n], kv[1:, at:at + n].rearrange("(t p) n -> p t n", p=P))\
                    .then_inc(S["s_qs"], 16)
            total = chunk_total(sp)
            sp.wait_ge(kvq["product"], 2 * pairs)
            sp.dma_start(wtb[:, 0, :], wt.to_broadcast([P, TD])).then_inc(S["s_wt"], 16)
            sp.dma_start(wtb[:, 1, :], bt.to_broadcast([P, TD])).then_inc(S["s_wt"], 16)

            def window(w, at):
                sp.dma_start(payw[:, at, :].rearrange("p (i c) w -> p i (c w)", c=C),
                             ell_win[w, :, :, :].rearrange("o p i w -> (o p) i w")).then_inc(S["s_payw"], 16)

            for w in range(RING - 1):
                if w:
                    sp.wait_ge(S["s_payw"], 16 * w)
                window(slice(w, w + 1), slice(w * WCOL, (w + 1) * WCOL))
            pieces_done, indices_done, loaded = (sp.alloc_register(n) for n in ("pieces", "indices", "loaded"))
            with sp.Fori(RING - 1, (total - 1) // WIN + 3, 1) as w:
                at, w_at = sp.snap((w % RING) * WCOL), sp.snap(w)
                sp.reg_mov(pieces_done, (WIN // 2) * (w - RING + 2))
                sp.reg_mov(indices_done, WIN * (w - RING + 2))
                sp.reg_mov(loaded, 16 * w)
                sp.wait_ge(S["s_pvc"], pieces_done)
                sp.wait_ge(S["s_pen"], pieces_done)
                sp.wait_ge(S["s_idx"], indices_done)
                sp.wait_ge(S["s_payw"], loaded)
                window(bass.ds(w_at, 1), bass.ds(at, WCOL))
            sp.wait_ge(S["s_last"], 1)
            sp.wait_ge(S["s_pool3"], 1)
            sp.wait_ge(S["s_payw"], 16 * ((total + WIN - 1) // WIN + 2))
            for k in range(KC):
                sp.dma_start(w_out[:, k, :, :], Wa[:, k, :, :]).then_inc(s_w4[k], 16)
                if k:
                    sp.wait_ge(S["s_w4m"], 1)
                sp.dma_start(w_low, Wa[:, KC + k, :, :]).then_inc(s_w4[k], 16)
            sp.dma_start(b_out[0:TYPES, :], ba).then_inc(S["s_gb"], 16)
            sp.dma_start(gb_sb[0:TYPES, :], gb).then_inc(S["s_gb"], 16)
            sp.dma_start(typrow4_i, types.to_broadcast([P, TILES * P])).then_inc(S["s_typ4"], 16)
            sp.wait_ge(S["s_aggd"], 1)
            sp.dma_start(agg_rows[1:, :].rearrange("(t p) n -> p t n", p=P), agg).then_inc(S["s_aggw"], 16)
            for b in range(2):
                sp.wait_ge(outp[f"put{b}"], 16 * pairs)
            sp.dma_start(agg, out_rows[1:, :].rearrange("(t p) n -> p t n", p=P)).then_inc(S["s_od"], 16)
            sp.wait_ge(outp["product"], 2 * pairs)
            sp.dma_start(xraw, x.rearrange("(t p) n -> p t n", p=P)).then_inc(S["s_xraw"], 16)
            sp.wait_ge(S["s_z4"], TILES)
            sp.dma_start(gw_sb, gate_w).then_inc(S["s_w5"], 16)
            sp.dma_start(gb16[0:1, :], gate_b).then_inc(S["s_w5"], 16)
            sp.dma_start(b2_sb[0:EXPERTS, :], b2).then_inc(S["s_w5"], 16)
            sp.dma_start(fgb_sb, fgb.to_broadcast([P, 2 * IN])).then_inc(S["s_w5"], 16)
            for b in range(2):
                sp.dma_start(wexp[:, b, :], ew[b, :, :]).then_inc(s_we[b], 16)
            with sp.Fori(1, EXPERTS // 2, 1) as e:
                for b in range(2):
                    sp.wait_ge(S["s_op"], (2 * e + b - 1) * TILES)
                    sp.dma_start(wexp[:, b, :], ew[bass.ds(2 * e + b, 1), :, :].rearrange("o p w -> (o p) w"))\
                        .then_inc(s_we[b], 16)
            out_t = out.rearrange("(t p) n -> t p n", p=P)
            with sp.Fori(0, TILES, 1) as t:
                sp.wait_ge(S["s_o5"], t + 1)
                sp.dma_start(out_t[bass.ds(t, 1), :, :].rearrange("o p n -> (o p) n"), flat(xn[:, bass.ds(t, 1), :]))\
                    .then_inc(S["s_out"], 16)
            sp.wait_ge(S["s_out"], 16 * TILES)
        @block.gpsimd
        def _(pool):
            pool.memset(dummy[:, :], 0.0).then_inc(S["s_hold"], 1)

            def hold(n):
                pool.wait_ge(S["s_hold"], n)
                pool.tensor_tensor(dummy[:, 0:1], dummy[:, 1:2], dummy[:, 2:3], ALU.add).then_inc(S["s_hold"], 1)

            pool.wait_ge(S["s_order"], 1)
            pool.wait_ge(S["s_full"], 16)
            hold(1)
            for t in range(TILES):
                pool.indirect_dma_start(
                    out=order, out_offset=bass.IndirectOffsetOnAxis(ap=place_i[:, t:t + 1], axis=0),
                    in_=row_i[:, t:t + 1], in_offset=None, bounds_check=TCOLS * P - 1,
                    oob_is_err=False).then_inc(S["s_scat"], 16)
            pairs = tile_pairs(pool)

            for l in range(2):
                pool.wait_ge(S["s_deg"], l + 1)
                pool.partition_all_reduce(maxdeg, deg, P, RMAX).then_inc(S["s_mdeg"], 1)
                pool.wait_ge(S["s_start"], l + 1)
                hi = pool.value_load(fills_i[0:1, 2 * l + 1:2 * l + 2], min_val=1, max_val=GMAX // 16)
                pool.wait_ge(S["s_fill"], 16 * hi)
                hold(2 + l * (UNITS + 1))
                with pool.Fori(0, UNITS // 2, 1) as i:
                    for b in range(2):
                        pool.wait_ge(S["s_slot"], 2 * i + b + 1 + l * UNITS)
                        hold(2 * i + b + 3 + l * (UNITS + 1))
                        for c in range(4):
                            pool.indirect_dma_start(
                                out=ell, out_offset=bass.IndirectOffsetOnAxis(ap=slot[:, b, c:c + 1], axis=0),
                                in_=stage[:, b, c, :], in_offset=None, bounds_check=GMAX * C * P - 1,
                                oob_is_err=False).then_inc(s_sc[b], 16)
            def by_type(sems, table_in, table_out, width, held):
                def fetch(j, b, first=False):
                    if not first:
                        pool.wait_ge(sems[f"in{b}"], 16 * (j // 2))
                        pool.wait_ge(sems["turned"], j - 1)
                    pool.tensor_copy(idx_in[b][:, :], node_of[:, bass.ds(j, 1)]).then_inc(sems["idx_in"], 1)
                    pool.wait_ge(sems["idx_in"], j + 1)
                    hold(held(j))
                    pool.indirect_dma_start(
                        out=rows_g[b][:, :], out_offset=None, in_=table_in,
                        in_offset=bass.IndirectOffsetOnAxis(ap=idx_in[b][:, 0:1], axis=0),
                        bounds_check=TILES * P, oob_is_err=False).then_inc(sems[f"in{b}"], 16)

                def put(j, b, first=False):
                    if not first:
                        pool.wait_ge(sems[f"put{b}"], 16 * (j // 2))
                    pool.tensor_copy(idx_out[b][:, :], node_of[:, bass.ds(j, 1)]).then_inc(sems["idx_out"], 1)
                    pool.wait_ge(sems["idx_out"], j + 1)
                    pool.wait_ge(sems["out"], j + 1)
                    hold(held(j + 2) + 1)
                    pool.indirect_dma_start(
                        out=table_out, out_offset=bass.IndirectOffsetOnAxis(ap=idx_out[b][:, 0:1], axis=0),
                        in_=rows_o[b][:, 0:width], in_offset=None, bounds_check=TILES * P,
                        oob_is_err=False).then_inc(sems[f"put{b}"], 16)

                for b in range(2):
                    fetch(b, b, True)
                for b in range(2):
                    fetch(b + 2, b)
                    put(b, b, True)
                with pool.Fori(1, pairs, 1) as h:
                    for b in range(2):
                        fetch(2 * h + b + 2, b)
                        put(2 * h + b, b)
                for b in range(2):
                    pool.wait_ge(sems[f"in{b}"], 16 * (pairs + 1))
                    pool.wait_ge(sems[f"put{b}"], 16 * pairs)
                hold(held(2 * pairs + 2))

            def held_from(base):
                return lambda j: base + j if isinstance(j, int) and j < 2 else base + 2 * j - 2

            pool.wait_ge(S["s_full"], 32)
            pool.wait_ge(S["s_rin"], 16)
            pool.wait_ge(S["s_kvz"], 16 * 5)
            HELD2 = 2 + 2 * (UNITS + 1)
            total = chunk_total(pool)
            by_type(passes[0], rows_in, kv, ROW, held_from(HELD2))
            HELD = HELD2 + 4 * pairs + 3

            def gather(g, j):
                pool.wait_ge(S["s_payw"], 16 * (g // WIN + 1))
                pool.tensor_copy(idx[j], payw_i[:, bass.ds((g % (RING * WIN)) * C, C), 0:1]
                                 .rearrange("p c o -> p (c o)")).then_inc(S["s_idx"], 1)
                pool.wait_ge(S["s_idx"], g + 1)
                hold(g + HELD)
                for c in range(C):
                    pool.indirect_dma_start(
                        out=rows[:, j * C + c, :], out_offset=None, in_=kv,
                        in_offset=bass.IndirectOffsetOnAxis(ap=idx[j][:, c:c + 1], axis=0)).then_inc(s_g[j], 16)

            for j in range(4):
                if j == 3:
                    pool.wait_ge(S["s_pvd"], 1)
                gather(j, j)
            rounds = (total + 5) // 4
            with pool.Fori(1, rounds, 1) as h:
                for j in range(4):
                    pool.wait_ge(S["s_pvd"], 4 * h + j - 2)
                    pool.wait_ge(s_g[j], 16 * C * h)
                    gather(4 * h + j, j)
            for j in range(4):
                pool.wait_ge(s_g[j], 16 * C * rounds)
            hold(HELD + 4 * rounds)
            pool.memset(dummy[:, 3:4], 0.0).then_inc(S["s_pool3"], 1)
            pool.wait_ge(S["s_aggw"], 16)
            by_type(passes[1], agg_rows, out_rows, IN, held_from(HELD + 4 * rounds + 1))

        @block.scalar
        def _(act):
            act.wait_ge(S["s_attr"], 16)
            for l in range(2):
                for k, src in enumerate((0, 1 + l, 2 - l)):
                    act.activation(pay[:, l, :, 1 + k:2 + k], attr_sb[:, :, src:src + 1], ACT.Ln, bias=1.0)\
                        .then_inc(S["s_log"], 1)
            act.wait_ge(S["s_log"], 6)
            for l in range(2):
                with act.Fori(0, GROUPS // 2, 1) as i:
                    for b in range(2):
                        act.wait_ge(S["s_hps"], 2 * i + b + 1 + l * GROUPS)
                        act.copy(hist[:, bass.ds((2 * i + b) * HG, HG), :],
                                 bank[b][:, 0:HG * TILES].rearrange("p (e b) -> p e b", b=TILES))\
                            .then_inc(S["s_hcp"], 1)
            act.wait_ge(S["s_ln"], 1)
            act.activation(lnv[:, 4, :], lnv[:, 3, :], ACT.Sqrt).then_inc(S["s_sq"], 1)

            def by_type(sems, pieces):
                def turned(j, b, first=False):
                    act.wait_ge(sems["turned"], j + 1)
                    if not first:
                        act.wait_ge(sems["product"], j - 1)
                    act.copy(rows_t[b][:, :, :], bank[2][:, 0:IN].rearrange("p (k n) -> p k n", k=KC))\
                        .then_inc(sems["rows"], 1)

                def give(j, b, first=False):
                    act.wait_ge(sems["product"], j + 1)
                    if not first:
                        act.wait_ge(sems[f"put{b}"], 16 * (j // 2))
                    for to, at, n in pieces:
                        last = act.copy(rows_o[b][:, to:to + n], bank[3 + b][:, at:at + n])
                    last.then_inc(sems["out"], 1)

                turned(0, 0, True)
                turned(1, 1, True)
                give(0, 0, True)
                turned(2, 0)
                give(1, 1, True)
                with act.Fori(1, tile_pairs(act), 1) as h:
                    for b in range(2):
                        turned(2 * h + b + 1, 1 - b)
                        give(2 * h + b, b)

            act.wait_ge(S["s_fold"], 1)
            by_type(passes[0], ((0, 0, PROJ), (HD, PROJ, PROJ), (PROJ, 2 * PROJ, TD),
                                (HD + PROJ, 2 * PROJ + TD, DK - TD)))

            def piece_in(i):
                act.wait_ge(S["s_payw"], 16 * (i // (WIN // 2) + 1))
                if not (isinstance(i, int) and i == 0):
                    act.wait_ge(S["s_ptp"], i)
                act.copy(piece[:, 0:PCOL * PAY], payw[:, bass.ds((i % (RING * WIN // 2)) * PCOL, PCOL), :]
                         .rearrange("p c w -> p (c w)")).then_inc(S["s_pvc"], 1)

            def piece_turned(i):
                act.wait_ge(S["s_ptp"], i + 1)
                if not (isinstance(i, int) and i == 0):
                    act.wait_ge(S["s_pang"], i)
                act.copy(piecet[0:PCOL * PAY, :], bank[2][0:PCOL * PAY, 0:P]).then_inc(S["s_ptc"], 1)

            def rounded(i):
                act.wait_ge(S["s_pang"], i + 1)
                if not (isinstance(i, int) and i == 0):
                    act.wait_ge(S["s_ang"], i)
                act.activation(rnd[:, 0, :], bank[3][:, 0:C * PW], ACT.Identity, bias=roundc)
                act.activation(rnd[:, 1, :], bank[4][:, 0:C * PW], ACT.Identity, bias=roundc).then_inc(S["s_rnd"], 1)

            def cosines(w):
                act.wait_ge(S["s_ang"], (WIN // 2) * (w + 1))
                at = bass.ds((w % 2) * WCOL, WCOL)
                act.activation(emb[:, at, :, :], emb[:, at, :, :], ACT.Sin, scale=-TWO_PI).then_inc(S["s_emb"], 1)

            def embed_rows(g, j):
                act.wait_ge(s_g[j], 16 * C * (g // 4 + 1))
                act.wait_ge(S["s_emb"], g // WIN + 1)
                src = emb[:, bass.ds((g % (2 * WIN)) * C, C), 1, :]
                for k in range(2):
                    act.copy(rows[:, j * C:(j + 1) * C, HD * k + PROJ:HD * k + HD], src).then_inc(S["s_gap"], 1)

            def exponentials(g, b):
                act.wait_ge(S["s_ex"], g + 2)
                act.wait_ge(s_pa[b], g // 2 + 1)
                act.activation(pvh[b][:, 0:C, :, DK], ex[b][:, 0:C, :], ACT.Exp, scale=HEAD_SCALE)
                act.activation(rescale[:, bass.ds(g % 4, 1), :], ex[b][:, C:C + 1, :], ACT.Exp,
                               scale=HEAD_SCALE).then_inc(S["s_pe"], 1)
                act.copy(pv[b][:, 0:C, SUMW:PVW], emb[:, bass.ds((g % (2 * WIN)) * C, C), 0, :]).then_inc(S["s_e0"], 1)

            def attend(g, j):
                exponentials(g, j % 2)
                embed_rows(g + 2, (j + 2) % 4)
                if j % 2 == 0:
                    piece_in(g // 2 + AHEAD + 2)
                else:
                    piece_turned(g // 2 + AHEAD + 2)
                    rounded(g // 2 + AHEAD + 1)

            act.wait_ge(S["s_init"], 1)
            for i in range(AHEAD + 2):
                piece_in(i)
                piece_turned(i)
                if i < AHEAD + 1:
                    rounded(i)
            cosines(0)
            embed_rows(0, 0)
            embed_rows(1, 1)
            total = chunk_total(act)
            with act.Fori(0, total, 1) as g:
                with act.If(g % 2 == 0):
                    with act.If(g % 4 == 0):
                        attend(g, 0)
                    with act.Else():
                        attend(g, 2)
                    with act.If(g % WIN == 2):
                        cosines((g + 2 * AHEAD) // WIN)
                with act.Else():
                    with act.If(g % 4 == 1):
                        attend(g, 1)
                    with act.Else():
                        attend(g, 3)
            by_type(passes[1], ((0, 0, IN),))
            for n in range(2):
                act.wait_ge(S["s_ln"], n + 2)
                act.activation(lnv[:, 4, :], lnv[:, 3, :], ACT.Sqrt).then_inc(S["s_sq"], 1)

            def turned5(t, b):
                act.wait_ge(S["s_tp5"], t + 1)
                src = bank[b][:, 0:IN].rearrange("p (k n) -> p k n", k=KC)
                act.copy(tt5[:, b, :, :], src)
                act.copy(xn2t[:, :, bass.ds(t * P, P)], src).then_inc(S["s_t5"], 1)

            turned5(0, 0)
            with act.Fori(0, TILES // 2, 1) as i:
                for b in range(2):
                    turned5(2 * i + b + 1, 1 - b)
            act.wait_ge(S["s_e5"], 1)
            act.activation(top[:, 3, :], top[:, 2, :], ACT.Exp).then_inc(S["s_e5d"], 1)
            with act.Fori(0, TILES, 1) as t:
                act.wait_ge(S["s_gtp"], t + 1)
                act.copy(gt_sb[0:EXPERTS, :], bank[2][0:EXPERTS, 0:P]).then_inc(S["s_gt"], 1)

            def relu(e, b, gi, first=False):
                it = (2 * e + b) * NG + gi
                hb = (b * NG + gi) % 2
                for f in range(FC):
                    for hh in range(2):
                        act.wait_ge(S["s_hp"], it * FC * 2 + f * 2 + hh + 1)
                        if f == 0 and hh == 0 and not first:
                            act.wait_ge(S["s_op"], (it - 1) * TPG)
                        act.activation(ht[:, hb, f, hh * HALF:(hh + 1) * HALF], bank[2 * (f % 2) + hh][:, 0:HALF],
                                       ACT.Relu, bias=wexp[:, b, EW - FC + f:EW - FC + f + 1]).then_inc(S["s_relu"], 1)

            for b in range(2):
                for gi in range(NG):
                    relu(0, b, gi, b * NG + gi < 2)
            with act.Fori(1, EXPERTS // 2, 1) as e:
                for b in range(2):
                    for gi in range(NG):
                        relu(e, b, gi)
            act.wait_ge(S["s_ln"], 4)
            act.activation(lnv[:, 4, :], lnv[:, 3, :], ACT.Sqrt).then_inc(S["s_sq"], 1)
        @block.tensor
        def _(pe):
            pe.wait_ge(S["s_cnt"], 1)
            pe.matmul(bank[0][:, 0:TILES * TYPES], tri, oh_node.rearrange("p t y -> p (t y)"), start=True, stop=True)
            pe.matmul(bank[1][:, 0:TILES * TYPES], ones_sq[:, :], oh_node.rearrange("p t y -> p (t y)"),
                      start=True, stop=True).then_inc(S["s_cntp"], 1)
            pe.wait_ge(S["s_order"], 1)

            def counts(n, b, l, first=False):
                pe.wait_ge(S["s_oh"], n + 1 + l * GROUPS)
                if not first:
                    pe.wait_ge(S["s_hcp"], n - 1 + l * GROUPS)
                for c in range(HG):
                    last = pe.matmul(bank[b][:, c * TILES:(c + 1) * TILES], ohl[:, b, c, :],
                                     ohh[:, b, c, 0:TILES], start=True, stop=True)
                last.then_inc(S["s_hps"], 1)

            def places(i, b, l):
                n = 2 * i + b + 1 + l * UNITS
                pe.wait_ge(S["s_rows"], n)
                for c in range(4):
                    pe.matmul(bank[2 + b][:, c * P:(c + 1) * P], lohs[:, b, c, 0:1].to_broadcast([P, P]),
                              identb, start=True, stop=True)
                for c in range(4):
                    pe.matmul(bank[4 + b][:, c * P:(c + 1) * P], lohs[:, b, c, 0:1].to_broadcast([P, P]),
                              identb, start=True, stop=False)
                    last = pe.matmul(bank[4 + b][:, c * P:(c + 1) * P], lohs[:, b, c, 1:2].to_broadcast([P, P]),
                                     identb, start=False, stop=True)
                last.then_inc(S["s_copy"], 1)
                pe.wait_ge(S["s_oht"], n)
                for c in range(4):
                    pe.matmul(bank[6 + b][:, (2 * c) * TILES:(2 * c + 1) * TILES], oht[:, b, c, :],
                              flat(excl[:, bass.ds((2 * i + b) * 4 + c, 1), :]), start=True, stop=True)
                    last = pe.matmul(bank[6 + b][:, (2 * c + 1) * TILES:(2 * c + 2) * TILES], oht[:, b, c, :],
                                     base, start=True, stop=True)
                last.then_inc(S["s_pg"], 1)

            for l in range(2):
                for b in range(2):
                    counts(b, b, l, l == 0)
                with pe.Fori(1, GROUPS // 2, 1) as i:
                    for b in range(2):
                        counts(2 * i + b, b, l)
                with pe.Fori(0, UNITS // 2, 1) as i:
                    for b in range(2):
                        places(i, b, l)

            def by_type(sems, weights, bias, width):
                def turn(j, b, first=False):
                    pe.wait_ge(sems[f"in{b}"], 16 * (j // 2 + 1))
                    if not first:
                        pe.wait_ge(sems["rows"], j)
                    for k in range(KC):
                        last = pe.transpose(bank[2][:, k * P:(k + 1) * P], rows_g[b][:, k * P:(k + 1) * P], ident)
                    last.then_inc(sems["turned"], 1)

                def product(j, b, first=False):
                    kind = pe.value_load(tile_type_i[0:1, bass.ds(j, 1)], min_val=0, max_val=TYPES - 1)
                    pe.wait_ge(sems["onehot"], j + 1)
                    pe.wait_ge(sems["rows"], j + 1)
                    if not first:
                        pe.wait_ge(sems["out"], j - 1)
                    to = bank[3 + b][:, 0:width]
                    pe.matmul(to, oh_tile[b][0:TYPES, :], bias[0:TYPES, :], start=True, stop=False)
                    for k in range(KC):
                        last = pe.matmul(to, rows_t[b][:, k, :], weights[:, k, bass.ds(kind, 1), :]
                                         .rearrange("p o n -> p (o n)"), start=False, stop=(k == KC - 1))
                    last.then_inc(sems["product"], 1)

                turn(0, 0, True)
                turn(1, 1)
                product(0, 0, True)
                turn(2, 0)
                product(1, 1, True)
                pairs = tile_pairs(pe)
                with pe.Fori(1, pairs, 1) as h:
                    for b in range(2):
                        turn(2 * h + b + 1, 1 - b)
                        product(2 * h + b, b)

            def pass_out(sems):
                pairs = tile_pairs(pe)
                return (sems["rows"], 2 * pairs + 1), (sems["out"], 2 * pairs)

            pe.wait_ge(S["s_fold"], 1)
            total = chunk_total(pe)
            by_type(passes[0], w_kvq, b_kvq, WCOLS)

            def piece_turn(i):
                pe.wait_ge(S["s_pvc"], i + 1)
                if not (isinstance(i, int) and i == 0):
                    pe.wait_ge(S["s_ptc"], i)
                pe.transpose(bank[2][:, 0:P], piece, ident).then_inc(S["s_ptp"], 1)

            def piece_angles(i):
                pe.wait_ge(S["s_ptc"], i + 1)
                if not (isinstance(i, int) and i == 0):
                    pe.wait_ge(S["s_ang"], i)
                for k in range(2):
                    last = pe.matmul(bank[3 + k][:, 0:C * PW], piecet[0:PCOL * PAY, :],
                                     embw[0:PCOL * PAY, k * C:(k + 1) * C, :, :].rearrange("p c k d -> p (c k d)"),
                                     start=True, stop=True)
                last.then_inc(S["s_pang"], 1)

            def chunk(g, b):
                pe.wait_ge(S["s_pvd"], g + 2)
                pe.wait_ge(S["s_e0"], g + 1)
                for c in range(C):
                    last = pe.matmul(bank[b][:, 0:PVW], ident, pv[b][:, c, :], start=(c == 0), stop=(c == C - 1))
                last.then_inc(s_pa[b], 1)

            pe.wait_ge(S["s_init"], 1)
            for i in range(AHEAD + 2):
                piece_turn(i)
                piece_angles(i)
            with pe.Fori(0, total, 1) as g:
                with pe.If(g % 2 == 0):
                    chunk(g, 0)
                    piece_turn(g // 2 + AHEAD + 2)
                with pe.Else():
                    chunk(g, 1)
                    piece_angles(g // 2 + AHEAD + 2)
            pe.wait_ge(S["s_gb"], 32)
            pe.wait_ge(S["s_w4m"], KC)
            by_type(passes[1], w_out, b_out, IN)
            drained = pass_out(passes[1])
            with pe.Fori(0, TILES, 1) as t:
                pe.wait_ge(S["s_oht4"], t + 1)
                for given, n in drained:
                    pe.wait_ge(given, n)
                pe.matmul(bank[4][:, 0:2 * IN], oh_type4[0:TYPES, :], gb_sb[0:TYPES, :], start=True, stop=True)\
                    .then_inc(S["s_gbp"], 1)

            def turn5(t, b):
                pe.wait_ge(S["s_x5"], t + 1)
                for k in range(KC):
                    last = pe.transpose(bank[b][:, k * P:(k + 1) * P], xt5[:, b, k * P:(k + 1) * P], ident)
                last.then_inc(S["s_tp5"], 1)

            def gates(t, b):
                pe.wait_ge(S["s_t5"], t + 1)
                for k in range(KC):
                    pe.matmul(bank[2 + b][:, 0:EXPERTS], tt5[:, b, k, :], gw_sb[:, k, :], start=(k == 0), stop=False)
                pe.matmul(bank[2 + b][:, 0:EXPERTS], ones_row[:, :], gb16[0:1, :], start=False, stop=True)\
                    .then_inc(S["s_gps"], 1)

            pe.wait_ge(S["s_w5"], 64)
            turn5(0, 0)
            with pe.Fori(0, TILES // 2, 1) as i:
                for b in range(2):
                    turn5(2 * i + b + 1, 1 - b)
                    gates(2 * i + b, b)
            gates(TILES - 1, 0)
            with pe.Fori(0, TILES, 1) as t:
                pe.wait_ge(S["s_gst"], t + 1)
                pe.transpose(bank[2][0:EXPERTS, 0:P], gstat, ident).then_inc(S["s_gtp"], 1)
                pe.wait_ge(S["s_gt"], t + 1)
                pe.matmul(bank[3][:, 0:IN], gt_sb[0:EXPERTS, :], b2_sb[0:EXPERTS, :], start=True, stop=True)\
                    .then_inc(S["s_b2p"], 1)

            def hidden(e, b, gi, first=False):
                it = (2 * e + b) * NG + gi
                if gi == 0:
                    pe.wait_ge(s_we[b], 16 * (e + 1))
                for f in range(FC):
                    for hh in range(2):
                        if not first or f > 1:
                            pe.wait_ge(S["s_relu"], it * FC * 2 + f * 2 + hh - 3)
                        for k in range(KC):
                            last = pe.matmul(bank[2 * (f % 2) + hh][:, 0:HALF],
                                             wexp[:, b, k * FF + f * P:k * FF + (f + 1) * P],
                                             xn2t[:, k, (2 * gi + hh) * HALF:(2 * gi + hh + 1) * HALF],
                                             start=(k == 0), stop=(k == KC - 1))
                        last.then_inc(S["s_hp"], 1)

            def outs(e, b, gi, first=False):
                it = (2 * e + b) * NG + gi
                hb = (b * NG + gi) % 2
                pe.wait_ge(S["s_relu"], (it + 1) * FC * 2)
                for ti in range(TPG):
                    if ti == TPG - 1:
                        pe.wait_ge(S["s_acc5"], it * TPG + 2)
                    elif not first:
                        pe.wait_ge(S["s_acc5"], (it - 1) * TPG + (ti if ti else TPG - 1) + 2)
                    place = bank[4 + ti % 4][:, (ti // 4) * IN:(ti // 4 + 1) * IN]
                    for f in range(FC):
                        last = pe.matmul(place, ht[:, hb, f, ti * P:(ti + 1) * P],
                                         wexp[:, b, KC * FF + f * IN:KC * FF + (f + 1) * IN],
                                         start=(f == 0), stop=(f == FC - 1))
                    last.then_inc(S["s_op"], 1)

            order = [(b, gi) for b in range(2) for gi in range(NG)]

            def pair(e, first=False, final=False):
                for n, (b, gi) in enumerate(order):
                    if n + 1 < len(order):
                        hidden(e, *order[n + 1])
                    elif not final:
                        hidden(e + 1, 0, 0)
                    outs(e, b, gi, first and n == 0)

            pe.wait_ge(S["s_mo"], TILES)
            hidden(0, 0, 0, True)
            pair(0, first=True)
            with pe.Fori(1, EXPERTS // 2 - 1, 1) as e:
                pair(e)
            pair(EXPERTS // 2 - 1, final=True)
        @block.vector
        def _(dve):
            ch = Chain(dve, S["s_dve"])
            dve.memset(zero[:, :], 0.0).then_inc(S["s_zero"], 1)
            ch.mark(dve.memset(ones[:, :], 1.0))
            ch.mark(dve.memset(ones_row[:, :], 1.0))
            ch.mark(dve.memset(ones_sq[:, :], 1.0))
            dve.memset(node_of[:, :], 1 << 20).then_inc(S["s_nodes"], 1)
            for b in range(2):
                ch.mark(dve.memset(rows_g[b][:, :], 0.0))
                ch.mark(dve.memset(rows_o[b][:, :], 0.0))
            dve.wait_ge(S["s_types"], 16)
            dve.wait_ge(S["s_con"], 16)
            ch.link(dve.tensor_copy(type_f, type_i[:, :]))
            dve.tensor_tensor(oh_node, iota[:, 0:TYPES].unsqueeze(1).to_broadcast([P, TILES, TYPES]),
                              type_f.unsqueeze(2).to_broadcast([P, TILES, TYPES]), ALU.is_equal).then_inc(S["s_cnt"], 1)
            ch.mark(dve.tensor_scalar(tgrid, iota[:, 0:TT], float(P), None, ALU.mult))
            ch.mark(dve.tensor_scalar(place, iota[:, 0:TILES], float(P), 1.0, ALU.mult, ALU.add))
            ch.wait()
            ch.mark(dve.tensor_scalar(row_i[:, :], place, pidx, None, ALU.add))
            dve.wait_ge(S["s_cntp"], 1)
            by_y = lambda b_: bank[b_][:, 0:TILES * TYPES].rearrange("p (t y) -> p y t", y=TYPES)
            ch.link(dve.tensor_copy(tcount[:, :, 0:TILES], by_y(1)))
            ch.link(dve.tensor_reduce(tnum[:, 0, :], tcount[:, :, 0:TILES], AX_X, ALU.add))
            ch.link(dve.tensor_scalar(tnum_i, tnum[:, 0, :], float(P - 1), None, ALU.add))
            ch.link(dve.tensor_scalar(tnum_i, tnum_i, 7, None, ALU.logical_shift_right))
            ch.link(dve.tensor_copy(tnum[:, 1, :], tnum_i))
            ch.link(dve.scalar_tensor_tensor(tcount[:, :, TILES], tnum[:, 1, :], float(P), tnum[:, 0, :],
                                             ALU.mult, ALU.subtract))
            flat2 = lambda v: v.rearrange("p y t -> p (y t)")
            ch.link(dve.tensor_tensor_scan(flat2(tscan), ones_sq[:, 0:1].to_broadcast([P, TYPES * (TILES + 1)]),
                                           flat2(tcount), 0.0, ALU.mult, ALU.add))
            ch.mark(dve.tensor_tensor(tend, tscan[:, :, TILES].unsqueeze(1).to_broadcast([P, TT, TYPES]),
                                      tgrid.unsqueeze(2).to_broadcast([P, TT, TYPES]), ALU.is_le))
            ch.mark(dve.tensor_scalar(tnum_i[:, 0:1], tscan[:, TYPES - 1, TILES:TILES + 1], float(P), None, ALU.add))
            ch.link(dve.tensor_tensor(tcount, tscan, tcount, ALU.subtract))
            ch.mark(dve.tensor_scalar(pairs_i[:, :], tnum_i[:, 0:1], 8, None, ALU.logical_shift_right))
            ch.mark(dve.tensor_reduce(tile_type[:, :], tend, AX_X, ALU.add))
            ch.link(dve.tensor_tensor(tbefore, bank[0][:, 0:TILES * TYPES].rearrange("p (t y) -> p t y", y=TYPES),
                                      tcount[:, :, 0:TILES].rearrange("p y t -> p t y"), ALU.add))
            ch.mark(dve.tensor_scalar(tile_type[:, :], tile_type[:, :], float(TYPES - 1), None, ALU.min))
            ch.link(dve.tensor_tensor(tbefore, tbefore, oh_node, ALU.mult))
            ch.mark(dve.tensor_copy(tile_type_i[:, :], tile_type[:, :]))
            ch.link(dve.tensor_reduce(place, tbefore, AX_X, ALU.add))
            ch.link(dve.tensor_copy(place_i[:, :], place))
            ch.link(dve.tensor_scalar(place_i[:, :], place_i[:, :], 7, None, ALU.logical_shift_right))
            ch.link(dve.tensor_copy(type_f, place_i[:, :]))
            ch.link(dve.tensor_scalar(place, place, float(TCOLS), None, ALU.mult))
            ch.link(dve.scalar_tensor_tensor(place, type_f, float(1 - P * TCOLS), place, ALU.mult, ALU.add))
            dve.tensor_copy(place_i[:, :], place).then_inc(S["s_order"], 1)
            dve.wait_ge(S["s_ids"], 16)
            ch.mark(dve.tensor_copy(identb, ident))
            ch.mark(dve.tensor_copy(idf, ids_i))
            ch.link(dve.tensor_scalar(tmp_i, ids_i, P - 1, None, ALU.bitwise_and))
            ch.link(dve.tensor_copy(lof, tmp_i))
            ch.mark(dve.tensor_copy(lohb[:, :, :, 0], lof))
            ch.link(dve.tensor_scalar(tmp_i, ids_i, 7, None, ALU.logical_shift_right))
            ch.link(dve.tensor_copy(hif, tmp_i))
            ch.mark(dve.tensor_scalar(lohb[:, :, :, 1], hif, float(P), None, ALU.mult))
            for l in range(2):
                ch.mark(dve.tensor_scalar(pay_i[:, l, :, 0], ids_i[:, 1 - l, :], 1.0, None, ALU.add))
                ch.mark(dve.memset(pay[:, l, :, PAY - 1], 1.0))
            ch.wait()

            def one_hots(n, b, l, first=False):
                if not first:
                    dve.wait_ge(S["s_hps"], n - 1 + l * GROUPS)
                at = bass.ds(n * HG, HG)
                dve.tensor_tensor(ohl[:, b, :, :], iota.unsqueeze(1).to_broadcast([P, HG, P]),
                                  lof[:, l, at].unsqueeze(2).to_broadcast([P, HG, P]), ALU.is_equal)
                dve.tensor_tensor(ohh[:, b, :, 0:TILES], iota[:, 0:TILES].unsqueeze(1).to_broadcast([P, HG, TILES]),
                                  hif[:, l, at].unsqueeze(2).to_broadcast([P, HG, TILES]), ALU.is_equal)\
                    .then_inc(S["s_oh"], 1)

            def row_parts(u, b, l):
                dve.tensor_copy(lohs[:, b, :, :], lohb[:, l, bass.ds(u * 4, 4), :]).then_inc(S["s_rows"], 1)

            def slots(u, b, l, first=False):
                at = bass.ds(u * 4, 4)
                n = u + 1 + l * UNITS
                dve.wait_ge(S["s_copy"], n)
                dve.tensor_scalar(oht[:, b, :, :], bank[2 + b][:, :].rearrange("p (c n) -> p c n", c=4), pidx, None,
                                  ALU.is_equal).then_inc(S["s_oht"], 1)
                for c in range(4):
                    ins = dve.scalar_tensor_tensor(junk[:, c, :], bank[4 + b][:, c * P:(c + 1) * P],
                                                   idf[:, l, bass.ds(u * 4 + c, 1)], tri, ALU.is_equal, ALU.mult,
                                                   accum_out=rank[:, c:c + 1])
                    ch.mark(ins)
                ch.link(dve.tensor_tensor(ohhf, iota[:, 0:TILES].unsqueeze(1).to_broadcast([P, 4, TILES]),
                                          hif[:, l, at].unsqueeze(2).to_broadcast([P, 4, TILES]), ALU.is_equal))
                dve.wait_ge(S["s_pg"], n)
                ch.link(dve.tensor_tensor(selp, bank[6 + b][:, 0:8 * TILES].rearrange("p (c k b) -> p c k b", c=4, k=2),
                                          ohhf.unsqueeze(2).to_broadcast([P, 4, 2, TILES]), ALU.mult))
                ch.link(dve.tensor_reduce(selv, selp, AX_X, ALU.add))
                ch.mark(dve.tensor_tensor(rtot, rank, selv[:, :, 0], ALU.add))
                ch.link(dve.tensor_scalar(padp, hif[:, l, at], float(TILES), PAD_SLOT, ALU.is_ge, ALU.mult))
                ch.link(dve.tensor_copy(rank_i, rtot))
                dve.tensor_scalar(quad_i, rank_i, 2, None, ALU.logical_shift_right).then_inc(S["s_dvf"], 1)
                dve.wait_ge(S["s_dvf"], 4 * (u + l * UNITS) + 1)
                dve.tensor_copy(quad, quad_i).then_inc(S["s_dvf"], 1)
                dve.wait_ge(S["s_dvf"], 4 * (u + l * UNITS) + 2)
                dve.scalar_tensor_tensor(slotf, quad, float((P - 1) * C), rtot, ALU.mult, ALU.add)\
                    .then_inc(S["s_dvf"], 1)
                dve.wait_ge(S["s_dvf"], 4 * (u + l * UNITS) + 3)
                dve.tensor_tensor(slotf, slotf, selv[:, :, 1], ALU.add).then_inc(S["s_dvf"], 1)
                dve.wait_ge(S["s_dvf"], 4 * (u + l * UNITS) + 4)
                if not first:
                    dve.wait_ge(s_sc[b], 64 * ((u + l * UNITS) // 2))
                ch.mark(dve.tensor_scalar(stage_i[:, b, :, :], pay_i[:, l, at, :], 0, None, ALU.bitwise_or))
                dve.tensor_tensor(slot[:, b, :], slotf, padp, ALU.add).then_inc(S["s_slot"], 1)

            dve.wait_ge(S["s_log"], 6)
            for l in range(2):
                for b in range(2):
                    one_hots(b, b, l, l == 0)
                with dve.Fori(1, GROUPS // 2, 1) as i:
                    for b in range(2):
                        one_hots(2 * i + b, b, l)
                dve.wait_ge(S["s_hcp"], GROUPS * (l + 1))
                with dve.Fori(0, TILES, 1) as t:
                    dve.tensor_tensor_scan(excl[:, :, bass.ds(t, 1)].rearrange("p e o -> p (e o)"),
                                           ones[:, 0:1].to_broadcast([P, EC]),
                                           hist[:, :, bass.ds(t, 1)].rearrange("p e o -> p (e o)"),
                                           0.0, ALU.mult, ALU.add).then_inc(S["s_agg"], 1)
                dve.wait_ge(S["s_agg"], TILES * (l + 1))
                dve.tensor_copy(deg, excl[:, EC - 1, :]).then_inc(S["s_deg"], 1)
                dve.wait_ge(S["s_deg"], l + 1)
                ch.link(dve.tensor_tensor(excl, excl, hist, ALU.subtract))
                dve.wait_ge(S["s_mdeg"], l + 1)
                if l == 0:
                    ch.mark(dve.memset(startf[:, 0:1], 0.0))
                ch.link(dve.tensor_scalar(chunks_i, maxdeg, float(C - 1), None, ALU.add))
                ch.link(dve.tensor_scalar(chunks_i, chunks_i, 2, None, ALU.logical_shift_right))
                ch.link(dve.tensor_copy(chunks, chunks_i))
                ch.link(dve.tensor_scalar(chunks, chunks, 1.0, None, ALU.max))
                o = l * TILES
                ch.link(dve.tensor_tensor_scan(startf[:, o + 1:o + TILES + 1], ones[:, :], chunks,
                                               startf[:, o:o + 1], ALU.mult, ALU.add))
                ch.mark(dve.tensor_copy(start_i[:, o:o + TILES + 1], startf[:, o:o + TILES + 1]))
                ch.mark(dve.tensor_scalar(fillf[:, 1:2], startf[:, o + TILES:o + TILES + 1],
                                          float(15 + l * 24), None, ALU.add))
                ch.link(dve.tensor_scalar(base, startf[:, o:o + TILES], float(C * P), None, ALU.mult))
                ch.mark(dve.tensor_scalar(fillf[:, 0:1], pidx, float(C), None, ALU.mult))
                ch.link(dve.tensor_copy(fills_i[:, 2 * l + 1:2 * l + 2], fillf[:, 1:2]))
                ch.mark(dve.tensor_scalar(base, base, fillf[:, 0:1], None, ALU.add))
                ch.link(dve.tensor_scalar(fills_i[:, 2 * l + 1:2 * l + 2], fills_i[:, 2 * l + 1:2 * l + 2], 4, None,
                                          ALU.logical_shift_right))
                if l == 0:
                    ch.mark(dve.tensor_copy(fills_i[:, 2:3], fills_i[:, 1:2]))
                    ch.link(dve.memset(fills_i[:, 0:1], 0))
                dve.tensor_copy(fillf[:, 2:3], fillf[:, 1:2]).then_inc(S["s_start"], 1)
                row_parts(0, 0, l)
                k0 = ch.base + ch.n
                for b in range(2):
                    row_parts(b + 1, (b + 1) % 2, l)
                    slots(b, b, l, l == 0)
                per = ch.base + ch.n - k0
                with dve.Fori(1, UNITS // 2 - 1, 1) as i:
                    for b in range(2):
                        ch.at(k0 + i * per + b * (per // 2))
                        row_parts(2 * i + b + 1, (b + 1) % 2, l)
                        slots(2 * i + b, b, l)
                ch.at(k0 + (UNITS // 2 - 1) * per)
                row_parts(UNITS - 1, 1, l)
                slots(UNITS - 2, 0, l)
                slots(UNITS - 1, 1, l)

            def ln_rest(k):
                me, mo, ve, vo = (stats[:, :, j] for j in (1, 4, 2, 5))
                ch.mark(dve.tensor_tensor(lnv[:, 0, :], me, mo, ALU.add))
                ch.mark(dve.tensor_tensor(lnv[:, 1, :], me, mo, ALU.subtract))
                ch.link(dve.tensor_tensor(lnv[:, 2, :], ve, vo, ALU.add))
                ch.mark(dve.tensor_scalar(lnv[:, 0, :], lnv[:, 0, :], 0.5, None, ALU.mult))
                ch.mark(dve.tensor_tensor(lnv[:, 1, :], lnv[:, 1, :], lnv[:, 1, :], ALU.mult))
                ch.link(dve.tensor_scalar(lnv[:, 2, :], lnv[:, 2, :], 1.0 / IN, EPS, ALU.mult, ALU.add))
                dve.scalar_tensor_tensor(lnv[:, 3, :], lnv[:, 1, :], 0.25, lnv[:, 2, :], ALU.mult, ALU.add)\
                    .then_inc(S["s_ln"], 1)
                dve.wait_ge(S["s_sq"], k)
                ch.link(dve.reciprocal(lnv[:, 5, :], lnv[:, 4, :]))

            dve.wait_ge(S["s_x"], 16)
            with dve.Fori(0, TILES, 1) as t:
                dve.bn_stats(flat(stats[:, bass.ds(t, 1), :]), flat(xn[:, bass.ds(t, 1), :])).then_inc(S["s_dvs"], 1)
            dve.wait_ge(S["s_dvs"], TILES)
            ln_rest(1)

            with dve.Fori(0, TILES, 1) as t:
                tl, ti = flat(xn[:, bass.ds(t, 1), :]), bass.ds(t, 1)
                dve.tensor_scalar(tl, tl, mean[:, ti], rstd[:, ti], ALU.subtract, ALU.mult).then_inc(S["s_xn"], 1)
            dve.wait_ge(S["s_w"], 16 * 12)
            q = w_kvq[:, :, :, 2 * PROJ:WCOLS]
            qb = b_kvq[0:TYPES, 2 * PROJ:WCOLS]
            for j in range(3):
                n = min(DK, PROJ - DK - j * DK)
                ch.mark(dve.tensor_tensor(q[:, :, :, 0:n], q[:, :, :, 0:n], q_rest[:, :, :, j * DK:j * DK + n], ALU.add))
                ch.link(dve.tensor_tensor(qb[:, 0:n], qb[:, 0:n], bq_rest[0:TYPES, j * DK:j * DK + n], ALU.add))
            dve.memset(init_done[:, :], 0.0).then_inc(S["s_fold"], 1)

            def by_type(sems):
                def one_hot(j, b, first=False):
                    if not first:
                        dve.wait_ge(sems["product"], j - 1)
                    dve.tensor_scalar(oh_tile[b][0:TYPES, :], tile_type[0:TYPES, bass.ds(j, 1)]
                                      .to_broadcast([TYPES, P]), pidx[0:TYPES, :], None,
                                      ALU.is_equal).then_inc(sems["onehot"], 1)

                for b in range(2):
                    one_hot(b, b, True)
                pairs = tile_pairs(dve)
                with dve.Fori(1, pairs, 1) as h:
                    for b in range(2):
                        one_hot(2 * h + b, b)
                for b in range(2):
                    dve.wait_ge(sems[f"put{b}"], 16 * pairs)
                dve.wait_ge(sems["rows"], 2 * pairs + 1)
                dve.wait_ge(sems["in0"], 16 * (pairs + 1))
                dve.wait_ge(sems["in1"], 16 * (pairs + 1))

            by_type(passes[0])
            dve.wait_ge(S["s_qs"], 32)
            dve.wait_ge(S["s_xn"], TILES)
            dve.wait_ge(S["s_wt"], 32)
            ch.mark(dve.memset(acc[:, :, :, :], 0.0))
            ch.mark(dve.memset(esum[:, :, :], 0.0))
            ch.mark(dve.memset(rows[:, 3 * C:4 * C, :], 0.0))
            ch.mark(dve.memset(roundc, ROUND))
            ch.mark(dve.memset(piece, 0.0))
            for b in range(2):
                ch.mark(dve.memset(pv[b], 0.0))
            ch.mark(dve.tensor_scalar(wtb[:, 1, :], wtb[:, 1, :], TWO_PI / 4, None, ALU.add))
            ch.wait()
            ch.mark(dve.memset(rescale, 1.0))
            ch.link(dve.tensor_scalar(wtb, wtb, 1.0 / TWO_PI, None, ALU.mult))
            for k, emb_part in enumerate((embw, embb)):
                sel = (embsel[:, 0:3 * PCOL].rearrange("p (c k) -> p c k", c=PCOL) if k == 0
                       else embsel[:, 3 * PCOL:4 * PCOL].unsqueeze(2).to_broadcast([P, PCOL, 3]))
                ch.mark(dve.tensor_tensor(emb_part, sel.unsqueeze(3).to_broadcast([P, PCOL, 3, TD]),
                                          wtb[:, k, :].unsqueeze(1).unsqueeze(1).to_broadcast([P, PCOL, 3, TD]),
                                          ALU.mult))
            ch.wait()
            ch.link(dve.tensor_tensor(embw, embw, embb, ALU.add))
            for b in range(2):
                dve.memset(bank[b][:, :], 0.0).then_inc(s_pa[b], 1)
                dve.wait_ge(s_pa[b], 1)
            dve.memset(ex[0], 0.0).then_inc(S["s_ex"], 1)
            dve.wait_ge(S["s_ex"], 1)
            dve.memset(init_done[:, :], 0.0).then_inc(S["s_init"], 1)

            def angles(i):
                at = bass.ds((i % WIN) * PCOL, PCOL)
                dve.wait_ge(S["s_rnd"], i + 1)
                if not (isinstance(i, int) and i == 0):
                    dve.wait_ge(S["s_pen"], i)
                dve.tensor_scalar(penal[:, at], payw_i[:, bass.ds((i % (RING * WIN // 2)) * PCOL, PCOL), 0], 0.0, PEN,
                                  ALU.is_equal, ALU.mult).then_inc(S["s_pen"], 1)
                for k in range(2):
                    ins = dve.scalar_tensor_tensor(
                        emb[:, bass.ds((i % WIN) * PCOL + k * C, C), :, :].rearrange("p c k d -> p (c k d)"),
                        rnd[:, k, :], ROUND, bank[3 + k][:, 0:C * PW], ALU.subtract, ALU.subtract)
                ins.then_inc(S["s_ang"], 1)

            def fold(prev, b, at4):
                c3.link(scale(prev, at4))
                c3.mark(add(prev, b))

            def scale(prev, at4):
                tot = acc_all[:, bass.ds(prev, 1), 0:SUMW].rearrange("p o (h d) -> p (o h) d", h=HEADS)
                return dve.tensor_tensor(tot, tot, flat(rescale[:, bass.ds(at4, 1), :]).unsqueeze(2).to_broadcast([P, HEADS, DK + 1]),
                                         ALU.mult)

            def add(prev, b):
                tot = flat(acc_all[:, bass.ds(prev, 1), :])
                return dve.tensor_tensor(tot, tot, bank[b][:, 0:PVW], ALU.add)

            def chunk(g, b, own, prev2):
                at = bass.ds(dve.snap((g % (2 * WIN)) * C, min_val=0, max_val=2 * WCOL - C), C)
                at_rows = bass.ds(dve.snap((g % 4) * C, min_val=0, max_val=3 * C), C)
                dve.wait_ge(S["s_emb"], g // WIN + 1)
                c3.mark(dve.tensor_tensor(qe[:, :, DK - TD:DK], emb[:, at, 2, :],
                                          own[:, DK - TD:DK].unsqueeze(1).to_broadcast([P, C, TD]), ALU.add))
                c3.wait(1)
                dve.wait_ge(S["s_gap"], 2 * g + 2)
                keys = rows[:, at_rows, 0:HD].rearrange("p c (h d) -> p c h d", h=HEADS)
                c3.mark(dve.tensor_tensor(prod, keys, qe.unsqueeze(2).to_broadcast([P, C, HEADS, DK]), ALU.mult))
                c3.wait(2)
                dve.wait_ge(S["s_ex"], g + 1)
                c3.mark(dve.tensor_reduce(att[b][:, 0:C, :], prod, AX_X, ALU.add))
                c3.wait(3)
                c3.link(dve.tensor_tensor(att[b][:, 0:C, :], att[b][:, 0:C, :],
                                          penal[:, at].unsqueeze(2).to_broadcast([P, C, HEADS]), ALU.add))
                c3.link(dve.tensor_reduce(att[1 - b][:, C, :], att[b].rearrange("p c h -> p h c"), AX_X, ALU.max))
                dve.tensor_tensor(ex[b], att[b], att[1 - b][:, C, :].unsqueeze(1).to_broadcast([P, C + 1, HEADS]),
                                  ALU.subtract).then_inc(S["s_ex"], 1)
                dve.wait_ge(s_pa[b], g // 2 + 1)
                c3.mark(scale(prev2, (g + 2) % 4))
                values_before(g, 1 - b)
                if b == 0:
                    angles(g // 2 + AHEAD)
                c3.wait(6)
                c3.mark(add(prev2, b))

            def values_before(g, b):
                dve.wait_ge(S["s_pe"], g + 1)
                vals = rows[:, bass.ds(((g + 3) % 4) * C, C), HD:ROW].rearrange("p c (h d) -> p c h d", h=HEADS)
                dve.tensor_tensor(pvh[b][:, 0:C, :, 0:DK], vals, pvh[b][:, 0:C, :, DK].unsqueeze(3)
                                  .to_broadcast([P, C, HEADS, DK]), ALU.mult).then_inc(S["s_pvd"], 1)

            c3 = Chain(dve, S["s_dv3"])
            PER = 7
            for i in range(AHEAD):
                angles(i)
            dve.memset(ex[1], 0.0).then_inc(S["s_pe"], 1)
            total = chunk_total(dve)
            before, before2 = (dve.alloc_register(n) for n in ("block_before", "block_before2"))
            dve.reg_mov(before, 0)
            dve.reg_mov(before2, 0)
            with dve.Fori(0, 2, 1) as l:
                with dve.Fori(0, TILES, 1) as tile:
                    blk = l * TILES + tile
                    lo, hi = chunk_range(dve, blk)
                    own = flat(qs[:, bass.ds(tile, 1), :])
                    dve.wait_ge(S["s_ex"], lo + 1)
                    c3.at(lo * PER + blk * 3)
                    for b in range(2):
                        c3.mark(dve.memset(att[b][:, C, :], MINIT))
                    c3.mark(dve.tensor_scalar(qe[:, :, 0:DK - TD], own[:, 0:DK - TD].unsqueeze(1)
                                              .to_broadcast([P, C, DK - TD]), 0.0, None, ALU.add))
                    with dve.Fori(lo, hi, 1) as g:
                        prev2 = dve.snap(before2, min_val=0, max_val=BLOCKS - 1)
                        marks = dve.snap(g * PER + (blk + 1) * 3, min_val=3, max_val=GMAX * PER)
                        for b in range(2):
                            with (dve.Else() if b else dve.If(g % 2 == 0)):
                                c3.at(marks)
                                chunk(g, b, own, prev2)
                                assert c3.n == PER, c3.n
                        dve.reg_mov(before2, before)
                        dve.reg_mov(before, blk)
            prev2 = dve.snap(before2, min_val=0, max_val=BLOCKS - 1)
            for b in range(2):
                with (dve.Else() if b else dve.If(total % 2 == 0)):
                    c3.at(total * PER + BLOCKS * 3)
                    dve.wait_ge(s_pa[b], total // 2 + 1)
                    if b == 0:
                        angles(total // 2 + AHEAD)
                    c3.wait()
                    fold(prev2, b, (total + 2) % 4)
                    c3.wait()
                    values_before(total, 1 - b)
                    dve.wait_ge(s_pa[1 - b], (total + 1) // 2 + 1)
                    c3.wait()
                    fold(BLOCKS - 1, 1 - b, (total + 3) % 4)
            dve.memset(ex[1], 0.0).then_inc(S["s_pvd"], 4)
            dve.wait_ge(S["s_gap"], 2 * total + 4)
            dve.wait_ge(S["s_emb"], (total + 5) // WIN + 1)
            dve.wait_ge(S["s_ptp"], (total + 1) // 2 + AHEAD + 2)
            dve.wait_ge(S["s_pang"], total // 2 + AHEAD + 2)
            dve.wait_ge(S["s_rnd"], total // 2 + AHEAD + 1)
            dve.wait_ge(S["s_ang"], total // 2 + AHEAD + 1)
            dve.wait_ge(S["s_dv3"], total * PER + BLOCKS * 3 + 4)
            dve.wait_ge(S["s_pool3"], 1)
            ch.mark(dve.tensor_scalar(inv, acc[:, :, :, DK], 1e-16, None, ALU.add))
            dve.memset(init_done[:, :], 0.0).then_inc(S["s_last"], 1)
            ch.wait()
            ch.link(dve.reciprocal(inv, inv))
            mean_v = acc[:, :, :, 0:DK]
            ch.mark(dve.tensor_tensor(agg[:, :, HD:IN], esum[:, 0:TILES, :], esum[:, TILES:BLOCKS, :], ALU.add))
            ch.link(dve.tensor_tensor(mean_v, mean_v, inv.unsqueeze(3).to_broadcast([P, BLOCKS, HEADS, DK]), ALU.mult))
            dve.tensor_tensor(agg[:, :, 0:HD].rearrange("p t (h d) -> p t h d", h=HEADS), mean_v[:, 0:TILES],
                              mean_v[:, TILES:BLOCKS], ALU.add).then_inc(S["s_aggd"], 1)
            for k in range(KC):
                dve.wait_ge(s_w4[k], 32)
                dve.tensor_tensor(w_out[:, k, :, :], w_out[:, k, :, :], w_low, ALU.add).then_inc(S["s_w4m"], 1)
            dve.wait_ge(S["s_typ4"], 16)
            dve.wait_ge(S["s_w4m"], KC)
            ch.link(dve.tensor_copy(typrow4, typrow4_i))

            def one_hot4(t):
                dve.tensor_scalar(oh_type4[0:TYPES, :], typrow4[0:TYPES, bass.ds(t * P, P)], pidx[0:TYPES, :], None,
                                  ALU.is_equal).then_inc(S["s_oht4"], 1)

            by_type(passes[1])
            c4 = Chain(dve, S["s_dv4"])
            dve.wait_ge(S["s_od"], 16)
            ch.link(dve.tensor_tensor(xn[:, :, :], agg, xn[:, :, :], ALU.add))
            with dve.Fori(0, TILES, 1) as t:
                dve.bn_stats(flat(stats[:, bass.ds(t, 1), :]), flat(xn[:, bass.ds(t, 1), :])).then_inc(S["s_bn"], 1)
            dve.wait_ge(S["s_bn"], TILES)
            ln_rest(2)
            dve.wait_ge(S["s_xraw"], 16)
            k4 = 0

            def scale4(t, first=False):
                if not first:
                    dve.wait_ge(S["s_gbp"], t)
                one_hot4(t)
                c4.at(k4 + t * 4)
                tl, ti = flat(xn[:, bass.ds(t, 1), :]), bass.ds(t, 1)
                c4.link(dve.tensor_scalar(ln4[:, 0, :], tl, mean[:, ti], rstd[:, ti], ALU.subtract, ALU.mult))
                dve.wait_ge(S["s_gbp"], t + 1)
                c4.link(dve.tensor_tensor(ln4[:, 1, :], ln4[:, 0, :], bank[4][:, 0:IN], ALU.mult))
                c4.link(dve.tensor_tensor(ln4[:, 0, :], ln4[:, 1, :], bank[4][:, IN:2 * IN], ALU.add))
                c4.link(dve.tensor_tensor(tl, ln4[:, 0, :], xraw[:, ti, :].rearrange("p o n -> p (o n)"), ALU.add))
                dve.bn_stats(flat(stats[:, ti, :]), tl).then_inc(S["s_z4"], 1)

            scale4(0, True)
            with dve.Fori(1, TILES, 1) as t:
                scale4(t)
            dve.wait_ge(S["s_z4"], TILES)
            c4.at(k4 + TILES * 4)
            ln_rest(3)

            def tile_in5(t, b, first=False):
                if not first:
                    dve.wait_ge(S["s_tp5"], t - 1)
                ti = bass.ds(t, 1)
                dve.tensor_scalar(xt5[:, b, :], flat(xn[:, ti, :]), mean[:, ti], rstd[:, ti], ALU.subtract, ALU.mult)\
                    .then_inc(S["s_x5"], 1)
                dve.tensor_scalar(flat(xn2[:, ti, :]), flat(xn[:, ti, :]), mean[:, ti], rstd[:, ti],
                                  ALU.subtract, ALU.mult).then_inc(S["s_xn2"], 1)

            def logits(t, b):
                dve.wait_ge(S["s_gps"], t + 1)
                dve.tensor_scalar(flat(logit[:, bass.ds(t, 1), :]), bank[2 + b][:, 0:EXPERTS], 0.0, None, ALU.add)\
                    .then_inc(S["s_lg"], 1)

            tile_in5(0, 0, True)
            tile_in5(1, 1, True)
            with dve.Fori(0, (TILES - 3) // 2, 1) as i:
                for b in range(2):
                    logits(2 * i + b, b)
                    tile_in5(2 * i + b + 2, b)
            logits(TILES - 3, 0)
            tile_in5(TILES - 1, 0)
            logits(TILES - 2, 1)
            logits(TILES - 1, 0)
            dve.wait_ge(S["s_lg"], TILES)
            wide = [P, TILES, EXPERTS]
            rev = gstat
            ch.link(dve.tensor_scalar(rev, iota[:, 0:EXPERTS], -1.0, float(EXPERTS), ALU.mult, ALU.add))
            for k, sel in enumerate((sel1, sel2)):
                ch.link(dve.tensor_reduce(top[:, k, :], logit, AX_X, ALU.max))
                ch.link(dve.tensor_tensor(cand, logit, top[:, k, :].unsqueeze(2).to_broadcast(wide), ALU.is_equal))
                ch.link(dve.tensor_tensor(cand, cand, rev.unsqueeze(1).to_broadcast(wide), ALU.mult))
                ch.link(dve.tensor_reduce(top[:, 4, :], cand, AX_X, ALU.max))
                ch.link(dve.tensor_tensor(sel, cand, top[:, 4, :].unsqueeze(2).to_broadcast(wide), ALU.is_equal))
                if k == 0:
                    ch.link(dve.scalar_tensor_tensor(logit, sel, PEN, logit, ALU.mult, ALU.add))
            dve.tensor_tensor(top[:, 2, :], top[:, 1, :], top[:, 0, :], ALU.subtract).then_inc(S["s_e5"], 1)
            dve.wait_ge(S["s_e5d"], 1)
            ch.link(dve.tensor_scalar(top[:, 4, :], top[:, 3, :], 1.0, None, ALU.add))
            ch.link(dve.reciprocal(top[:, 4, :], top[:, 4, :]))
            ch.mark(dve.tensor_tensor(sel1, sel1, top[:, 4, :].unsqueeze(2).to_broadcast(wide), ALU.mult))
            ch.link(dve.tensor_tensor(top[:, 5, :], top[:, 3, :], top[:, 4, :], ALU.mult))
            ch.link(dve.tensor_tensor(sel2, sel2, top[:, 5, :].unsqueeze(2).to_broadcast(wide), ALU.mult))
            ch.link(dve.tensor_tensor(gate, sel1, sel2, ALU.add))

            def bias5(t, first=False):
                if not first:
                    dve.wait_ge(S["s_mo"], t)
                dve.tensor_scalar(gstat, flat(gate[:, bass.ds(t, 1), :]), 0.0, None, ALU.add).then_inc(S["s_gst"], 1)
                dve.wait_ge(S["s_b2p"], t + 1)
                dve.tensor_scalar(flat(moe[:, bass.ds(t, 1), :]), bank[3][:, 0:IN], 0.0, None, ALU.add)\
                    .then_inc(S["s_mo"], 1)

            bias5(0, True)
            with dve.Fori(1, TILES, 1) as t:
                bias5(t)
            dve.wait_ge(S["s_mo"], TILES)
            dve.memset(init_done[:, :], 0.0).then_inc(S["s_acc5"], 1)
            with dve.Fori(0, EXPERTS, 1) as e:
                for tile in range(TILES):
                    dve.wait_ge(S["s_op"], e * TILES + tile + 1)
                    dve.wait_ge(S["s_acc5"], e * TILES + tile + 1)
                    ti = tile % TPG
                    dve.scalar_tensor_tensor(moe[:, tile, :], bank[4 + ti % 4][:, (ti // 4) * IN:(ti // 4 + 1) * IN],
                                             gate[:, tile, bass.ds(e, 1)], moe[:, tile, :], ALU.mult, ALU.add)\
                        .then_inc(S["s_acc5"], 1)
            dve.wait_ge(S["s_acc5"], EXPERTS * TILES + 1)
            ch.link(dve.tensor_tensor(moe, moe, xn2, ALU.add))
            with dve.Fori(0, TILES, 1) as t:
                dve.bn_stats(flat(stats[:, bass.ds(t, 1), :]), flat(moe[:, bass.ds(t, 1), :])).then_inc(S["s_bn"], 1)
            dve.wait_ge(S["s_bn"], 2 * TILES)
            ln_rest(4)
            with dve.Fori(0, TILES, 1) as t:
                c4.at(k4 + TILES * 4 + t * 3)
                m, tl, ti = flat(moe[:, bass.ds(t, 1), :]), flat(xn[:, bass.ds(t, 1), :]), bass.ds(t, 1)
                c4.link(dve.tensor_scalar(m, m, mean[:, ti], rstd[:, ti], ALU.subtract, ALU.mult))
                c4.link(dve.tensor_tensor(m, m, fgb_sb[:, 0:IN], ALU.mult))
                c4.link(dve.tensor_tensor(m, m, fgb_sb[:, IN:2 * IN], ALU.add))
                dve.tensor_tensor(tl, tl, m, ALU.add).then_inc(S["s_o5"], 1)


def kernel(x, src, dst, edge_attr_5, node_type_19, L0_gnn_Wk, L0_gnn_bk, L0_gnn_Wq, L0_gnn_bq, L0_gnn_Wv, L0_gnn_bv,
           L0_gnn_Wa, L0_gnn_ba, L0_gnn_gamma, L0_gnn_beta, L0_gnn_w_time, L0_gnn_b_time, L0_ffn_gate_w,
           L0_ffn_gate_b, L0_ffn_w1, L0_ffn_b1, L0_ffn_w2, L0_ffn_b2, L0_ffn_gamma, L0_ffn_beta):
    import numpy as np
    import concourse.bacc as bacc
    from concourse import mybir as mb
    from concourse.bass_utils import run_bass_kernel_spmd as run

    def rows_first(a, *shape):
        return a

    f32 = np.float32
    a = np.arange(P)
    r, c, k = a[:, None, None], np.arange(PCOL)[None, :, None], np.arange(3)[None, None, :]
    emb_sel = np.concatenate([(r == c * PAY + k + 1).reshape(P, -1), (r == c * PAY + PAY - 1).reshape(P, -1)], 1)
    cst = np.concatenate([np.eye(P), np.broadcast_to(a, (P, P)), (a[None, :] < a[:, None]), a[:, None], emb_sel], 1).astype(f32)
    pad_e = P * EC - EDGES
    edge = lambda v, fill: np.concatenate([np.asarray(v), np.full((pad_e,) + v.shape[1:], fill, np.asarray(v).dtype)])
    ids = np.stack([edge(dst, 4095).reshape(P, EC), edge(src, 4095).reshape(P, EC)], 1)
    attr = edge(edge_attr_5, 0).reshape(P, EC, 5)
    pad_n = TILES * P - NODES
    xp = np.concatenate([np.asarray(x), np.zeros((pad_n, IN), f32)])
    types = np.concatenate([np.asarray(node_type_19), np.zeros(pad_n, np.int32)])[None]
    by_type = lambda w: np.asarray(w).reshape(TYPES, -1, P, w.shape[-1]).transpose(2, 1, 0, 3)
    w1 = np.asarray(L0_ffn_w1).reshape(EXPERTS, KC, P, FF).transpose(0, 2, 1, 3).reshape(EXPERTS, P, KC * FF)
    w2 = np.asarray(L0_ffn_w2).reshape(EXPERTS, FC, P, IN).transpose(0, 2, 1, 3).reshape(EXPERTS, P, FC * IN)
    b1 = np.asarray(L0_ffn_b1).reshape(EXPERTS, FC, P).transpose(0, 2, 1)
    ins = dict(
        cst=cst, ids=ids, attr=attr, x=xp, types=types, types_col=types.reshape(TILES, P).T, Wk=by_type(L0_gnn_Wk), Wv=by_type(L0_gnn_Wv),
        Wq=by_type(L0_gnn_Wq), bk=L0_gnn_bk, bv=L0_gnn_bv, bq=L0_gnn_bq, Wa=by_type(L0_gnn_Wa), ba=L0_gnn_ba,
        gb=np.concatenate([np.asarray(L0_gnn_gamma), np.asarray(L0_gnn_beta)], 1),
        wt=np.asarray(L0_gnn_w_time)[None], bt=np.asarray(L0_gnn_b_time)[None],
        gate_w=np.asarray(L0_ffn_gate_w).reshape(KC, P, EXPERTS).transpose(1, 0, 2),
        gate_b=np.asarray(L0_ffn_gate_b)[None], ew=np.concatenate([w1, w2, b1], 2), b2=L0_ffn_b2,
        fgb=np.concatenate([np.asarray(L0_ffn_gamma), np.asarray(L0_ffn_beta)])[None])
    nc = bacc.Bacc("TRN2", target_bir_lowering=False, num_devices=1)
    arrays, args = {}, {}
    for name, v in ins.items():
        v = np.ascontiguousarray(v)
        arrays[f"in_{name}_dram"] = v
        args[name] = nc.dram_tensor(f"in_{name}_dram", v.shape, mb.dt.from_np(v.dtype), kind="ExternalInput").ap()
    args["out"] = nc.dram_tensor("out_dram", (TILES * P, IN), mb.dt.float32, kind="ExternalOutput").ap()
    build(nc, **args)
    r = run(nc, [arrays], core_ids=[0])
    return r.results[0]["out_dram"][:NODES]
```

```python
from contextlib import ExitStack

import concourse.bass as bass
from concourse import mybir

P = 128
F32 = mybir.dt.float32
BF16 = mybir.dt.bfloat16
I32 = mybir.dt.int32
ALU = mybir.AluOpType
ACT = mybir.ActivationFunctionType
AX_X = mybir.AxisListType.X
RMAX = bass.bass_isa.ReduceOp.max

NODES = 3125
EDGES = 50000
TILES = -(-NODES // P)
TYPES = 19
IN = 256
KC = IN // P
PROJ = 192
TD = 32
HEADS = 4
DK = 56
HD = HEADS * DK
HEAD_SCALE = 1.0 / 56.0 ** 0.5
EPS = 1e-5
WCOLS = 2 * PROJ + DK
ROW = 2 * HD
EXPERTS = 16
FF = 512
FC = FF // P

EC = 400
HG = 20
C = 4
BLOCKS = 2 * TILES
WIN = 8
WCOL = WIN * C
GMAX = -(-(2 * EDGES // C + BLOCKS + 4 * WIN) // 16) * 16
UNITS = EC // 4
TT = 2 * ((TILES + TYPES) // 2)
TCOLS = TT + 2
PICKS = 2 * TILES
GROUP = 5
CLASSES = 64
CLASS_TILES = 512 // CLASSES - 1
MT = PICKS + EXPERTS
MCOLS = MT + 2
PAD_SLOT = 1.3e7
ROUND = 1.5 * 2.0 ** 23
TWO_PI = 6.283185307179586
PEN = -1e30
MINIT = -1e20
SUMW = HEADS * (DK + 1)
PVW = SUMW + TD
PAY = 5
PCOL = 2 * C
PW = 3 * TD
AHEAD = WIN // 2 + 2
RING = 4
EW = KC * FF + FC * IN + FC


class Chain:

    def __init__(self, eng, sem):
        self.eng, self.sem, self.base, self.n = eng, sem, 0, 0

    def mark(self, ins):
        ins.then_inc(self.sem, 1)
        self.n += 1

    def wait(self, n=None):
        self.eng.wait_ge(self.sem, self.base + (self.n if n is None else n))

    def link(self, ins):
        self.mark(ins)
        self.wait()

    def at(self, base):
        self.base, self.n = base, 0


def build(nc, cst, ids, attr, x, types, types_col, Wk, Wv, Wq, bk, bv, bq, Wa, ba, gb, wt, bt,
          gate_w, gate_b, ew, b2, fgb, out):
    with ExitStack() as ctx:
        def sb(name, shape, dt=F32):
            return ctx.enter_context(nc.sbuf_tensor(name, shape, dt))

        def sem(name):
            return ctx.enter_context(nc.semaphore(name))

        ell = nc.dram_tensor("ell", [GMAX * C * P, PAY], F32, kind="Internal").ap()
        kv = nc.dram_tensor("kv", [TILES * P + 1, ROW], F32, kind="Internal").ap()
        order = nc.dram_tensor("order", [TCOLS * P, 1], I32, kind="Internal").ap()
        rows_in, agg_rows, out_rows = (nc.dram_tensor(n, [TILES * P + 1, IN], F32, kind="Internal").ap()
                                       for n in ("rows_in", "agg_rows", "out_rows"))
        dispatch = nc.dram_tensor("dispatch", [MCOLS * P, 3], I32, kind="Internal").ap()
        picked = nc.dram_tensor("picked", [PICKS * P + 1, IN], F32, kind="Internal").ap()
        qs_rows = nc.dram_tensor("qs_rows", [BLOCKS * P, DK], F32, kind="Internal").ap()
        acc_rows = nc.dram_tensor("acc_rows", [BLOCKS * P, PVW], F32, kind="Internal").ap()
        ell_fill = ell.rearrange("(n p r) w -> n p (r w)", p=P, r=16 * C)
        ell_win = ell.rearrange("(n i p) w -> n p i w", i=WCOL, p=P)

        con = sb("con", [P, 3 * P + 1 + 4 * PCOL])
        ident, iota, tri, pidx = con[:, 0:P], con[:, P:2 * P], con[:, 2 * P:3 * P], con[:, 3 * P:3 * P + 1]
        embsel = con[:, 3 * P + 1:]
        xn = sb("xn", [P, TILES, IN])
        qs2 = sb("qs2", [P, BLOCKS, DK])
        order_i = sb("order_i", [P, BLOCKS], I32)
        start_i = sb("start_i", [P, BLOCKS + 1], I32)
        fills_i = sb("fills_i", [P, 4], I32)
        stats = sb("stats", [P, TILES, 6])
        lnv = sb("lnv", [P, 6, TILES])
        mean, rstd = lnv[:, 0, :], lnv[:, 5, :]
        acc_all = sb("acc", [P, BLOCKS, PVW])
        acc = acc_all[:, :, 0:SUMW].rearrange("p b (h d) -> p b h d", h=HEADS)
        esum = acc_all[:, :, SUMW:PVW]
        ones_sq = sb("ones_sq", [P, P])
        zero = sb("zero", [P, 16 * C * PAY])
        hold_cells = sb("hold_in", [P, 4])
        signal_cell = sb("signal_cell", [P, 1])
        ones = sb("ones", [P, TILES])
        ones_row = sb("ones_row", [1, P])
        node_of = sb("node_of", [P, TCOLS], I32)
        tile_type = sb("tile_type", [P, TT])
        tile_type_i = sb("tile_type_i", [P, TT], I32)
        pairs_i = sb("pairs_i", [P, 1], I32)
        place_i = sb("place_i", [P, TILES], I32)
        row_i = sb("row_i", [P, TILES], I32)
        type_i = sb("type_i", [P, TILES], I32)
        idx_in, idx_out = ([sb(f"{n}{b}", [P, 1], I32) for b in range(2)] for n in ("idx_in", "idx_out"))
        rows_g = [sb(f"rows_g{b}", [P, IN]) for b in range(2)]
        rows_t = [sb(f"rows_t{b}", [P, KC, P]) for b in range(2)]
        rows_o = [sb(f"rows_o{b}", [P, ROW]) for b in range(2)]
        oh_tile = [sb(f"oh_tile{b}", [P, P]) for b in range(2)]
        accflat = acc_all[:, :, :].rearrange("p a b -> p (a b)")

        ARENA = 26600
        arena = sb("arena", [P, ARENA])

        class Arena:

            def __init__(self, at=0):
                self.at = at

            def take(self, *shape, dt=F32):
                n = 1
                for s in shape:
                    n *= s
                words = n if dt != BF16 else (n + 1) // 2
                v = arena[:, self.at:self.at + words]
                self.at += words
                assert self.at <= ARENA, self.at
                if dt != F32:
                    v = v.bitcast(dt)
                if len(shape) == 2:
                    v = v.rearrange("p (a b) -> p a b", a=shape[0])
                elif len(shape) == 3:
                    v = v.rearrange("p (a b c) -> p a b c", a=shape[0], b=shape[1])
                elif len(shape) == 4:
                    v = v.rearrange("p (a b c d) -> p a b c d", a=shape[0], b=shape[1], c=shape[2])
                return v

        bank = [ctx.enter_context(nc.psum_tensor(f"bank{i}", [P, 512], F32)) for i in range(8)]

        s1 = Arena()
        ids_i = s1.take(2, EC, dt=I32)
        tmp_i = s1.take(2, EC, dt=I32)
        idf = s1.take(2, EC)
        hif = s1.take(2, EC)
        lohb = s1.take(2, EC, 2, dt=BF16)
        lof = s1.take(2, EC)
        pay = s1.take(2, EC, PAY)
        pay_i = pay.bitcast(I32)
        ohl = s1.take(2, HG, P, dt=BF16)
        ohh = s1.take(2, HG, TILES + 1, dt=BF16)
        identb = s1.take(P, dt=BF16)
        lohs = s1.take(2, 4, 2, dt=BF16)
        oht = s1.take(2, 4, P)
        junk = s1.take(4, P)
        ohhf = s1.take(4, TILES)
        selp = s1.take(4, TILES)
        selv = s1.take(4)
        rank = s1.take(4)
        padp = s1.take(2, 4)
        slotf = s1.take(4)
        slot = s1.take(2, 4, dt=I32)
        stage = s1.take(2, 4, PAY)
        stage_i = stage.bitcast(I32)
        base = s1.take(TILES)
        deg = s1.take(TILES)
        maxdeg = s1.take(TILES)
        deg_sorted = s1.take(TILES)
        chunks_i = s1.take(TILES, dt=I32)
        chunks = s1.take(TILES)
        startf = s1.take(BLOCKS + 1)
        fillf = s1.take(4)
        at_hist = s1.at
        hist = s1.take(EC, TILES)
        attr_sb = arena[:, at_hist:at_hist + EC * 5].rearrange("p (e w) -> p e w", w=5)
        h_at = [at_hist]

        def over_counts(a, b):
            v = arena[:, h_at[0]:h_at[0] + a * b].rearrange("p (a b) -> p a b", a=a)
            h_at[0] += a * b
            return v

        oh_class = over_counts(TILES, CLASSES)
        ccount = over_counts(CLASSES, TILES)
        cscan = over_counts(CLASSES, TILES)
        cbefore = over_counts(TILES, CLASSES)
        oh_tile_of = over_counts(TILES, TILES)
        tile_work = over_counts(TILES, TILES)
        node_class, place_r, tile_r, start_diff = (over_counts(1, TILES)[:, 0, :] for _ in range(4))
        tile_ri = over_counts(1, TILES)[:, 0, :].bitcast(I32)
        assert h_at[0] <= at_hist + EC * TILES
        qs = accflat[:, 0:TILES * DK].rearrange("p (t d) -> p t d", d=DK)
        excl = accflat[:, 0:EC * TILES].rearrange("p (e b) -> p e b", b=TILES)

        s2 = Arena()
        w_kvq = s2.take(KC, TYPES, WCOLS)
        at_q = s2.at
        q_rest = s2.take(KC, TYPES, PROJ - DK)
        b_kvq = s2.take(WCOLS)
        bq_rest = s2.take(PROJ - DK)

        so_at = [EC * TILES]

        def so(*shape):
            n = shape[0] * (shape[1] if len(shape) > 1 else 1)
            v = accflat[:, so_at[0]:so_at[0] + n]
            so_at[0] += n
            return v if len(shape) == 1 else v.rearrange("p (a b) -> p a b", a=shape[0])

        type_f = so(TILES)
        oh_node = so(TILES, TYPES)
        tcount = so(TYPES, TILES + 1)
        tscan = so(TYPES, TILES + 1)
        tbefore = so(TILES, TYPES)
        tnum = so(4, TYPES)
        tnum_i = so(TYPES).bitcast(I32)
        tgrid = so(TT)
        tend = so(TT, TYPES)
        place = so(TILES)

        s3 = Arena()
        payw = s3.take(RING * WCOL, PAY)
        payw_i = payw.bitcast(I32)
        emb = s3.take(2 * WCOL, 3, TD)
        piece = s3.take(P)
        piecet = s3.take(P)
        rnd = s3.take(2, C * PW)
        embw = s3.take(PCOL, 3, TD)
        embb = s3.take(PCOL, 3, TD)
        penal = s3.take(2 * WCOL)
        roundc = s3.take(1)
        idx = [s3.take(C, dt=I32) for _ in range(4)]
        rows = s3.take(4 * C, ROW)
        qe = s3.take(C, DK)
        prod = s3.take(C, HEADS, DK)
        att = [s3.take(C + 1, HEADS) for _ in range(2)]
        ex = [s3.take(C + 1, HEADS) for _ in range(2)]
        pv = [s3.take(C, PVW) for _ in range(2)]
        pvh = [v[:, :, 0:SUMW].rearrange("p c (h d) -> p c h d", h=HEADS) for v in pv]
        wtb = s3.take(2, TD)
        rescale = s3.take(4, HEADS)

        s4 = Arena()
        w_out = s4.take(KC, TYPES, IN)
        w_low = s4.take(TYPES, IN)
        b_out = s4.take(IN)
        gb_sb = s4.take(2 * IN)
        agg = s4.take(TILES, IN)
        inv = s4.take(BLOCKS, HEADS)
        oh_type4 = s4.take(2, P)
        typrow4 = s4.take(TILES * P)
        typrow4_i = typrow4.bitcast(I32)
        xraw = arena[:, 0:TILES * IN].rearrange("p (t n) -> p t n", t=TILES)
        ln4 = s4.take(2, IN)

        xn2 = accflat[:, 0:TILES * IN].rearrange("p (t n) -> p t n", t=TILES)
        s5 = Arena()
        wexp = s5.take(2, EW)
        ht = s5.take(2, FC, P)
        moe = s5.take(TILES, IN)
        moe2 = s5.take(TILES, IN)
        logit = s5.take(TILES, EXPERTS)
        cand = s5.take(TILES, EXPERTS)
        gate = s5.take(TILES, EXPERTS)
        top = s5.take(6, TILES)
        xt5 = s5.take(2, IN)
        tt5 = s5.take(2, KC, P)
        gw_sb = s5.take(KC, EXPERTS)
        gb16 = s5.take(EXPERTS)
        b2_row = s5.take(EXPERTS * IN)
        gstat = s5.take(EXPERTS)
        fgb_sb = s5.take(2 * IN)
        items = s5.take(PICKS, 3)
        items_i = items.bitcast(I32)
        item_of = s5.take(MCOLS, 3)
        item_of_i = item_of.bitcast(I32)
        place5 = s5.take(PICKS)
        hi5 = s5.take(PICKS)
        place5_i = s5.take(PICKS, dt=I32)
        num5 = s5.take(4, EXPERTS)
        num5_i = s5.take(EXPERTS, dt=I32)
        first_i = s5.take(EXPERTS + 1, dt=I32)
        firstf = s5.take(EXPERTS + 1)
        pairs5_i = s5.take(1, dt=I32)
        so_at[0] = TILES * IN
        sel = so(PICKS, EXPERTS)
        sel1, sel2 = sel[:, 0:TILES, :], sel[:, TILES:PICKS, :]
        ecount = so(EXPERTS, PICKS + 1)
        escan = so(EXPERTS, PICKS + 1)
        ebefore = so(PICKS, EXPERTS)

        names = """s_cls s_clsp s_qput s_qs2 s_accw s_accg s_aggs s_relu5 s_outs5 s_ready5 s_xw s_po s_cnt5 s_cntp5 s_order5 s_scat5 s_types s_cnt s_cntp s_order
            s_full s_scat s_nodes s_rin s_fold s_qs s_aggd s_aggw s_od s_con s_ids s_attr s_x s_wt s_w s_out
            s_dve s_ln s_sq s_zero s_oh s_hps s_hcp s_deg s_mdeg s_start s_rows s_copy s_oht s_pg s_slot s_hold
            s_fill s_kvz s_log s_payw s_idx s_gap s_ang s_emb s_ex s_pe s_pvd s_dv3 s_pa0 s_pa1 s_g0 s_g1 s_g2
            s_g3 s_pvc s_ptp s_ptc s_pang s_rnd s_pen s_e0 s_pool3 s_sc0 s_sc1 s_agg s_init s_dvf s_dvs s_xn
            s_last s_w40 s_w41 s_w4m s_gb s_typ4 s_oht4 s_bn s_xraw s_gbp s_z4 s_x5 s_tp5 s_t5 s_w5 s_gps s_lg
            s_xn2 s_e5 s_e5d s_we0 s_we1 s_o5 s_dv4""".split()
        S = {n: sem(n) for n in names}
        passes = [{n: sem(f"s_{n}_{name}") for n in ("idx_in", "idx_out", "in0", "in1", "turned", "rows", "onehot",
                                                     "product", "out", "put0", "put1")} for name in ("kvq", "out", "moe")]
        s_pa, s_sc = ([S[f"{n}{i}"] for i in range(2)] for n in ("s_pa", "s_sc"))
        s_g = [S[f"s_g{i}"] for i in range(4)]
        s_we, s_w4 = [S["s_we0"], S["s_we1"]], [S["s_w40"], S["s_w41"]]

        block = ctx.enter_context(nc.Block())
        GROUPS = EC // HG

        def chunk_range(eng, b):
            lo = eng.value_load(start_i[0:1, bass.ds(b, 1)], min_val=0, max_val=GMAX - 64)
            hi = eng.value_load(start_i[0:1, bass.ds(b + 1, 1)], min_val=1, max_val=GMAX - 48)
            return lo, hi

        def chunk_total(eng):
            return eng.value_load(start_i[0:1, BLOCKS:BLOCKS + 1], min_val=BLOCKS, max_val=GMAX - 48)

        def starts(i):
            return isinstance(i, int) and i == 0

        def tile_pairs(eng):
            return eng.value_load(pairs_i[0:1, 0:1], min_val=TILES // 2, max_val=TT // 2)

        def by_expert(eng, tile):
            with eng.Fori(0, EXPERTS // 2, 1) as e:
                for eb in range(2):
                    lo = eng.value_load(first_i[0:1, bass.ds(2 * e + eb, 1)], min_val=0, max_val=MT - 1)
                    hi = eng.value_load(first_i[0:1, bass.ds(2 * e + eb + 1, 1)], min_val=1, max_val=MT)
                    with eng.Fori(lo, hi, 1) as j:
                        with eng.If(j % 2 == 0):
                            tile(j, 0, e, eb)
                        with eng.Else():
                            tile(j, 1, e, eb)

        def expert_pairs(eng):
            return eng.value_load(pairs5_i[0:1, 0:1], min_val=TILES, max_val=MT // 2)

        def flat(ap):
            return ap.rearrange("p o n -> p (o n)")

        @block.sync
        def _(sp):
            sp.dma_start(con[:, :], cst).then_inc(S["s_con"], 16)
            sp.dma_start(ids_i, ids).then_inc(S["s_ids"], 16)
            sp.dma_start(attr_sb, attr).then_inc(S["s_attr"], 16)
            sp.dma_start(xn[:, :, :], x.rearrange("(t p) n -> p t n", p=P)).then_inc(S["s_x"], 16)
            sp.dma_start(type_i[:, :], types_col).then_inc(S["s_types"], 16)
            sp.wait_ge(S["s_nodes"], 1)
            sp.dma_start(order.rearrange("(p j) o -> p (j o)", p=P), node_of[:, :]).then_inc(S["s_full"], 16)
            sp.wait_ge(S["s_zero"], 1)
            for k in range(2):
                sp.dma_start(kv[0:1, HD * k:HD * k + HD], zero[0:1, 0:HD]).then_inc(S["s_kvz"], 16)
            for table in (rows_in, agg_rows, out_rows):
                sp.dma_start(table[0:1, :], zero[0:1, 0:IN]).then_inc(S["s_kvz"], 16)
            for l in range(2):
                sp.wait_ge(S["s_start"], l + 1)
                lo = sp.value_load(fills_i[0:1, 2 * l:2 * l + 1], min_val=0, max_val=GMAX // 16 - 1)
                hi = sp.value_load(fills_i[0:1, 2 * l + 1:2 * l + 2], min_val=1, max_val=GMAX // 16)
                with sp.Fori(lo, hi, 1) as i:
                    sp.dma_start(ell_fill[bass.ds(i, 1), :, :].rearrange("o p w -> (o p) w"),
                                 zero[:, :]).then_inc(S["s_fill"], 16)
            sp.wait_ge(S["s_slot"], 2 * UNITS)
            sp.wait_ge(s_sc[0], 64 * UNITS)
            sp.wait_ge(s_sc[1], 64 * UNITS)
            for k in range(KC):
                sp.dma_start(w_kvq[:, k, :, 0:PROJ], Wk[:, k, :, :]).then_inc(S["s_w"], 16)
                sp.dma_start(w_kvq[:, k, :, PROJ:2 * PROJ], Wv[:, k, :, :]).then_inc(S["s_w"], 16)
                sp.dma_start(w_kvq[:, k, :, 2 * PROJ:WCOLS], Wq[:, k, :, 0:DK]).then_inc(S["s_w"], 16)
                sp.dma_start(q_rest[:, k, :, :], Wq[:, k, :, DK:PROJ]).then_inc(S["s_w"], 16)
            sp.dma_start(b_kvq[0:TYPES, 0:PROJ], bk).then_inc(S["s_w"], 16)
            sp.dma_start(b_kvq[0:TYPES, PROJ:2 * PROJ], bv).then_inc(S["s_w"], 16)
            sp.dma_start(b_kvq[0:TYPES, 2 * PROJ:WCOLS], bq[:, 0:DK]).then_inc(S["s_w"], 16)
            sp.dma_start(bq_rest[0:TYPES, :], bq[:, DK:PROJ]).then_inc(S["s_w"], 16)
            sp.wait_ge(S["s_scat"], 16 * TILES)
            sp.dma_start(node_of[:, :], order.rearrange("(p j) o -> p (j o)", p=P)).then_inc(S["s_full"], 16)
            sp.wait_ge(S["s_xn"], TILES)
            sp.dma_start(rows_in[1:, :].rearrange("(t p) n -> p t n", p=P), xn[:, :, :]).then_inc(S["s_rin"], 16)
            pairs = tile_pairs(sp)
            kvq, outp = passes[0:2]
            for b in range(2):
                sp.wait_ge(kvq[f"put{b}"], 16 * pairs)
            for at, lo, n in ((PROJ, 0, TD), (HD + PROJ, TD, DK - TD)):
                sp.dma_start(qs[:, :, lo:lo + n], kv[1:, at:at + n].rearrange("(t p) n -> p t n", p=P))\
                    .then_inc(S["s_qs"], 16)
            sp.wait_ge(S["s_qput"], 16 * BLOCKS)
            sp.dma_start(qs2[:, :, :], qs_rows.rearrange("(b p) d -> p b d", p=P)).then_inc(S["s_qs2"], 16)
            total = chunk_total(sp)
            sp.wait_ge(kvq["product"], 2 * pairs)
            sp.dma_start(wtb[:, 0, :], wt.to_broadcast([P, TD])).then_inc(S["s_wt"], 16)
            sp.dma_start(wtb[:, 1, :], bt.to_broadcast([P, TD])).then_inc(S["s_wt"], 16)

            def window(w, at):
                sp.dma_start(payw[:, at, :], ell_win[w, :, :, :].rearrange("o p i w -> (o p) i w"))\
                    .then_inc(S["s_payw"], 16)

            for w in range(RING - 1):
                if w:
                    sp.wait_ge(S["s_payw"], 16 * w)
                window(slice(w, w + 1), slice(w * WCOL, (w + 1) * WCOL))
            pieces_done, indices_done, loaded = (sp.alloc_register(n) for n in ("pieces", "indices", "loaded"))
            with sp.Fori(RING - 1, (total - 1) // WIN + 3, 1) as w:
                at, w_at = sp.snap((w % RING) * WCOL), sp.snap(w)
                sp.reg_mov(pieces_done, (WIN // 2) * (w - RING + 2))
                sp.reg_mov(indices_done, WIN * (w - RING + 2))
                sp.reg_mov(loaded, 16 * w)
                sp.wait_ge(S["s_pvc"], pieces_done)
                sp.wait_ge(S["s_pen"], pieces_done)
                sp.wait_ge(S["s_idx"], indices_done)
                sp.wait_ge(S["s_payw"], loaded)
                window(bass.ds(w_at, 1), bass.ds(at, WCOL))
            sp.wait_ge(S["s_last"], 1)
            sp.wait_ge(S["s_pool3"], 1)
            sp.wait_ge(S["s_payw"], 16 * ((total + WIN - 1) // WIN + 2))
            sp.wait_ge(S["s_aggd"], 1)
            sp.dma_start(acc_rows.rearrange("(b p) d -> p b d", p=P), acc_all[:, :, :]).then_inc(S["s_accw"], 16)
            for k in range(KC):
                sp.dma_start(w_out[:, k, :, :], Wa[:, k, :, :]).then_inc(s_w4[k], 16)
                if k:
                    sp.wait_ge(S["s_w4m"], 1)
                sp.dma_start(w_low, Wa[:, KC + k, :, :]).then_inc(s_w4[k], 16)
            sp.dma_start(b_out[0:TYPES, :], ba).then_inc(S["s_gb"], 16)
            sp.dma_start(gb_sb[0:TYPES, :], gb).then_inc(S["s_gb"], 16)
            sp.dma_start(typrow4_i, types.to_broadcast([P, TILES * P])).then_inc(S["s_typ4"], 16)
            sp.wait_ge(S["s_aggs"], 1)
            sp.dma_start(agg_rows[1:, :].rearrange("(t p) n -> p t n", p=P), agg).then_inc(S["s_aggw"], 16)
            for b in range(2):
                sp.wait_ge(outp[f"put{b}"], 16 * pairs)
            sp.dma_start(agg, out_rows[1:, :].rearrange("(t p) n -> p t n", p=P)).then_inc(S["s_od"], 16)
            sp.wait_ge(outp["product"], 2 * pairs)
            sp.dma_start(xraw, x.rearrange("(t p) n -> p t n", p=P)).then_inc(S["s_xraw"], 16)
            sp.wait_ge(S["s_z4"], TILES)
            sp.dma_start(gw_sb, gate_w).then_inc(S["s_w5"], 16)
            sp.dma_start(gb16[0:1, :], gate_b).then_inc(S["s_w5"], 16)
            sp.dma_start(b2_row[0:1, :], b2).then_inc(S["s_w5"], 16)
            sp.dma_start(fgb_sb, fgb.to_broadcast([P, 2 * IN])).then_inc(S["s_w5"], 16)
            for b in range(2):
                sp.dma_start(wexp[:, b, :], ew[b, :, :]).then_inc(s_we[b], 16)
            sp.wait_ge(S["s_nodes"], 2)
            sp.dma_start(dispatch.rearrange("(p j) w -> p (j w)", p=P), item_of_i.rearrange("p j w -> p (j w)"))\
                .then_inc(S["s_full"], 16)
            sp.wait_ge(S["s_xn2"], TILES)
            sp.dma_start(rows_in[1:, :].rearrange("(t p) n -> p t n", p=P), xn2).then_inc(S["s_xw"], 16)
            sp.wait_ge(S["s_scat5"], 16 * PICKS)
            sp.dma_start(item_of_i.rearrange("p j w -> p (j w)"), dispatch.rearrange("(p j) w -> p (j w)", p=P))\
                .then_inc(S["s_full"], 16)
            pairs5 = expert_pairs(sp)
            with sp.Fori(1, EXPERTS // 2, 1) as e:
                for b in range(2):
                    done = sp.value_load(first_i[0:1, bass.ds(2 * e + b - 1, 1)], min_val=1, max_val=MT)
                    sp.wait_ge(S["s_outs5"], done)
                    sp.dma_start(wexp[:, b, :], ew[bass.ds(2 * e + b, 1), :, :].rearrange("o p w -> (o p) w"))\
                        .then_inc(s_we[b], 16)
            for b in range(2):
                sp.wait_ge(passes[2][f"put{b}"], 16 * pairs5)
            for k, half in enumerate((moe, moe2)):
                sp.dma_start(half, picked[1 + k * TILES * P:1 + (k + 1) * TILES * P, :]
                             .rearrange("(t p) n -> p t n", p=P)).then_inc(S["s_po"], 16)
            out_t = out.rearrange("(t p) n -> t p n", p=P)
            with sp.Fori(0, TILES // GROUP, 1) as i:
                sp.wait_ge(S["s_o5"], i + 1)
                sp.dma_start(out_t[bass.ds(i * GROUP, GROUP), :, :].rearrange("t p n -> p t n"),
                             xn[:, bass.ds(i * GROUP, GROUP), :]).then_inc(S["s_out"], 16)
            sp.wait_ge(S["s_out"], 16 * (TILES // GROUP))
        @block.gpsimd
        def _(pool):
            pool.memset(hold_cells[:, :], 0.0).then_inc(S["s_hold"], 1)

            def hold(n):
                pool.wait_ge(S["s_hold"], n)
                pool.tensor_tensor(hold_cells[:, 0:1], hold_cells[:, 1:2], hold_cells[:, 2:3], ALU.add).then_inc(S["s_hold"], 1)

            pool.wait_ge(S["s_order"], 1)
            pool.wait_ge(S["s_full"], 16)
            hold(1)
            for t in range(TILES):
                pool.indirect_dma_start(
                    out=order, out_offset=bass.IndirectOffsetOnAxis(ap=place_i[:, t:t + 1], axis=0),
                    in_=row_i[:, t:t + 1], in_offset=None, bounds_check=TCOLS * P - 1,
                    oob_is_err=False).then_inc(S["s_scat"], 16)
            pairs = tile_pairs(pool)

            for l in range(2):
                pool.wait_ge(S["s_deg"], l + 1)
                pool.partition_all_reduce(maxdeg, deg_sorted, P, RMAX).then_inc(S["s_mdeg"], 1)
                pool.wait_ge(S["s_start"], l + 1)
                hi = pool.value_load(fills_i[0:1, 2 * l + 1:2 * l + 2], min_val=1, max_val=GMAX // 16)
                pool.wait_ge(S["s_fill"], 16 * hi)
                hold(2 + l * (UNITS + 1))
                with pool.Fori(0, UNITS // 2, 1) as i:
                    for b in range(2):
                        pool.wait_ge(S["s_slot"], 2 * i + b + 1 + l * UNITS)
                        hold(2 * i + b + 3 + l * (UNITS + 1))
                        for c in range(4):
                            pool.indirect_dma_start(
                                out=ell, out_offset=bass.IndirectOffsetOnAxis(ap=slot[:, b, c:c + 1], axis=0),
                                in_=stage[:, b, c, :], in_offset=None, bounds_check=GMAX * C * P - 1,
                                oob_is_err=False).then_inc(s_sc[b], 16)
            def by_type(sems, table_in, table_out, width, held, pairs, source_in, source_out, last_out, given=0):
                def fetch(j, b, first=False):
                    if not first:
                        pool.wait_ge(sems[f"in{b}"], 16 * (j // 2))
                        pool.wait_ge(sems["turned"], j - 1)
                    pool.tensor_copy(idx_in[b][:, :], source_in(j)).then_inc(sems["idx_in"], 1)
                    pool.wait_ge(sems["idx_in"], j + 1)
                    hold(held(j))
                    pool.indirect_dma_start(
                        out=rows_g[b][:, :], out_offset=None, in_=table_in,
                        in_offset=bass.IndirectOffsetOnAxis(ap=idx_in[b][:, 0:1], axis=0),
                        bounds_check=TILES * P, oob_is_err=False).then_inc(sems[f"in{b}"], 16)

                def put(j, b, first=False):
                    if not first:
                        pool.wait_ge(sems[f"put{b}"], 16 * (j // 2))
                    pool.tensor_copy(idx_out[b][:, :], source_out(j)).then_inc(sems["idx_out"], 1)
                    pool.wait_ge(sems["idx_out"], j + 1)
                    pool.wait_ge(sems["out"], j + 1 + given)
                    hold(held(j + 2) + 1)
                    pool.indirect_dma_start(
                        out=table_out, out_offset=bass.IndirectOffsetOnAxis(ap=idx_out[b][:, 0:1], axis=0),
                        in_=rows_o[b][:, 0:width], in_offset=None, bounds_check=last_out,
                        oob_is_err=False).then_inc(sems[f"put{b}"], 16)

                for b in range(2):
                    fetch(b, b, True)
                for b in range(2):
                    fetch(b + 2, b)
                    put(b, b, True)
                with pool.Fori(1, pairs, 1) as h:
                    for b in range(2):
                        fetch(2 * h + b + 2, b)
                        put(2 * h + b, b)
                for b in range(2):
                    pool.wait_ge(sems[f"in{b}"], 16 * (pairs + 1))
                    pool.wait_ge(sems[f"put{b}"], 16 * pairs)
                hold(held(2 * pairs + 2))

            def held_from(base):
                return lambda j: base + j if isinstance(j, int) and j < 2 else base + 2 * j - 2

            pool.wait_ge(S["s_full"], 32)
            pool.wait_ge(S["s_rin"], 16)
            pool.wait_ge(S["s_kvz"], 16 * 5)
            HELD2 = 2 + 2 * (UNITS + 1)
            total = chunk_total(pool)
            node = lambda j: node_of[:, bass.ds(j, 1)]
            by_type(passes[0], rows_in, kv, ROW, held_from(HELD2), pairs, node, node, TILES * P)
            pool.wait_ge(S["s_qs"], 32)
            hold(HELD2 + 4 * pairs + 3)
            for b in range(BLOCKS):
                pool.indirect_dma_start(
                    out=qs_rows, out_offset=bass.IndirectOffsetOnAxis(ap=order_i[:, b:b + 1], axis=0),
                    in_=qs[:, b % TILES, :], in_offset=None).then_inc(S["s_qput"], 16)
            HELD = HELD2 + 4 * pairs + 4

            def gather(g, j):
                pool.wait_ge(S["s_payw"], 16 * (g // WIN + 1))
                pool.tensor_copy(idx[j], payw_i[:, bass.ds((g % (RING * WIN)) * C, C), 0:1]
                                 .rearrange("p c o -> p (c o)")).then_inc(S["s_idx"], 1)
                pool.wait_ge(S["s_idx"], g + 1)
                hold(g + HELD)
                for c in range(C):
                    pool.indirect_dma_start(
                        out=rows[:, j * C + c, :], out_offset=None, in_=kv,
                        in_offset=bass.IndirectOffsetOnAxis(ap=idx[j][:, c:c + 1], axis=0)).then_inc(s_g[j], 16)

            for j in range(4):
                if j == 3:
                    pool.wait_ge(S["s_pvd"], 1)
                gather(j, j)
            rounds = (total + 5) // 4
            with pool.Fori(1, rounds, 1) as h:
                for j in range(4):
                    pool.wait_ge(S["s_pvd"], 4 * h + j - 2)
                    pool.wait_ge(s_g[j], 16 * C * h)
                    gather(4 * h + j, j)
            for j in range(4):
                pool.wait_ge(s_g[j], 16 * C * rounds)
            hold(HELD + 4 * rounds)
            pool.memset(hold_cells[:, 3:4], 0.0).then_inc(S["s_pool3"], 1)
            pool.wait_ge(S["s_accw"], 16)
            hold(HELD + 4 * rounds + 1)
            for b in range(BLOCKS):
                pool.indirect_dma_start(
                    out=acc_all[:, b, :], out_offset=None, in_=acc_rows,
                    in_offset=bass.IndirectOffsetOnAxis(ap=order_i[:, b:b + 1], axis=0)).then_inc(S["s_accg"], 16)
            pool.wait_ge(S["s_aggw"], 16)
            HELD4 = HELD + 4 * rounds + 2
            by_type(passes[1], agg_rows, out_rows, IN, held_from(HELD4), pairs, node, node, TILES * P)
            pool.wait_ge(S["s_order5"], 1)
            pool.wait_ge(S["s_full"], 48)
            hold(HELD4 + 4 * pairs + 3)
            for t in range(PICKS):
                pool.indirect_dma_start(
                    out=dispatch, out_offset=bass.IndirectOffsetOnAxis(ap=place5_i[:, t:t + 1], axis=0),
                    in_=items_i[:, t, :], in_offset=None, bounds_check=MCOLS * P - 1,
                    oob_is_err=False).then_inc(S["s_scat5"], 16)
            pool.wait_ge(S["s_full"], 64)
            pool.wait_ge(S["s_xw"], 16)
            word = lambda k: lambda j: item_of_i[:, bass.ds(j, 1), k]
            by_type(passes[2], rows_in, picked, IN, held_from(HELD4 + 4 * pairs + 4), expert_pairs(pool),
                    word(0), word(1), PICKS * P, given=2)

        @block.scalar
        def _(act):
            act.wait_ge(S["s_attr"], 16)
            for l in range(2):
                for k, src in enumerate((0, 1 + l, 2 - l)):
                    act.activation(pay[:, l, :, 1 + k:2 + k], attr_sb[:, :, src:src + 1], ACT.Ln, bias=1.0)\
                        .then_inc(S["s_log"], 1)
            act.wait_ge(S["s_log"], 6)
            for l in range(2):
                with act.Fori(0, GROUPS // 2, 1) as i:
                    for b in range(2):
                        act.wait_ge(S["s_hps"], 2 * i + b + 1 + l * GROUPS)
                        act.copy(hist[:, bass.ds((2 * i + b) * HG, HG), :],
                                 bank[b][:, 0:HG * TILES].rearrange("p (e b) -> p e b", b=TILES))\
                            .then_inc(S["s_hcp"], 1)
            act.wait_ge(S["s_ln"], 1)
            act.activation(lnv[:, 4, :], lnv[:, 3, :], ACT.Sqrt).then_inc(S["s_sq"], 1)

            def by_type(sems, pieces):
                def turned(j, b, first=False):
                    act.wait_ge(sems["turned"], j + 1)
                    if not first:
                        act.wait_ge(sems["product"], j - 1)
                    act.copy(rows_t[b][:, :, :], bank[2][:, 0:IN].rearrange("p (k n) -> p k n", k=KC))\
                        .then_inc(sems["rows"], 1)

                def give(j, b, first=False):
                    act.wait_ge(sems["product"], j + 1)
                    if not first:
                        act.wait_ge(sems[f"put{b}"], 16 * (j // 2))
                    for to, at, n in pieces:
                        last = act.copy(rows_o[b][:, to:to + n], bank[3 + b][:, at:at + n])
                    last.then_inc(sems["out"], 1)

                turned(0, 0, True)
                turned(1, 1, True)
                give(0, 0, True)
                turned(2, 0)
                give(1, 1, True)
                with act.Fori(1, tile_pairs(act), 1) as h:
                    for b in range(2):
                        turned(2 * h + b + 1, 1 - b)
                        give(2 * h + b, b)

            act.wait_ge(S["s_fold"], 1)
            by_type(passes[0], ((0, 0, PROJ), (HD, PROJ, PROJ), (PROJ, 2 * PROJ, TD),
                                (HD + PROJ, 2 * PROJ + TD, DK - TD)))

            def piece_in(i):
                act.wait_ge(S["s_payw"], 16 * (i // (WIN // 2) + 1))
                if not starts(i):
                    act.wait_ge(S["s_ptp"], i)
                act.copy(piece[:, 0:PCOL * PAY], payw[:, bass.ds((i % (RING * WIN // 2)) * PCOL, PCOL), :]
                         .rearrange("p c w -> p (c w)")).then_inc(S["s_pvc"], 1)

            def piece_turned(i):
                act.wait_ge(S["s_ptp"], i + 1)
                if not starts(i):
                    act.wait_ge(S["s_pang"], i)
                act.copy(piecet[0:PCOL * PAY, :], bank[2][0:PCOL * PAY, 0:P]).then_inc(S["s_ptc"], 1)

            def rounded(i):
                act.wait_ge(S["s_pang"], i + 1)
                if not starts(i):
                    act.wait_ge(S["s_ang"], i)
                act.activation(rnd[:, 0, :], bank[3][:, 0:C * PW], ACT.Identity, bias=roundc)
                act.activation(rnd[:, 1, :], bank[4][:, 0:C * PW], ACT.Identity, bias=roundc).then_inc(S["s_rnd"], 1)

            def cosines(w):
                act.wait_ge(S["s_ang"], (WIN // 2) * (w + 1))
                at = bass.ds((w % 2) * WCOL, WCOL)
                act.activation(emb[:, at, :, :], emb[:, at, :, :], ACT.Sin, scale=-TWO_PI).then_inc(S["s_emb"], 1)

            def embed_rows(g, j):
                act.wait_ge(s_g[j], 16 * C * (g // 4 + 1))
                act.wait_ge(S["s_emb"], g // WIN + 1)
                src = emb[:, bass.ds((g % (2 * WIN)) * C, C), 1, :]
                for k in range(2):
                    act.copy(rows[:, j * C:(j + 1) * C, HD * k + PROJ:HD * k + HD], src).then_inc(S["s_gap"], 1)

            def exponentials(g, b):
                act.wait_ge(S["s_ex"], g + 2)
                act.wait_ge(s_pa[b], g // 2 + 1)
                act.activation(pvh[b][:, 0:C, :, DK], ex[b][:, 0:C, :], ACT.Exp, scale=HEAD_SCALE)
                act.activation(rescale[:, bass.ds(g % 4, 1), :], ex[b][:, C:C + 1, :], ACT.Exp,
                               scale=HEAD_SCALE).then_inc(S["s_pe"], 1)
                act.copy(pv[b][:, 0:C, SUMW:PVW], emb[:, bass.ds((g % (2 * WIN)) * C, C), 0, :]).then_inc(S["s_e0"], 1)

            def attend(g, j):
                if j % 2:
                    rounded(g // 2 + AHEAD + 1)
                exponentials(g, j % 2)
                embed_rows(g + 2, (j + 2) % 4)
                if j % 2 == 0:
                    piece_in(g // 2 + AHEAD + 2)
                else:
                    piece_turned(g // 2 + AHEAD + 2)

            act.wait_ge(S["s_init"], 1)
            for i in range(AHEAD + 2):
                piece_in(i)
                piece_turned(i)
                if i < AHEAD + 1:
                    rounded(i)
            cosines(0)
            embed_rows(0, 0)
            embed_rows(1, 1)
            total = chunk_total(act)
            with act.Fori(0, total, 1) as g:
                with act.If(g % 2 == 0):
                    with act.If(g % 4 == 0):
                        attend(g, 0)
                    with act.Else():
                        attend(g, 2)
                    with act.If(g % WIN == 2):
                        cosines((g + 2 * AHEAD) // WIN)
                with act.Else():
                    with act.If(g % 4 == 1):
                        attend(g, 1)
                    with act.Else():
                        attend(g, 3)
            by_type(passes[1], ((0, 0, IN),))
            for n in range(2):
                act.wait_ge(S["s_ln"], n + 2)
                act.activation(lnv[:, 4, :], lnv[:, 3, :], ACT.Sqrt).then_inc(S["s_sq"], 1)

            def turned5(t, b):
                act.wait_ge(S["s_tp5"], t + 1)
                act.copy(tt5[:, b, :, :], bank[b][:, 0:IN].rearrange("p (k n) -> p k n", k=KC)).then_inc(S["s_t5"], 1)

            turned5(0, 0)
            with act.Fori(0, TILES // 2, 1) as i:
                for b in range(2):
                    turned5(2 * i + b + 1, 1 - b)
            act.wait_ge(S["s_e5"], 1)
            act.activation(top[:, 3, :], top[:, 2, :], ACT.Exp).then_inc(S["s_e5d"], 1)

            def turned(j, b):
                act.wait_ge(passes[2]["turned"], j + 1)
                act.copy(rows_t[b][:, :, :], bank[2][:, 0:IN].rearrange("p (k n) -> p k n", k=KC))\
                    .then_inc(passes[2]["rows"], 1)

            def hidden_out(j, b, e, eb):
                act.wait_ge(s_we[eb], 16 * (e + 1))
                act.wait_ge(passes[2]["product"], j + 1)
                for f in range(FC):
                    act.activation(ht[:, b, f, :], bank[3][:, f * P:(f + 1) * P], ACT.Relu,
                                   bias=wexp[:, eb, EW - FC + f:EW - FC + f + 1]).then_inc(S["s_relu5"], 1)
                turned(j + 1, 1 - b)

            turned(0, 0)
            by_expert(act, hidden_out)
            act.wait_ge(S["s_ln"], 4)
            act.activation(lnv[:, 4, :], lnv[:, 3, :], ACT.Sqrt).then_inc(S["s_sq"], 1)
        @block.tensor
        def _(pe):
            pe.wait_ge(S["s_cnt"], 1)
            pe.matmul(bank[0][:, 0:TILES * TYPES], tri, oh_node.rearrange("p t y -> p (t y)"), start=True, stop=True)
            pe.matmul(bank[1][:, 0:TILES * TYPES], ones_sq[:, :], oh_node.rearrange("p t y -> p (t y)"),
                      start=True, stop=True).then_inc(S["s_cntp"], 1)
            pe.wait_ge(S["s_order"], 1)

            def counts(n, b, l, first=False):
                pe.wait_ge(S["s_oh"], n + 1 + l * GROUPS)
                if not first:
                    pe.wait_ge(S["s_hcp"], n - 1 + l * GROUPS)
                for c in range(HG):
                    last = pe.matmul(bank[b][:, c * TILES:(c + 1) * TILES], ohl[:, b, c, :],
                                     ohh[:, b, c, 0:TILES], start=True, stop=True)
                last.then_inc(S["s_hps"], 1)

            def rows_out(u, b, l):
                pe.wait_ge(S["s_rows"], u + 1 + l * UNITS)
                for c in range(4):
                    pe.matmul(bank[2 + b][:, c * P:(c + 1) * P], lohs[:, b, c, 0:1].to_broadcast([P, P]),
                              identb, start=True, stop=True)
                for c in range(4):
                    pe.matmul(bank[4 + b][:, c * P:(c + 1) * P], lohs[:, b, c, 0:1].to_broadcast([P, P]),
                              identb, start=True, stop=False)
                    last = pe.matmul(bank[4 + b][:, c * P:(c + 1) * P], lohs[:, b, c, 1:2].to_broadcast([P, P]),
                                     identb, start=False, stop=True)
                last.then_inc(S["s_copy"], 1)

            def look_up(u, b, l):
                pe.wait_ge(S["s_oht"], u + 1 + l * UNITS)
                for c in range(4):
                    last = pe.matmul(bank[6 + b][:, c * TILES:(c + 1) * TILES], oht[:, b, c, :],
                                     flat(excl[:, bass.ds(u * 4 + c, 1), :]), start=True, stop=True)
                last.then_inc(S["s_pg"], 1)

            for l in range(2):
                for b in range(2):
                    counts(b, b, l, l == 0)
                with pe.Fori(1, GROUPS // 2, 1) as i:
                    for b in range(2):
                        counts(2 * i + b, b, l)
                pe.wait_ge(S["s_cls"], l + 1)
                for k in range(4):
                    tiles = slice(k * CLASS_TILES, min(TILES, (k + 1) * CLASS_TILES))
                    picks = oh_class[:, tiles, :].rearrange("p t y -> p (t y)")
                    n = (tiles.stop - tiles.start) * CLASSES
                    pe.matmul(bank[k][:, 0:n], tri, picks, start=True, stop=True)
                    last = pe.matmul(bank[4 + k][:, 0:n], ones_sq[:, :], picks, start=True, stop=True)
                last.then_inc(S["s_clsp"], 1)
                rows_out(0, 0, l)
                with pe.Fori(0, UNITS // 2 - 1, 1) as i:
                    for b in range(2):
                        look_up(2 * i + b, b, l)
                        rows_out(2 * i + b + 1, 1 - b, l)
                look_up(UNITS - 2, 0, l)
                rows_out(UNITS - 1, 1, l)
                look_up(UNITS - 1, 1, l)

            def by_type(sems, weights, bias, width):
                def turn(j, b, first=False):
                    pe.wait_ge(sems[f"in{b}"], 16 * (j // 2 + 1))
                    if not first:
                        pe.wait_ge(sems["rows"], j)
                    for k in range(KC):
                        last = pe.transpose(bank[2][:, k * P:(k + 1) * P], rows_g[b][:, k * P:(k + 1) * P], ident)
                    last.then_inc(sems["turned"], 1)

                def product(j, b, first=False):
                    kind = pe.value_load(tile_type_i[0:1, bass.ds(j, 1)], min_val=0, max_val=TYPES - 1)
                    pe.wait_ge(sems["onehot"], j + 1)
                    pe.wait_ge(sems["rows"], j + 1)
                    if not first:
                        pe.wait_ge(sems["out"], j - 1)
                    to = bank[3 + b][:, 0:width]
                    pe.matmul(to, oh_tile[b][0:TYPES, :], bias[0:TYPES, :], start=True, stop=False)
                    for k in range(KC):
                        last = pe.matmul(to, rows_t[b][:, k, :], weights[:, k, bass.ds(kind, 1), :]
                                         .rearrange("p o n -> p (o n)"), start=False, stop=(k == KC - 1))
                    last.then_inc(sems["product"], 1)

                turn(0, 0, True)
                turn(1, 1)
                product(0, 0, True)
                turn(2, 0)
                product(1, 1, True)
                pairs = tile_pairs(pe)
                with pe.Fori(1, pairs, 1) as h:
                    for b in range(2):
                        turn(2 * h + b + 1, 1 - b)
                        product(2 * h + b, b)

            def pass_out(sems):
                pairs = tile_pairs(pe)
                return (sems["rows"], 2 * pairs + 1), (sems["out"], 2 * pairs)

            pe.wait_ge(S["s_fold"], 1)
            total = chunk_total(pe)
            by_type(passes[0], w_kvq, b_kvq, WCOLS)

            def piece_turn(i):
                pe.wait_ge(S["s_pvc"], i + 1)
                if not starts(i):
                    pe.wait_ge(S["s_ptc"], i)
                pe.transpose(bank[2][:, 0:P], piece, ident).then_inc(S["s_ptp"], 1)

            def piece_angles(i):
                pe.wait_ge(S["s_ptc"], i + 1)
                if not starts(i):
                    pe.wait_ge(S["s_ang"], i)
                for k in range(2):
                    last = pe.matmul(bank[3 + k][:, 0:C * PW], piecet[0:PCOL * PAY, :],
                                     embw[0:PCOL * PAY, k * C:(k + 1) * C, :, :].rearrange("p c k d -> p (c k d)"),
                                     start=True, stop=True)
                last.then_inc(S["s_pang"], 1)

            def chunk(g, b):
                pe.wait_ge(S["s_pvd"], g + 2)
                pe.wait_ge(S["s_e0"], g + 1)
                for c in range(C):
                    last = pe.matmul(bank[b][:, 0:PVW], ident, pv[b][:, c, :], start=(c == 0), stop=(c == C - 1))
                last.then_inc(s_pa[b], 1)

            pe.wait_ge(S["s_init"], 1)
            for i in range(AHEAD + 2):
                piece_turn(i)
                piece_angles(i)
            with pe.Fori(0, total, 1) as g:
                with pe.If(g % 2 == 0):
                    chunk(g, 0)
                    piece_turn(g // 2 + AHEAD + 2)
                with pe.Else():
                    chunk(g, 1)
                    piece_angles(g // 2 + AHEAD + 2)
            pe.wait_ge(S["s_gb"], 32)
            pe.wait_ge(S["s_w4m"], KC)
            by_type(passes[1], w_out, b_out, IN)
            drained = pass_out(passes[1])
            def scales(t, b):
                pe.wait_ge(S["s_oht4"], t + 1)
                for given, n in drained:
                    pe.wait_ge(given, n)
                pe.matmul(bank[3 + b][:, 0:2 * IN], oh_type4[0:TYPES, b, :], gb_sb[0:TYPES, :], start=True, stop=True)\
                    .then_inc(S["s_gbp"], 1)

            with pe.Fori(0, TILES // 2, 1) as i:
                for b in range(2):
                    scales(2 * i + b, b)
            scales(TILES - 1, 0)

            def turn5(t, b):
                pe.wait_ge(S["s_x5"], t + 1)
                for k in range(KC):
                    last = pe.transpose(bank[b][:, k * P:(k + 1) * P], xt5[:, b, k * P:(k + 1) * P], ident)
                last.then_inc(S["s_tp5"], 1)

            def gates(t, b):
                pe.wait_ge(S["s_t5"], t + 1)
                for k in range(KC):
                    pe.matmul(bank[2 + b][:, 0:EXPERTS], tt5[:, b, k, :], gw_sb[:, k, :], start=(k == 0), stop=False)
                pe.matmul(bank[2 + b][:, 0:EXPERTS], ones_row[:, :], gb16[0:1, :], start=False, stop=True)\
                    .then_inc(S["s_gps"], 1)

            pe.wait_ge(S["s_w5"], 64)
            turn5(0, 0)
            with pe.Fori(0, TILES // 2, 1) as i:
                for b in range(2):
                    turn5(2 * i + b + 1, 1 - b)
                    gates(2 * i + b, b)
            gates(TILES - 1, 0)
            pe.wait_ge(S["s_cnt5"], 1)
            for k in range(2):
                picks = sel[:, k * TILES:(k + 1) * TILES, :].rearrange("p t y -> p (t y)")
                pe.matmul(bank[k][:, 0:TILES * EXPERTS], tri, picks, start=True, stop=True)
                last = pe.matmul(bank[5 + k][:, 0:TILES * EXPERTS], ones_sq[:, :], picks, start=True, stop=True)
            last.then_inc(S["s_cntp5"], 1)
            moe_pass = passes[2]

            def turn(j, b, first=False):
                pe.wait_ge(moe_pass[f"in{b}"], 16 * (j // 2 + 1))
                if not first:
                    pe.wait_ge(moe_pass["rows"], j)
                for k in range(KC):
                    last = pe.transpose(bank[2][:, k * P:(k + 1) * P], rows_g[b][:, k * P:(k + 1) * P], ident)
                last.then_inc(moe_pass["turned"], 1)

            def expert_tile(j, b, e, eb):
                turn(j + 1, 1 - b)
                pe.wait_ge(s_we[eb], 16 * (e + 1))
                for f in range(FC):
                    for k in range(KC):
                        last = pe.matmul(bank[3][:, f * P:(f + 1) * P], wexp[:, eb, k * FF + f * P:k * FF + (f + 1) * P],
                                         rows_t[b][:, k, :], start=(k == 0), stop=(k == KC - 1))
                last.then_inc(moe_pass["product"], 1)
                pe.wait_ge(moe_pass["out"], j + 1)
                to = bank[4 + b][:, 0:IN]
                pe.matmul(to, ones_row[:, :], b2_row[0:1, bass.ds((2 * e + eb) * IN, IN)], start=True, stop=False)
                for f in range(FC):
                    pe.wait_ge(S["s_relu5"], FC * j + f + 1)
                    last = pe.matmul(to, ht[:, b, f, :], wexp[:, eb, KC * FF + f * IN:KC * FF + (f + 1) * IN],
                                     start=False, stop=(f == FC - 1))
                last.then_inc(S["s_outs5"], 1)

            pe.wait_ge(S["s_ready5"], 1)
            turn(0, 0, True)
            by_expert(pe, expert_tile)
        @block.vector
        def _(dve):
            ch = Chain(dve, S["s_dve"])
            dve.memset(zero[:, :], 0.0).then_inc(S["s_zero"], 1)
            ch.mark(dve.memset(ones[:, :], 1.0))
            ch.mark(dve.memset(ones_row[:, :], 1.0))
            ch.mark(dve.memset(ones_sq[:, :], 1.0))
            dve.memset(node_of[:, :], 1 << 20).then_inc(S["s_nodes"], 1)
            for b in range(2):
                ch.mark(dve.memset(rows_g[b][:, :], 0.0))
                ch.mark(dve.memset(rows_o[b][:, :], 0.0))
            dve.wait_ge(S["s_types"], 16)
            dve.wait_ge(S["s_con"], 16)
            ch.link(dve.tensor_copy(type_f, type_i[:, :]))
            dve.tensor_tensor(oh_node, iota[:, 0:TYPES].unsqueeze(1).to_broadcast([P, TILES, TYPES]),
                              type_f.unsqueeze(2).to_broadcast([P, TILES, TYPES]), ALU.is_equal).then_inc(S["s_cnt"], 1)
            ch.mark(dve.tensor_scalar(tgrid, iota[:, 0:TT], float(P), None, ALU.mult))
            ch.mark(dve.tensor_scalar(place, iota[:, 0:TILES], float(P), 1.0, ALU.mult, ALU.add))
            ch.wait()
            ch.mark(dve.tensor_scalar(row_i[:, :], place, pidx, None, ALU.add))
            dve.wait_ge(S["s_cntp"], 1)
            by_y = lambda b_: bank[b_][:, 0:TILES * TYPES].rearrange("p (t y) -> p y t", y=TYPES)
            ch.link(dve.tensor_copy(tcount[:, :, 0:TILES], by_y(1)))
            ch.link(dve.tensor_reduce(tnum[:, 0, :], tcount[:, :, 0:TILES], AX_X, ALU.add))
            ch.link(dve.tensor_scalar(tnum_i, tnum[:, 0, :], float(P - 1), None, ALU.add))
            ch.link(dve.tensor_scalar(tnum_i, tnum_i, 7, None, ALU.logical_shift_right))
            ch.link(dve.tensor_copy(tnum[:, 1, :], tnum_i))
            ch.link(dve.scalar_tensor_tensor(tcount[:, :, TILES], tnum[:, 1, :], float(P), tnum[:, 0, :],
                                             ALU.mult, ALU.subtract))
            flat2 = lambda v: v.rearrange("p y t -> p (y t)")
            ch.link(dve.tensor_tensor_scan(flat2(tscan), ones_sq[:, 0:1].to_broadcast([P, TYPES * (TILES + 1)]),
                                           flat2(tcount), 0.0, ALU.mult, ALU.add))
            ch.mark(dve.tensor_tensor(tend, tscan[:, :, TILES].unsqueeze(1).to_broadcast([P, TT, TYPES]),
                                      tgrid.unsqueeze(2).to_broadcast([P, TT, TYPES]), ALU.is_le))
            ch.mark(dve.tensor_scalar(tnum_i[:, 0:1], tscan[:, TYPES - 1, TILES:TILES + 1], float(P), None, ALU.add))
            ch.link(dve.tensor_tensor(tcount, tscan, tcount, ALU.subtract))
            ch.mark(dve.tensor_scalar(pairs_i[:, :], tnum_i[:, 0:1], 8, None, ALU.logical_shift_right))
            ch.mark(dve.tensor_reduce(tile_type[:, :], tend, AX_X, ALU.add))
            ch.link(dve.tensor_tensor(tbefore, bank[0][:, 0:TILES * TYPES].rearrange("p (t y) -> p t y", y=TYPES),
                                      tcount[:, :, 0:TILES].rearrange("p y t -> p t y"), ALU.add))
            ch.mark(dve.tensor_scalar(tile_type[:, :], tile_type[:, :], float(TYPES - 1), None, ALU.min))
            ch.link(dve.tensor_tensor(tbefore, tbefore, oh_node, ALU.mult))
            ch.mark(dve.tensor_copy(tile_type_i[:, :], tile_type[:, :]))
            ch.link(dve.tensor_reduce(place, tbefore, AX_X, ALU.add))
            ch.link(dve.tensor_copy(place_i[:, :], place))
            ch.link(dve.tensor_scalar(place_i[:, :], place_i[:, :], 7, None, ALU.logical_shift_right))
            ch.link(dve.tensor_copy(type_f, place_i[:, :]))
            ch.link(dve.tensor_scalar(place, place, float(TCOLS), None, ALU.mult))
            ch.link(dve.scalar_tensor_tensor(place, type_f, float(1 - P * TCOLS), place, ALU.mult, ALU.add))
            dve.tensor_copy(place_i[:, :], place).then_inc(S["s_order"], 1)
            dve.wait_ge(S["s_ids"], 16)
            ch.mark(dve.tensor_copy(identb, ident))
            ch.mark(dve.tensor_copy(idf, ids_i))
            ch.link(dve.tensor_scalar(tmp_i, ids_i, P - 1, None, ALU.bitwise_and))
            ch.link(dve.tensor_copy(lof, tmp_i))
            ch.mark(dve.tensor_copy(lohb[:, :, :, 0], lof))
            ch.link(dve.tensor_scalar(tmp_i, ids_i, 7, None, ALU.logical_shift_right))
            ch.link(dve.tensor_copy(hif, tmp_i))
            ch.mark(dve.tensor_scalar(lohb[:, :, :, 1], hif, float(P), None, ALU.mult))
            for l in range(2):
                ch.mark(dve.tensor_scalar(pay_i[:, l, :, 0], ids_i[:, 1 - l, :], 1.0, None, ALU.add))
                ch.mark(dve.memset(pay[:, l, :, PAY - 1], 1.0))
            ch.wait()

            def one_hots(n, b, l, first=False):
                if not first:
                    dve.wait_ge(S["s_hps"], n - 1 + l * GROUPS)
                at = bass.ds(n * HG, HG)
                dve.tensor_tensor(ohl[:, b, :, :], iota.unsqueeze(1).to_broadcast([P, HG, P]),
                                  lof[:, l, at].unsqueeze(2).to_broadcast([P, HG, P]), ALU.is_equal)
                dve.tensor_tensor(ohh[:, b, :, 0:TILES], iota[:, 0:TILES].unsqueeze(1).to_broadcast([P, HG, TILES]),
                                  hif[:, l, at].unsqueeze(2).to_broadcast([P, HG, TILES]), ALU.is_equal)\
                    .then_inc(S["s_oh"], 1)

            def row_parts(u, b, l):
                dve.tensor_copy(lohs[:, b, :, :], lohb[:, l, bass.ds(u * 4, 4), :]).then_inc(S["s_rows"], 1)

            def places(u, b, l):
                dve.wait_ge(S["s_copy"], u + 1 + l * UNITS)
                dve.tensor_scalar(oht[:, b, :, :], bank[2 + b][:, :].rearrange("p (c n) -> p c n", c=4), pidx, None,
                                  ALU.is_equal).then_inc(S["s_oht"], 1)

            def slots(u, b, l, first=False, last=0):
                at = bass.ds(u * 4, 4)
                if last < 2:
                    places(u + 1, 1 - b, l)
                for c in range(4):
                    ch.mark(dve.scalar_tensor_tensor(junk[:, c, :], bank[4 + b][:, c * P:(c + 1) * P],
                                                     idf[:, l, bass.ds(u * 4 + c, 1)], tri, ALU.is_equal, ALU.mult,
                                                     accum_out=rank[:, c:c + 1]))
                if last < 1:
                    row_parts(u + 2, b, l)
                ch.mark(dve.tensor_scalar(padp[:, b, :], hif[:, l, at], float(TILES), PAD_SLOT, ALU.is_ge, ALU.mult))
                ch.link(dve.tensor_tensor(ohhf, iota[:, 0:TILES].unsqueeze(1).to_broadcast([P, 4, TILES]),
                                          hif[:, l, at].unsqueeze(2).to_broadcast([P, 4, TILES]), ALU.is_equal))
                dve.wait_ge(S["s_pg"], u + 1 + l * UNITS)
                ch.link(dve.tensor_tensor(selp, bank[6 + b][:, 0:4 * TILES].rearrange("p (c b) -> p c b", c=4),
                                          ohhf, ALU.mult))
                ch.link(dve.tensor_reduce(selv, selp, AX_X, ALU.add))
                ch.link(dve.scalar_tensor_tensor(slotf, rank, float(P), selv, ALU.mult, ALU.add))
                if not first:
                    dve.wait_ge(s_sc[b], 64 * ((u + l * UNITS) // 2))
                ch.mark(dve.tensor_scalar(stage_i[:, b, :, :], pay_i[:, l, at, :], 0, None, ALU.bitwise_or))
                dve.tensor_tensor(slot[:, b, :], slotf, padp[:, b, :], ALU.add).then_inc(S["s_slot"], 1)

            dve.wait_ge(S["s_log"], 6)
            for l in range(2):
                for b in range(2):
                    one_hots(b, b, l, l == 0)
                with dve.Fori(1, GROUPS // 2, 1) as i:
                    for b in range(2):
                        one_hots(2 * i + b, b, l)
                dve.wait_ge(S["s_hcp"], GROUPS * (l + 1))
                with dve.Fori(0, TILES, 1) as t:
                    dve.tensor_tensor_scan(excl[:, :, bass.ds(t, 1)].rearrange("p e o -> p (e o)"),
                                           ones[:, 0:1].to_broadcast([P, EC]),
                                           hist[:, :, bass.ds(t, 1)].rearrange("p e o -> p (e o)"),
                                           0.0, ALU.mult, ALU.add).then_inc(S["s_agg"], 1)
                dve.wait_ge(S["s_agg"], TILES * (l + 1))
                ch.link(dve.tensor_copy(deg, excl[:, EC - 1, :]))
                ch.link(dve.tensor_tensor(excl, excl, hist, ALU.subtract))
                ch.link(dve.tensor_scalar(node_class, deg, float(CLASSES - 1), None, ALU.min))
                ch.link(dve.tensor_scalar(node_class, node_class, -1.0, float(CLASSES - 1), ALU.mult, ALU.add))
                dve.tensor_tensor(oh_class, iota[:, 0:CLASSES].unsqueeze(1).to_broadcast([P, TILES, CLASSES]),
                                  node_class.unsqueeze(2).to_broadcast([P, TILES, CLASSES]), ALU.is_equal)\
                    .then_inc(S["s_cls"], 1)
                dve.wait_ge(S["s_cls"], l + 1)
                dve.wait_ge(S["s_clsp"], l + 1)
                parts = [(k, slice(k * CLASS_TILES, min(TILES, (k + 1) * CLASS_TILES))) for k in range(4)]
                counted = lambda n_, at_: bank[n_][:, 0:(at_.stop - at_.start) * CLASSES]
                for k, at in parts:
                    ch.mark(dve.tensor_copy(ccount[:, :, at], counted(4 + k, at).rearrange("p (t y) -> p y t", y=CLASSES)))
                ch.wait()
                ch.link(dve.tensor_tensor_scan(flat2(cscan), ones_sq[:, 0:1].to_broadcast([P, CLASSES * TILES]),
                                               flat2(ccount), 0.0, ALU.mult, ALU.add))
                ch.link(dve.tensor_tensor(ccount, cscan, ccount, ALU.subtract))
                for k, at in parts:
                    ch.mark(dve.tensor_tensor(cbefore[:, at, :], counted(k, at).rearrange("p (t y) -> p t y", y=CLASSES),
                                              ccount[:, :, at].rearrange("p y t -> p t y"), ALU.add))
                ch.wait()
                ch.link(dve.tensor_tensor(cbefore, cbefore, oh_class, ALU.mult))
                ch.link(dve.tensor_reduce(place_r, cbefore, AX_X, ALU.add))
                ch.mark(dve.tensor_scalar(order_i[:, l * TILES:(l + 1) * TILES], place_r, float(l * TILES * P), None,
                                          ALU.add))
                ch.link(dve.tensor_copy(tile_ri, place_r))
                ch.link(dve.tensor_scalar(tile_ri, tile_ri, 7, None, ALU.logical_shift_right))
                ch.link(dve.tensor_copy(tile_r, tile_ri))
                squared = [P, TILES, TILES]
                ch.link(dve.tensor_tensor(oh_tile_of, iota[:, 0:TILES].unsqueeze(1).to_broadcast(squared),
                                          tile_r.unsqueeze(2).to_broadcast(squared), ALU.is_equal))
                ch.link(dve.tensor_tensor(tile_work, oh_tile_of, deg.unsqueeze(2).to_broadcast(squared), ALU.mult))
                dve.tensor_reduce(deg_sorted, tile_work.rearrange("p t u -> p u t"), AX_X, ALU.max)\
                    .then_inc(S["s_deg"], 1)
                dve.wait_ge(S["s_mdeg"], l + 1)
                if l == 0:
                    ch.mark(dve.memset(startf[:, 0:1], 0.0))
                ch.link(dve.tensor_scalar(chunks_i, maxdeg, float(C - 1), None, ALU.add))
                ch.link(dve.tensor_scalar(chunks_i, chunks_i, 2, None, ALU.logical_shift_right))
                ch.link(dve.tensor_copy(chunks, chunks_i))
                ch.link(dve.tensor_scalar(chunks, chunks, 1.0, None, ALU.max))
                o = l * TILES
                ch.link(dve.tensor_tensor_scan(startf[:, o + 1:o + TILES + 1], ones[:, :], chunks,
                                               startf[:, o:o + 1], ALU.mult, ALU.add))
                ch.mark(dve.tensor_copy(start_i[:, o:o + TILES + 1], startf[:, o:o + TILES + 1]))
                ch.mark(dve.tensor_scalar(fillf[:, 1:2], startf[:, o + TILES:o + TILES + 1],
                                          float(15 + l * 24), None, ALU.add))
                ch.link(dve.scalar_tensor_tensor(start_diff, startf[:, o:o + TILES], float(C), iota[:, 0:TILES],
                                                 ALU.mult, ALU.subtract))
                ch.link(dve.tensor_tensor(tile_work, oh_tile_of, start_diff.unsqueeze(1).to_broadcast(squared),
                                          ALU.mult))
                ch.link(dve.tensor_reduce(base, tile_work, AX_X, ALU.add))
                ch.link(dve.scalar_tensor_tensor(base, base, float(P), place_r, ALU.mult, ALU.add))
                ch.mark(dve.scalar_tensor_tensor(excl, excl, float(P), base.unsqueeze(1)
                                                 .to_broadcast([P, EC, TILES]), ALU.mult, ALU.add))
                ch.link(dve.tensor_copy(fills_i[:, 2 * l + 1:2 * l + 2], fillf[:, 1:2]))
                ch.link(dve.tensor_scalar(fills_i[:, 2 * l + 1:2 * l + 2], fills_i[:, 2 * l + 1:2 * l + 2], 4, None,
                                          ALU.logical_shift_right))
                if l == 0:
                    ch.mark(dve.tensor_copy(fills_i[:, 2:3], fills_i[:, 1:2]))
                    ch.link(dve.memset(fills_i[:, 0:1], 0))
                dve.tensor_copy(fillf[:, 2:3], fillf[:, 1:2]).then_inc(S["s_start"], 1)
                ch.wait()
                row_parts(0, 0, l)
                row_parts(1, 1, l)
                places(0, 0, l)
                k0 = ch.base + ch.n
                for b in range(2):
                    slots(b, b, l, l == 0)
                per = ch.base + ch.n - k0
                with dve.Fori(1, UNITS // 2 - 1, 1) as i:
                    for b in range(2):
                        ch.at(k0 + i * per + b * (per // 2))
                        slots(2 * i + b, b, l)
                ch.at(k0 + (UNITS // 2 - 1) * per)
                slots(UNITS - 2, 0, l, last=1)
                slots(UNITS - 1, 1, l, last=2)

            def ln_rest(k):
                me, mo, ve, vo = (stats[:, :, j] for j in (1, 4, 2, 5))
                ch.mark(dve.tensor_tensor(lnv[:, 0, :], me, mo, ALU.add))
                ch.mark(dve.tensor_tensor(lnv[:, 1, :], me, mo, ALU.subtract))
                ch.link(dve.tensor_tensor(lnv[:, 2, :], ve, vo, ALU.add))
                ch.mark(dve.tensor_scalar(lnv[:, 0, :], lnv[:, 0, :], 0.5, None, ALU.mult))
                ch.mark(dve.tensor_tensor(lnv[:, 1, :], lnv[:, 1, :], lnv[:, 1, :], ALU.mult))
                ch.link(dve.tensor_scalar(lnv[:, 2, :], lnv[:, 2, :], 1.0 / IN, EPS, ALU.mult, ALU.add))
                dve.scalar_tensor_tensor(lnv[:, 3, :], lnv[:, 1, :], 0.25, lnv[:, 2, :], ALU.mult, ALU.add)\
                    .then_inc(S["s_ln"], 1)
                dve.wait_ge(S["s_sq"], k)
                ch.link(dve.reciprocal(lnv[:, 5, :], lnv[:, 4, :]))

            dve.wait_ge(S["s_x"], 16)
            with dve.Fori(0, TILES, 1) as t:
                dve.bn_stats(flat(stats[:, bass.ds(t, 1), :]), flat(xn[:, bass.ds(t, 1), :])).then_inc(S["s_dvs"], 1)
            dve.wait_ge(S["s_dvs"], TILES)
            ln_rest(1)

            with dve.Fori(0, TILES, 1) as t:
                tl, ti = flat(xn[:, bass.ds(t, 1), :]), bass.ds(t, 1)
                dve.tensor_scalar(tl, tl, mean[:, ti], rstd[:, ti], ALU.subtract, ALU.mult).then_inc(S["s_xn"], 1)
            dve.wait_ge(S["s_w"], 16 * 12)
            q = w_kvq[:, :, :, 2 * PROJ:WCOLS]
            qb = b_kvq[0:TYPES, 2 * PROJ:WCOLS]
            for j in range(3):
                n = min(DK, PROJ - DK - j * DK)
                ch.mark(dve.tensor_tensor(q[:, :, :, 0:n], q[:, :, :, 0:n], q_rest[:, :, :, j * DK:j * DK + n], ALU.add))
                ch.link(dve.tensor_tensor(qb[:, 0:n], qb[:, 0:n], bq_rest[0:TYPES, j * DK:j * DK + n], ALU.add))
            dve.memset(signal_cell[:, :], 0.0).then_inc(S["s_fold"], 1)

            def by_type(sems):
                def one_hot(j, b, first=False):
                    if not first:
                        dve.wait_ge(sems["product"], j - 1)
                    dve.tensor_scalar(oh_tile[b][0:TYPES, :], tile_type[0:TYPES, bass.ds(j, 1)]
                                      .to_broadcast([TYPES, P]), pidx[0:TYPES, :], None,
                                      ALU.is_equal).then_inc(sems["onehot"], 1)

                for b in range(2):
                    one_hot(b, b, True)
                pairs = tile_pairs(dve)
                with dve.Fori(1, pairs, 1) as h:
                    for b in range(2):
                        one_hot(2 * h + b, b)
                for b in range(2):
                    dve.wait_ge(sems[f"put{b}"], 16 * pairs)
                dve.wait_ge(sems["rows"], 2 * pairs + 1)
                dve.wait_ge(sems["in0"], 16 * (pairs + 1))
                dve.wait_ge(sems["in1"], 16 * (pairs + 1))

            by_type(passes[0])
            dve.wait_ge(S["s_qs2"], 16)
            dve.wait_ge(S["s_xn"], TILES)
            dve.wait_ge(S["s_wt"], 32)
            ch.mark(dve.memset(acc[:, :, :, :], 0.0))
            ch.mark(dve.memset(esum[:, :, :], 0.0))
            ch.mark(dve.memset(rows[:, 3 * C:4 * C, :], 0.0))
            ch.mark(dve.memset(roundc, ROUND))
            ch.mark(dve.memset(piece, 0.0))
            for b in range(2):
                ch.mark(dve.memset(pv[b], 0.0))
            ch.mark(dve.tensor_scalar(wtb[:, 1, :], wtb[:, 1, :], TWO_PI / 4, None, ALU.add))
            ch.wait()
            ch.mark(dve.memset(rescale, 1.0))
            ch.link(dve.tensor_scalar(wtb, wtb, 1.0 / TWO_PI, None, ALU.mult))
            for k, emb_part in enumerate((embw, embb)):
                words = (embsel[:, 0:3 * PCOL].rearrange("p (c k) -> p c k", c=PCOL) if k == 0
                         else embsel[:, 3 * PCOL:4 * PCOL].unsqueeze(2).to_broadcast([P, PCOL, 3]))
                ch.mark(dve.tensor_tensor(emb_part, words.unsqueeze(3).to_broadcast([P, PCOL, 3, TD]),
                                          wtb[:, k, :].unsqueeze(1).unsqueeze(1).to_broadcast([P, PCOL, 3, TD]),
                                          ALU.mult))
            ch.wait()
            ch.link(dve.tensor_tensor(embw, embw, embb, ALU.add))
            for b in range(2):
                dve.memset(bank[b][:, :], 0.0).then_inc(s_pa[b], 1)
                dve.wait_ge(s_pa[b], 1)
            dve.memset(ex[0], 0.0).then_inc(S["s_ex"], 1)
            dve.wait_ge(S["s_ex"], 1)
            dve.memset(signal_cell[:, :], 0.0).then_inc(S["s_init"], 1)

            def angles(i):
                at = bass.ds((i % WIN) * PCOL, PCOL)
                dve.wait_ge(S["s_rnd"], i + 1)
                if not starts(i):
                    dve.wait_ge(S["s_pen"], i)
                dve.tensor_scalar(penal[:, at], payw_i[:, bass.ds((i % (RING * WIN // 2)) * PCOL, PCOL), 0], 0.0, PEN,
                                  ALU.is_equal, ALU.mult).then_inc(S["s_pen"], 1)
                for k in range(2):
                    ins = dve.scalar_tensor_tensor(
                        emb[:, bass.ds((i % WIN) * PCOL + k * C, C), :, :].rearrange("p c k d -> p (c k d)"),
                        rnd[:, k, :], ROUND, bank[3 + k][:, 0:C * PW], ALU.subtract, ALU.subtract)
                ins.then_inc(S["s_ang"], 1)

            def fold(prev, b, at4):
                c3.link(scale(prev, at4))
                c3.mark(add(prev, b))

            def scale(prev, at4):
                tot = acc_all[:, bass.ds(prev, 1), 0:SUMW].rearrange("p o (h d) -> p (o h) d", h=HEADS)
                return dve.tensor_tensor(tot, tot, flat(rescale[:, bass.ds(at4, 1), :]).unsqueeze(2).to_broadcast([P, HEADS, DK + 1]),
                                         ALU.mult)

            def add(prev, b):
                tot = flat(acc_all[:, bass.ds(prev, 1), :])
                return dve.tensor_tensor(tot, tot, bank[b][:, 0:PVW], ALU.add)

            def chunk(g, b, own, prev2):
                at = bass.ds(dve.snap((g % (2 * WIN)) * C, min_val=0, max_val=2 * WCOL - C), C)
                at_rows = bass.ds(dve.snap((g % 4) * C, min_val=0, max_val=3 * C), C)
                dve.wait_ge(S["s_emb"], g // WIN + 1)
                c3.mark(dve.tensor_tensor(qe[:, :, DK - TD:DK], emb[:, at, 2, :],
                                          own[:, DK - TD:DK].unsqueeze(1).to_broadcast([P, C, TD]), ALU.add))
                c3.wait(1)
                dve.wait_ge(S["s_gap"], 2 * g + 2)
                keys = rows[:, at_rows, 0:HD].rearrange("p c (h d) -> p c h d", h=HEADS)
                c3.mark(dve.tensor_tensor(prod, keys, qe.unsqueeze(2).to_broadcast([P, C, HEADS, DK]), ALU.mult))
                c3.wait(2)
                dve.wait_ge(S["s_ex"], g + 1)
                c3.mark(dve.tensor_reduce(att[b][:, 0:C, :], prod, AX_X, ALU.add))
                c3.wait(3)
                c3.link(dve.tensor_tensor(att[b][:, 0:C, :], att[b][:, 0:C, :],
                                          penal[:, at].unsqueeze(2).to_broadcast([P, C, HEADS]), ALU.add))
                c3.link(dve.tensor_reduce(att[1 - b][:, C, :], att[b].rearrange("p c h -> p h c"), AX_X, ALU.max))
                dve.tensor_tensor(ex[b], att[b], att[1 - b][:, C, :].unsqueeze(1).to_broadcast([P, C + 1, HEADS]),
                                  ALU.subtract).then_inc(S["s_ex"], 1)
                dve.wait_ge(s_pa[b], g // 2 + 1)
                c3.mark(scale(prev2, (g + 2) % 4))
                if b == 0:
                    angles(g // 2 + AHEAD)
                values_before(g, 1 - b)
                c3.wait(6)
                c3.mark(add(prev2, b))

            def values_before(g, b):
                dve.wait_ge(S["s_pe"], g + 1)
                vals = rows[:, bass.ds(((g + 3) % 4) * C, C), HD:ROW].rearrange("p c (h d) -> p c h d", h=HEADS)
                dve.tensor_tensor(pvh[b][:, 0:C, :, 0:DK], vals, pvh[b][:, 0:C, :, DK].unsqueeze(3)
                                  .to_broadcast([P, C, HEADS, DK]), ALU.mult).then_inc(S["s_pvd"], 1)

            c3 = Chain(dve, S["s_dv3"])
            PER = 7
            for i in range(AHEAD):
                angles(i)
            dve.memset(ex[1], 0.0).then_inc(S["s_pe"], 1)
            total = chunk_total(dve)
            before, before2 = (dve.alloc_register(n) for n in ("block_before", "block_before2"))
            dve.reg_mov(before, 0)
            dve.reg_mov(before2, 0)
            with dve.Fori(0, 2, 1) as l:
                with dve.Fori(0, TILES, 1) as tile:
                    blk = l * TILES + tile
                    lo, hi = chunk_range(dve, blk)
                    own = flat(qs2[:, bass.ds(blk, 1), :])
                    dve.wait_ge(S["s_ex"], lo + 1)
                    c3.at(lo * PER + blk * 3)
                    for b in range(2):
                        c3.mark(dve.memset(att[b][:, C, :], MINIT))
                    c3.mark(dve.tensor_scalar(qe[:, :, 0:DK - TD], own[:, 0:DK - TD].unsqueeze(1)
                                              .to_broadcast([P, C, DK - TD]), 0.0, None, ALU.add))
                    with dve.Fori(lo, hi, 1) as g:
                        prev2 = dve.snap(before2, min_val=0, max_val=BLOCKS - 1)
                        marks = dve.snap(g * PER + (blk + 1) * 3, min_val=3, max_val=GMAX * PER)
                        for b in range(2):
                            with (dve.Else() if b else dve.If(g % 2 == 0)):
                                c3.at(marks)
                                chunk(g, b, own, prev2)
                                assert c3.n == PER, c3.n
                        dve.reg_mov(before2, before)
                        dve.reg_mov(before, blk)
            prev2 = dve.snap(before2, min_val=0, max_val=BLOCKS - 1)
            for b in range(2):
                with (dve.Else() if b else dve.If(total % 2 == 0)):
                    c3.at(total * PER + BLOCKS * 3)
                    dve.wait_ge(s_pa[b], total // 2 + 1)
                    if b == 0:
                        angles(total // 2 + AHEAD)
                    c3.wait()
                    fold(prev2, b, (total + 2) % 4)
                    c3.wait()
                    values_before(total, 1 - b)
                    dve.wait_ge(s_pa[1 - b], (total + 1) // 2 + 1)
                    c3.wait()
                    fold(BLOCKS - 1, 1 - b, (total + 3) % 4)
            dve.memset(ex[1], 0.0).then_inc(S["s_pvd"], 4)
            dve.wait_ge(S["s_gap"], 2 * total + 4)
            dve.wait_ge(S["s_emb"], (total + 5) // WIN + 1)
            dve.wait_ge(S["s_ptp"], (total + 1) // 2 + AHEAD + 2)
            dve.wait_ge(S["s_pang"], total // 2 + AHEAD + 2)
            dve.wait_ge(S["s_rnd"], total // 2 + AHEAD + 1)
            dve.wait_ge(S["s_ang"], total // 2 + AHEAD + 1)
            dve.wait_ge(S["s_dv3"], total * PER + BLOCKS * 3 + 4)
            dve.wait_ge(S["s_pool3"], 1)
            ch.mark(dve.tensor_scalar(inv, acc[:, :, :, DK], 1e-16, None, ALU.add))
            dve.memset(signal_cell[:, :], 0.0).then_inc(S["s_last"], 1)
            ch.wait()
            ch.link(dve.reciprocal(inv, inv))
            mean_v = acc[:, :, :, 0:DK]
            dve.tensor_tensor(mean_v, mean_v, inv.unsqueeze(3).to_broadcast([P, BLOCKS, HEADS, DK]), ALU.mult)\
                .then_inc(S["s_aggd"], 1)
            for k in range(KC):
                dve.wait_ge(s_w4[k], 32)
                dve.tensor_tensor(w_out[:, k, :, :], w_out[:, k, :, :], w_low, ALU.add).then_inc(S["s_w4m"], 1)
            dve.wait_ge(S["s_typ4"], 16)
            dve.wait_ge(S["s_w4m"], KC)
            ch.link(dve.tensor_copy(typrow4, typrow4_i))
            dve.wait_ge(S["s_accg"], 16 * BLOCKS)
            ch.link(dve.tensor_tensor(agg[:, :, HD:IN], esum[:, 0:TILES, :], esum[:, TILES:BLOCKS, :], ALU.add))
            dve.tensor_tensor(agg[:, :, 0:HD].rearrange("p t (h d) -> p t h d", h=HEADS), mean_v[:, 0:TILES],
                              mean_v[:, TILES:BLOCKS], ALU.add).then_inc(S["s_aggs"], 1)

            def one_hot4(t, b):
                dve.tensor_scalar(oh_type4[0:TYPES, b, :], typrow4[0:TYPES, bass.ds(t * P, P)], pidx[0:TYPES, :], None,
                                  ALU.is_equal).then_inc(S["s_oht4"], 1)

            by_type(passes[1])
            c4 = Chain(dve, S["s_dv4"])
            dve.wait_ge(S["s_od"], 16)
            ch.link(dve.tensor_tensor(xn[:, :, :], agg, xn[:, :, :], ALU.add))
            with dve.Fori(0, TILES, 1) as t:
                dve.bn_stats(flat(stats[:, bass.ds(t, 1), :]), flat(xn[:, bass.ds(t, 1), :])).then_inc(S["s_bn"], 1)
            dve.wait_ge(S["s_bn"], TILES)
            ln_rest(2)
            dve.wait_ge(S["s_xraw"], 16)
            with dve.Fori(0, TILES, 1) as t:
                tl, ti = flat(xn[:, bass.ds(t, 1), :]), bass.ds(t, 1)
                dve.tensor_scalar(tl, tl, mean[:, ti], rstd[:, ti], ALU.subtract, ALU.mult).then_inc(S["s_dv4"], 1)
            dve.wait_ge(S["s_dv4"], TILES)

            def scale4(t, b, last=False):
                if not last:
                    one_hot4(t + 1, 1 - b)
                c4.at(TILES + t * 2)
                tl = flat(xn[:, bass.ds(t, 1), :])
                dve.wait_ge(S["s_gbp"], t + 1)
                c4.link(dve.tensor_tensor(tl, tl, bank[3 + b][:, 0:IN], ALU.mult))
                c4.mark(dve.tensor_tensor(tl, tl, bank[3 + b][:, IN:2 * IN], ALU.add))

            one_hot4(0, 0)
            with dve.Fori(0, TILES // 2, 1) as i:
                for b in range(2):
                    scale4(2 * i + b, b)
            scale4(TILES - 1, 0, True)
            c4.wait()
            ch.link(dve.tensor_tensor(xn[:, :, :], xn[:, :, :], xraw, ALU.add))
            with dve.Fori(0, TILES, 1) as t:
                dve.bn_stats(flat(stats[:, bass.ds(t, 1), :]), flat(xn[:, bass.ds(t, 1), :])).then_inc(S["s_z4"], 1)
            dve.wait_ge(S["s_z4"], TILES)
            ln_rest(3)

            dve.memset(item_of_i, 1 << 20).then_inc(S["s_nodes"], 1)
            def tile_in5(t, b, first=False):
                if not first:
                    dve.wait_ge(S["s_tp5"], t - 1)
                ti = bass.ds(t, 1)
                dve.tensor_scalar(xt5[:, b, :], flat(xn[:, ti, :]), mean[:, ti], rstd[:, ti], ALU.subtract, ALU.mult)\
                    .then_inc(S["s_x5"], 1)
                dve.tensor_scalar(flat(xn2[:, ti, :]), flat(xn[:, ti, :]), mean[:, ti], rstd[:, ti],
                                  ALU.subtract, ALU.mult).then_inc(S["s_xn2"], 1)

            def logits(t, b):
                dve.wait_ge(S["s_gps"], t + 1)
                dve.tensor_scalar(flat(logit[:, bass.ds(t, 1), :]), bank[2 + b][:, 0:EXPERTS], 0.0, None, ALU.add)\
                    .then_inc(S["s_lg"], 1)

            tile_in5(0, 0, True)
            tile_in5(1, 1, True)
            with dve.Fori(0, (TILES - 3) // 2, 1) as i:
                for b in range(2):
                    logits(2 * i + b, b)
                    tile_in5(2 * i + b + 2, b)
            logits(TILES - 3, 0)
            tile_in5(TILES - 1, 0)
            logits(TILES - 2, 1)
            logits(TILES - 1, 0)
            dve.wait_ge(S["s_lg"], TILES)
            wide = [P, TILES, EXPERTS]
            rev = gstat
            ch.link(dve.tensor_scalar(rev, iota[:, 0:EXPERTS], -1.0, float(EXPERTS), ALU.mult, ALU.add))
            for k, chosen in enumerate((sel1, sel2)):
                ch.link(dve.tensor_reduce(top[:, k, :], logit, AX_X, ALU.max))
                ch.link(dve.tensor_tensor(cand, logit, top[:, k, :].unsqueeze(2).to_broadcast(wide), ALU.is_equal))
                ch.link(dve.tensor_tensor(cand, cand, rev.unsqueeze(1).to_broadcast(wide), ALU.mult))
                ch.link(dve.tensor_reduce(top[:, 4, :], cand, AX_X, ALU.max))
                ch.link(dve.tensor_tensor(chosen, cand, top[:, 4, :].unsqueeze(2).to_broadcast(wide), ALU.is_equal))
                if k == 0:
                    ch.link(dve.scalar_tensor_tensor(logit, chosen, PEN, logit, ALU.mult, ALU.add))
            dve.memset(signal_cell[:, :], 0.0).then_inc(S["s_cnt5"], 1)
            dve.tensor_tensor(top[:, 2, :], top[:, 1, :], top[:, 0, :], ALU.subtract).then_inc(S["s_e5"], 1)
            dve.wait_ge(S["s_e5d"], 1)
            ch.link(dve.tensor_scalar(top[:, 4, :], top[:, 3, :], 1.0, None, ALU.add))
            ch.link(dve.reciprocal(top[:, 4, :], top[:, 4, :]))
            ch.link(dve.tensor_tensor(top[:, 5, :], top[:, 3, :], top[:, 4, :], ALU.mult))
            for k in range(2):
                at = slice(k * TILES, (k + 1) * TILES)
                ch.mark(dve.tensor_copy(items_i[:, at, 0], row_i[:, :]))
                ch.mark(dve.tensor_scalar(items_i[:, at, 1], row_i[:, :], float(k * TILES * P), None, ALU.add))
                ch.mark(dve.tensor_copy(items[:, at, 2], top[:, 4 + k, :]))
            dve.wait_ge(S["s_cntp5"], 1)
            by_e = lambda b_: bank[b_][:, 0:TILES * EXPERTS].rearrange("p (t y) -> p y t", y=EXPERTS)
            for k in range(2):
                ch.mark(dve.tensor_copy(ecount[:, :, k * TILES:(k + 1) * TILES], by_e(5 + k)))
            ch.wait()
            ch.link(dve.tensor_reduce(num5[:, 0, :], ecount[:, :, 0:PICKS], AX_X, ALU.add))
            ch.link(dve.tensor_scalar(num5_i, num5[:, 0, :], float(P - 1), None, ALU.add))
            ch.link(dve.tensor_scalar(num5_i, num5_i, 7, None, ALU.logical_shift_right))
            ch.link(dve.tensor_copy(num5[:, 1, :], num5_i))
            ch.link(dve.tensor_scalar(num5[:, 1, :], num5[:, 1, :], 1.0, None, ALU.max))
            ch.link(dve.scalar_tensor_tensor(ecount[:, :, PICKS], num5[:, 1, :], float(P), num5[:, 0, :],
                                             ALU.mult, ALU.subtract))
            ch.link(dve.tensor_tensor_scan(flat2(escan), ones_sq[:, 0:1].to_broadcast([P, EXPERTS * (PICKS + 1)]),
                                           flat2(ecount), 0.0, ALU.mult, ALU.add))
            ch.mark(dve.memset(firstf[:, 0:1], 0.0))
            ch.mark(dve.tensor_scalar(firstf[:, 1:], escan[:, :, PICKS], 1.0 / P, None, ALU.mult))
            ch.link(dve.tensor_tensor(ecount, escan, ecount, ALU.subtract))
            ch.link(dve.tensor_copy(first_i, firstf))
            ch.link(dve.tensor_scalar(pairs5_i, firstf[:, EXPERTS:], 1.0, None, ALU.add))
            ch.link(dve.tensor_scalar(pairs5_i, pairs5_i, 1, None, ALU.logical_shift_right))
            ch.link(dve.tensor_scalar(first_i[:, EXPERTS:], pairs5_i, 1, None, ALU.logical_shift_left))
            for k in range(2):
                at = slice(k * TILES, (k + 1) * TILES)
                ch.mark(dve.tensor_tensor(ebefore[:, at, :], bank[k][:, 0:TILES * EXPERTS]
                                          .rearrange("p (t y) -> p t y", y=EXPERTS),
                                          ecount[:, :, at].rearrange("p y t -> p t y"), ALU.add))
            ch.wait()
            ch.link(dve.tensor_tensor(ebefore, ebefore, sel, ALU.mult))
            ch.link(dve.tensor_reduce(place5, ebefore, AX_X, ALU.add))
            ch.link(dve.tensor_copy(place5_i, place5))
            ch.link(dve.tensor_scalar(place5_i, place5_i, 7, None, ALU.logical_shift_right))
            ch.link(dve.tensor_copy(hi5, place5_i))
            ch.link(dve.tensor_scalar(place5, place5, float(MCOLS), None, ALU.mult))
            ch.link(dve.scalar_tensor_tensor(place5, hi5, float(1 - P * MCOLS), place5, ALU.mult, ALU.add))
            moe_pass = passes[2]
            for b in range(2):
                dve.memset(signal_cell[:, :], 0.0).then_inc(moe_pass["out"], 1)
                dve.wait_ge(moe_pass["out"], b + 1)
            ch.link(dve.tensor_copy(place5_i, place5))
            dve.memset(signal_cell[:, :], 0.0).then_inc(S["s_order5"], 1)
            dve.wait_ge(S["s_order5"], 1)
            dve.memset(signal_cell[:, :], 0.0).then_inc(S["s_ready5"], 1)
            dve.wait_ge(S["s_full"], 64)

            def weighted(j, b, e, eb):
                dve.wait_ge(S["s_outs5"], j + 1)
                dve.wait_ge(moe_pass["idx_out"], j + 1)
                dve.tensor_scalar(rows_o[b][:, 0:IN], bank[4 + b][:, 0:IN], flat(item_of[:, bass.ds(j, 1), :])[:, 2:3],
                                  None, ALU.mult).then_inc(moe_pass["out"], 1)

            by_expert(dve, weighted)
            dve.wait_ge(S["s_po"], 32)
            ch.link(dve.tensor_tensor(moe, moe, moe2, ALU.add))
            ch.link(dve.tensor_tensor(moe, moe, xn2, ALU.add))
            with dve.Fori(0, TILES, 1) as t:
                dve.bn_stats(flat(stats[:, bass.ds(t, 1), :]), flat(moe[:, bass.ds(t, 1), :])).then_inc(S["s_bn"], 1)
            dve.wait_ge(S["s_bn"], 2 * TILES)
            ln_rest(4)
            with dve.Fori(0, TILES // GROUP, 1) as i:
                c4.at(3 * TILES + i * (GROUP + 2))
                at = bass.ds(i * GROUP, GROUP)
                shape = [P, GROUP, IN]
                for k in range(GROUP):
                    m, ti = flat(moe[:, bass.ds(i * GROUP + k, 1), :]), bass.ds(i * GROUP + k, 1)
                    c4.mark(dve.tensor_scalar(m, m, mean[:, ti], rstd[:, ti], ALU.subtract, ALU.mult))
                c4.wait()
                c4.link(dve.tensor_tensor(moe[:, at, :], moe[:, at, :],
                                          fgb_sb[:, 0:IN].unsqueeze(1).to_broadcast(shape), ALU.mult))
                c4.link(dve.tensor_tensor(moe[:, at, :], moe[:, at, :],
                                          fgb_sb[:, IN:2 * IN].unsqueeze(1).to_broadcast(shape), ALU.add))
                dve.tensor_tensor(xn[:, at, :], xn[:, at, :], moe[:, at, :], ALU.add).then_inc(S["s_o5"], 1)


def kernel(x, src, dst, edge_attr_5, node_type_19, L0_gnn_Wk, L0_gnn_bk, L0_gnn_Wq, L0_gnn_bq, L0_gnn_Wv, L0_gnn_bv,
           L0_gnn_Wa, L0_gnn_ba, L0_gnn_gamma, L0_gnn_beta, L0_gnn_w_time, L0_gnn_b_time, L0_ffn_gate_w,
           L0_ffn_gate_b, L0_ffn_w1, L0_ffn_b1, L0_ffn_w2, L0_ffn_b2, L0_ffn_gamma, L0_ffn_beta):
    import numpy as np
    import concourse.bacc as bacc
    from concourse import mybir as mb
    from concourse.bass_utils import run_bass_kernel_spmd as run

    f32 = np.float32
    a = np.arange(P)
    r, c, k = a[:, None, None], np.arange(PCOL)[None, :, None], np.arange(3)[None, None, :]
    emb_sel = np.concatenate([(r == c * PAY + k + 1).reshape(P, -1), (r == c * PAY + PAY - 1).reshape(P, -1)], 1)
    cst = np.concatenate([np.eye(P), np.broadcast_to(a, (P, P)), (a[None, :] < a[:, None]), a[:, None], emb_sel], 1).astype(f32)
    pad_e = P * EC - EDGES
    edge = lambda v, fill: np.concatenate([np.asarray(v), np.full((pad_e,) + v.shape[1:], fill, np.asarray(v).dtype)])
    ids = np.stack([edge(dst, 4095).reshape(P, EC), edge(src, 4095).reshape(P, EC)], 1)
    attr = edge(edge_attr_5, 0).reshape(P, EC, 5)
    pad_n = TILES * P - NODES
    xp = np.concatenate([np.asarray(x), np.zeros((pad_n, IN), f32)])
    types = np.concatenate([np.asarray(node_type_19), np.zeros(pad_n, np.int32)])[None]
    by_type = lambda w: np.asarray(w).reshape(TYPES, -1, P, w.shape[-1]).transpose(2, 1, 0, 3)
    w1 = np.asarray(L0_ffn_w1).reshape(EXPERTS, KC, P, FF).transpose(0, 2, 1, 3).reshape(EXPERTS, P, KC * FF)
    w2 = np.asarray(L0_ffn_w2).reshape(EXPERTS, FC, P, IN).transpose(0, 2, 1, 3).reshape(EXPERTS, P, FC * IN)
    b1 = np.asarray(L0_ffn_b1).reshape(EXPERTS, FC, P).transpose(0, 2, 1)
    ins = dict(
        cst=cst, ids=ids, attr=attr, x=xp, types=types, types_col=types.reshape(TILES, P).T, Wk=by_type(L0_gnn_Wk), Wv=by_type(L0_gnn_Wv),
        Wq=by_type(L0_gnn_Wq), bk=L0_gnn_bk, bv=L0_gnn_bv, bq=L0_gnn_bq, Wa=by_type(L0_gnn_Wa), ba=L0_gnn_ba,
        gb=np.concatenate([np.asarray(L0_gnn_gamma), np.asarray(L0_gnn_beta)], 1),
        wt=np.asarray(L0_gnn_w_time)[None], bt=np.asarray(L0_gnn_b_time)[None],
        gate_w=np.asarray(L0_ffn_gate_w).reshape(KC, P, EXPERTS).transpose(1, 0, 2),
        gate_b=np.asarray(L0_ffn_gate_b)[None], ew=np.concatenate([w1, w2, b1], 2), b2=np.asarray(L0_ffn_b2).reshape(1, -1),
        fgb=np.concatenate([np.asarray(L0_ffn_gamma), np.asarray(L0_ffn_beta)])[None])
    nc = bacc.Bacc("TRN2", target_bir_lowering=False, num_devices=1)
    arrays, args = {}, {}
    for name, v in ins.items():
        v = np.ascontiguousarray(v)
        arrays[f"in_{name}_dram"] = v
        args[name] = nc.dram_tensor(f"in_{name}_dram", v.shape, mb.dt.from_np(v.dtype), kind="ExternalInput").ap()
    args["out"] = nc.dram_tensor("out_dram", (TILES * P, IN), mb.dt.float32, kind="ExternalOutput").ap()
    build(nc, **args)
    r = run(nc, [arrays], core_ids=[0])
    return r.results[0]["out_dram"][:NODES]
```
